# Optimizing a Trainium2 kernel written in Bass

```python
import numpy as np
import jax
import jax.numpy as jnp

def _softmax(x, axis=-1):
    return jax.nn.softmax(x, axis=axis)

def _gelu(x):
    return jax.nn.gelu(x, approximate=True)

def _silu(x):
    return jax.nn.silu(x)

def _sigmoid(x):
    return jax.nn.sigmoid(x)

def _layernorm(x, axis=-1, eps=1e-05):
    m = jnp.mean(x, axis=axis, keepdims=True)
    v = jnp.var(x, axis=axis, keepdims=True)
    return (x - m) / jnp.sqrt(v + eps)

def _scatter_add(tgt, idx, src, axis=0):
    return tgt.at[idx].add(src)

def _segment_sum(src, seg, n):
    return jax.ops.segment_sum(src, seg, n)
kernel_name = 'mk_adaln_attn_ffn_d1_seqx_r8_28af5c'

def setup_inputs(seed: int=0):
    np.random.seed(seed)
    _w = jnp.asarray

    def _rec_inputs():
        import jax
        import jax.numpy as jnp
        _rk = jax.random.key(seed)
        x = -0.0001538 + 1 * jax.random.normal(jax.random.fold_in(_rk, 1), (16, 128, 128), jnp.float32)
        _lenS = 128 - jax.random.randint(jax.random.fold_in(_rk, 7), (16,), 0, max(1, 128 // 4) + 1, jnp.int32)
        _lenS2 = 128 - jax.random.randint(jax.random.fold_in(_rk, 8), (16,), 0, max(1, 128 // 4) + 1, jnp.int32)
        cond_1024 = 0.00782532 + 1.00527 * jax.random.normal(jax.random.fold_in(_rk, 11), (16, 128), jnp.float32)
        return (x, cond_1024)
    x, cond_1024 = _rec_inputs()

    def _L0_cond_setup():
        import jax, jax.numpy as jnp
        import numpy as np
        NUM_EXPERTS = 4
        TOP_K = 2
        key = jax.random.key(seed)
        ks = jax.random.split(key, 16)
        B, L, D, E, H = (8, 96, 128, NUM_EXPERTS, 512)
        s = 0.02
        return {'context_c': jax.random.normal(ks[0], (B, L, D), jnp.float32), 'time_cond': jax.random.normal(ks[1], (B, D), jnp.float32), 'gate_w': jax.random.normal(ks[2], (3 * D, E), jnp.float32) * s, 'gate_b': jnp.zeros((E,), jnp.float32), 'time_w': jax.random.normal(ks[3], (D, 2 * E), jnp.float32) * s, 'time_b': jnp.zeros((2 * E,), jnp.float32), 'ew1': jax.random.normal(ks[4], (E, D, H), jnp.float32) * s, 'eb1': jnp.zeros((E, H), jnp.float32), 'ew2': jax.random.normal(ks[5], (E, H, D), jnp.float32) * s, 'eb2': jnp.zeros((E, D), jnp.float32), 'sw1': jax.random.normal(ks[6], (D, H), jnp.float32) * s, 'sb1': jnp.zeros((H,), jnp.float32), 'sw2': jax.random.normal(ks[7], (H, D), jnp.float32) * s, 'sb2': jnp.zeros((D,), jnp.float32)}
    _L0_cond_all = _L0_cond_setup()
    _L0_cond_in = {k: v for k, v in _L0_cond_all.items() if k in ('gate_w', 'gate_b', 'time_w', 'time_b', 'ew1', 'eb1', 'ew2', 'eb2', 'sw1', 'sb1', 'sw2', 'sb2')}
    del _L0_cond_all

    def _L0_attn_setup():
        import jax, jax.numpy as jnp
        import numpy as np
        D_MODEL = 128
        HEADDIM = 64
        EXPAND = 2
        D_STATE = 128
        D_CONV = 4
        NGROUPS = 1
        D_INNER = EXPAND * D_MODEL
        NHEADS = D_INNER // HEADDIM
        CONV_DIM = D_INNER + 2 * NGROUPS * D_STATE
        D_IN_PROJ = 2 * D_INNER + 2 * NGROUPS * D_STATE + NHEADS
        BATCH = 2
        SEQLEN = 128
        EPS = 1e-05

        def silu(v):
            return v * jax.nn.sigmoid(v)

        def _mamba2(x, in_proj_w, conv_w, conv_b, dt_bias, A_log, D, norm_w, out_proj_w):
            b, l, _ = x.shape
            zxbcdt = x @ in_proj_w.T
            z, xBC, dt = jnp.split(zxbcdt, [D_INNER, D_INNER + CONV_DIM], axis=-1)
            dt = jax.nn.softplus(dt + dt_bias)
            rhs = conv_w.T[:, None, :]
            xBC = jax.lax.conv_general_dilated(xBC, rhs, window_strides=(1,), padding=[(D_CONV - 1, 0)], dimension_numbers=('NWC', 'WIO', 'NWC'), feature_group_count=CONV_DIM)
            xBC = silu(xBC + conv_b)
            xs, Bm, Cm = jnp.split(xBC, [D_INNER, D_INNER + D_STATE], axis=-1)
            xs = xs.reshape(b, l, NHEADS, HEADDIM)
            A = -jnp.exp(A_log)
            dA = jnp.exp(dt * A)

            def step(h, inp):
                dA_t, x_t, B_t, dt_t, C_t = inp
                h = h * dA_t[:, :, None, None] + jnp.einsum('bh,bhp,bn->bhpn', dt_t, x_t, B_t)
                y = jnp.einsum('bhpn,bn->bhp', h, C_t)
                return (h, y)
            h0 = jnp.zeros((b, NHEADS, HEADDIM, D_STATE), x.dtype)
            xs_t = xs.transpose(1, 0, 2, 3)
            _, ys = jax.lax.scan(step, h0, (dA.transpose(1, 0, 2), xs_t, Bm.transpose(1, 0, 2), dt.transpose(1, 0, 2), Cm.transpose(1, 0, 2)))
            y = ys.transpose(1, 0, 2, 3) + D[None, None, :, None] * xs
            y = y.reshape(b, l, D_INNER)
            y = y * silu(z)
            y = y * jax.lax.rsqrt(jnp.mean(y * y, axis=-1, keepdims=True) + EPS) * norm_w
            return y @ out_proj_w.T
        key = jax.random.key(seed)
        ks = jax.random.split(key, 8)
        s = 0.02
        return {'x': jax.random.normal(ks[0], (BATCH, SEQLEN, D_MODEL), jnp.float32), 'in_proj_w': jax.random.normal(ks[1], (D_IN_PROJ, D_MODEL), jnp.float32) * s, 'conv_w': jax.random.normal(ks[2], (CONV_DIM, D_CONV), jnp.float32) * 0.2, 'conv_b': jax.random.normal(ks[3], (CONV_DIM,), jnp.float32) * 0.02, 'dt_bias': jax.random.normal(ks[4], (NHEADS,), jnp.float32) * 0.1, 'A_log': jax.random.normal(ks[5], (NHEADS,), jnp.float32) * 0.5, 'D': jax.random.normal(ks[6], (NHEADS,), jnp.float32) * 0.5, 'norm_w': jnp.ones((D_INNER,), jnp.float32), 'out_proj_w': jax.random.normal(ks[7], (D_MODEL, D_INNER), jnp.float32) * s}
    _L0_attn_all = _L0_attn_setup()
    _L0_attn_in = {k: v for k, v in _L0_attn_all.items() if k in ('in_proj_w', 'conv_w', 'conv_b', 'dt_bias', 'A_log', 'D', 'norm_w', 'out_proj_w')}
    del _L0_attn_all

    def _L0_cond2_setup():
        import jax, jax.numpy as jnp
        import numpy as np
        B, N, D, C = (32, 32, 128, 128)
        key = jax.random.key(seed)
        k1, k2, k3, k4 = jax.random.split(key, 4)
        scale = 1.0 / np.sqrt(D)
        return {'encoded_utterance': jax.random.normal(k1, (B, D), dtype=jnp.float32), 'element_embeddings': jax.random.normal(k2, (B, N, D), dtype=jnp.float32), 'weight_matrix': jax.random.normal(k3, (2 * D, C), dtype=jnp.float32) * scale, 'W_proj': jax.random.normal(k4, (D, D), dtype=jnp.float32) * scale, 'b_proj': jnp.zeros((D,), dtype=jnp.float32)}
    _L0_cond2_all = _L0_cond2_setup()
    _L0_cond2_in = {k: v for k, v in _L0_cond2_all.items() if k in ('weight_matrix', 'W_proj', 'b_proj')}
    del _L0_cond2_all

    def _L0_ffn_setup():
        import jax, jax.numpy as jnp
        import numpy as np
        EPS = 1e-05

        def rmsnorm(x):
            return x * jax.lax.rsqrt(jnp.mean(x * x, axis=-1, keepdims=True) + EPS)

        def act_quant(x):
            scale = 127.0 / jnp.clip(jnp.max(jnp.abs(x), axis=-1, keepdims=True), 1e-05)
            q = jnp.clip(jnp.round(x * scale), -128.0, 127.0) / scale
            return x + jax.lax.stop_gradient(q - x)

        def weight_quant(w):
            scale = 1.0 / jnp.clip(jnp.mean(jnp.abs(w)), 1e-05)
            q = jnp.clip(jnp.round(w * scale), -1.0, 1.0) / scale
            return w + jax.lax.stop_gradient(q - w)

        def bitlinear(x, w, b):
            xq = act_quant(rmsnorm(x))
            wq = weight_quant(w)
            return jnp.einsum('bsd,fd->bsf', xq, wq) + b
        key = jax.random.key(seed)
        k0, k1, k2 = jax.random.split(key, 3)
        B, S, D, F = (2, 1024, 128, 512)
        x = jax.random.normal(k0, (B, S, D), dtype=jnp.float32)
        w1 = jax.random.normal(k1, (F, D), dtype=jnp.float32) * (1.0 / np.sqrt(D))
        b1 = jnp.zeros((F,), dtype=jnp.float32)
        w2 = jax.random.normal(k2, (D, F), dtype=jnp.float32) * (1.0 / np.sqrt(F))
        b2 = jnp.zeros((D,), dtype=jnp.float32)
        return {'x': x, 'w1': w1, 'b1': b1, 'w2': w2, 'b2': b2}
    _L0_ffn_all = _L0_ffn_setup()
    _L0_ffn_in = {k: v for k, v in _L0_ffn_all.items() if k in ('w1', 'b1', 'w2', 'b2')}
    del _L0_ffn_all
    return {'x': x, 'cond_1024': cond_1024, 'L0_cond_gate_w': _L0_cond_in['gate_w'], 'L0_cond_gate_b': _L0_cond_in['gate_b'], 'L0_cond_time_w': _L0_cond_in['time_w'], 'L0_cond_time_b': _L0_cond_in['time_b'], 'L0_cond_ew1': _L0_cond_in['ew1'], 'L0_cond_eb1': _L0_cond_in['eb1'], 'L0_cond_ew2': _L0_cond_in['ew2'], 'L0_cond_eb2': _L0_cond_in['eb2'], 'L0_cond_sw1': _L0_cond_in['sw1'], 'L0_cond_sb1': _L0_cond_in['sb1'], 'L0_cond_sw2': _L0_cond_in['sw2'], 'L0_cond_sb2': _L0_cond_in['sb2'], 'L0_attn_in_proj_w': _L0_attn_in['in_proj_w'], 'L0_attn_conv_w': _L0_attn_in['conv_w'], 'L0_attn_conv_b': _L0_attn_in['conv_b'], 'L0_attn_dt_bias': _L0_attn_in['dt_bias'], 'L0_attn_A_log': _L0_attn_in['A_log'], 'L0_attn_D': _L0_attn_in['D'], 'L0_attn_norm_w': _L0_attn_in['norm_w'], 'L0_attn_out_proj_w': _L0_attn_in['out_proj_w'], 'L0_cond2_weight_matrix': _L0_cond2_in['weight_matrix'], 'L0_cond2_W_proj': _L0_cond2_in['W_proj'], 'L0_cond2_b_proj': _L0_cond2_in['b_proj'], 'L0_ffn_w1': _L0_ffn_in['w1'], 'L0_ffn_b1': _L0_ffn_in['b1'], 'L0_ffn_w2': _L0_ffn_in['w2'], 'L0_ffn_b2': _L0_ffn_in['b2']}

def reference(x, cond_1024, L0_cond_gate_w, L0_cond_gate_b, L0_cond_time_w, L0_cond_time_b, L0_cond_ew1, L0_cond_eb1, L0_cond_ew2, L0_cond_eb2, L0_cond_sw1, L0_cond_sb1, L0_cond_sw2, L0_cond_sb2, L0_attn_in_proj_w, L0_attn_conv_w, L0_attn_conv_b, L0_attn_dt_bias, L0_attn_A_log, L0_attn_D, L0_attn_norm_w, L0_attn_out_proj_w, L0_cond2_weight_matrix, L0_cond2_W_proj, L0_cond2_b_proj, L0_ffn_w1, L0_ffn_b1, L0_ffn_w2, L0_ffn_b2):
    import jax
    import jax.numpy as jnp

    def _L0_cond_ref(context_c, time_cond, gate_w, gate_b, time_w, time_b, ew1, eb1, ew2, eb2, sw1, sb1, sw2, sb2):
        import jax, jax.numpy as jnp
        import numpy as np
        NUM_EXPERTS = 4
        TOP_K = 2
        B, L, D = context_c.shape
        E, K = (NUM_EXPERTS, TOP_K)
        L_head = L_wrist = L // 3
        head = context_c[:, :L_head]
        wrist = context_c[:, L_head:L_head + L_wrist]
        proprio = context_c[:, L_head + L_wrist:]
        full_agg = context_c.mean(axis=1)
        hp_agg = jnp.concatenate([head, proprio], axis=1).mean(axis=1)
        wp_agg = jnp.concatenate([wrist, proprio], axis=1).mean(axis=1)
        gate_in = jnp.concatenate([full_agg, hp_agg, wp_agg], axis=-1)
        gate_logits = gate_in @ gate_w + gate_b
        mod = jax.nn.silu(time_cond) @ time_w + time_b
        scale, shift = jnp.split(mod, 2, axis=-1)
        gate_logits = gate_logits * (1.0 + scale) + shift
        gate_scores = jax.nn.softmax(gate_logits, axis=-1)
        topk_w, topk_i = jax.lax.top_k(gate_scores, K)
        topk_w = topk_w / (topk_w.sum(axis=-1, keepdims=True) + 1e-08)
        onehot = (topk_i[..., None] == jnp.arange(E)[None, None, :]).astype(context_c.dtype)
        w_be = jnp.sum(topk_w[..., None] * onehot, axis=1)
        mask = np.ones((E, L), dtype=np.float32)
        mask[1, L_head:L_head + L_wrist] = 0.0
        mask[2, :L_head] = 0.0
        mask = jnp.asarray(mask)
        out = jnp.zeros_like(context_c)
        for e in range(E):
            h = jax.nn.gelu(context_c @ ew1[e] + eb1[e], approximate=True)
            y = h @ ew2[e] + eb2[e]
            out = out + w_be[:, e][:, None, None] * mask[e][None, :, None] * y
        shared = jax.nn.gelu(context_c @ sw1 + sb1, approximate=True) @ sw2 + sb2
        return out + shared

    def _L0_attn_ref(x, in_proj_w, conv_w, conv_b, dt_bias, A_log, D, norm_w, out_proj_w):
        import jax, jax.numpy as jnp
        import numpy as np
        D_MODEL = 128
        HEADDIM = 64
        EXPAND = 2
        D_STATE = 128
        D_CONV = 4
        NGROUPS = 1
        D_INNER = EXPAND * D_MODEL
        NHEADS = D_INNER // HEADDIM
        CONV_DIM = D_INNER + 2 * NGROUPS * D_STATE
        D_IN_PROJ = 2 * D_INNER + 2 * NGROUPS * D_STATE + NHEADS
        BATCH = 2
        SEQLEN = 128
        EPS = 1e-05

        def silu(v):
            return v * jax.nn.sigmoid(v)

        def _mamba2(x, in_proj_w, conv_w, conv_b, dt_bias, A_log, D, norm_w, out_proj_w):
            b, l, _ = x.shape
            zxbcdt = x @ in_proj_w.T
            z, xBC, dt = jnp.split(zxbcdt, [D_INNER, D_INNER + CONV_DIM], axis=-1)
            dt = jax.nn.softplus(dt + dt_bias)
            rhs = conv_w.T[:, None, :]
            xBC = jax.lax.conv_general_dilated(xBC, rhs, window_strides=(1,), padding=[(D_CONV - 1, 0)], dimension_numbers=('NWC', 'WIO', 'NWC'), feature_group_count=CONV_DIM)
            xBC = silu(xBC + conv_b)
            xs, Bm, Cm = jnp.split(xBC, [D_INNER, D_INNER + D_STATE], axis=-1)
            xs = xs.reshape(b, l, NHEADS, HEADDIM)
            A = -jnp.exp(A_log)
            dA = jnp.exp(dt * A)

            def step(h, inp):
                dA_t, x_t, B_t, dt_t, C_t = inp
                h = h * dA_t[:, :, None, None] + jnp.einsum('bh,bhp,bn->bhpn', dt_t, x_t, B_t)
                y = jnp.einsum('bhpn,bn->bhp', h, C_t)
                return (h, y)
            h0 = jnp.zeros((b, NHEADS, HEADDIM, D_STATE), x.dtype)
            xs_t = xs.transpose(1, 0, 2, 3)
            _, ys = jax.lax.scan(step, h0, (dA.transpose(1, 0, 2), xs_t, Bm.transpose(1, 0, 2), dt.transpose(1, 0, 2), Cm.transpose(1, 0, 2)))
            y = ys.transpose(1, 0, 2, 3) + D[None, None, :, None] * xs
            y = y.reshape(b, l, D_INNER)
            y = y * silu(z)
            y = y * jax.lax.rsqrt(jnp.mean(y * y, axis=-1, keepdims=True) + EPS) * norm_w
            return y @ out_proj_w.T
        return x + _mamba2(x, in_proj_w, conv_w, conv_b, dt_bias, A_log, D, norm_w, out_proj_w)

    def _L0_cond2_ref(encoded_utterance, element_embeddings, weight_matrix, W_proj, b_proj):
        import jax, jax.numpy as jnp
        import numpy as np
        B, N, D, C = (32, 32, 128, 128)
        u = jax.nn.gelu(encoded_utterance @ W_proj + b_proj, approximate=False)
        W_u, W_e = (weight_matrix[:D], weight_matrix[D:])
        logits = (u @ W_u)[:, None, :] + jnp.einsum('bnd,dc->bnc', element_embeddings, W_e)
        return logits

    def _L0_ffn_ref(x, w1, b1, w2, b2):
        import jax, jax.numpy as jnp
        import numpy as np
        EPS = 1e-05

        def rmsnorm(x):
            return x * jax.lax.rsqrt(jnp.mean(x * x, axis=-1, keepdims=True) + EPS)

        def act_quant(x):
            scale = 127.0 / jnp.clip(jnp.max(jnp.abs(x), axis=-1, keepdims=True), 1e-05)
            q = jnp.clip(jnp.round(x * scale), -128.0, 127.0) / scale
            return x + jax.lax.stop_gradient(q - x)

        def weight_quant(w):
            scale = 1.0 / jnp.clip(jnp.mean(jnp.abs(w)), 1e-05)
            q = jnp.clip(jnp.round(w * scale), -1.0, 1.0) / scale
            return w + jax.lax.stop_gradient(q - w)

        def bitlinear(x, w, b):
            xq = act_quant(rmsnorm(x))
            wq = weight_quant(w)
            return jnp.einsum('bsd,fd->bsf', xq, wq) + b
        h = bitlinear(x, w1, b1)
        h = jax.nn.gelu(h, approximate=False)
        return bitlinear(h, w2, b2)
    x = x + _L0_attn_ref(_L0_cond_ref(x, cond_1024, L0_cond_gate_w, L0_cond_gate_b, L0_cond_time_w, L0_cond_time_b, L0_cond_ew1, L0_cond_eb1, L0_cond_ew2, L0_cond_eb2, L0_cond_sw1, L0_cond_sb1, L0_cond_sw2, L0_cond_sb2), L0_attn_in_proj_w, L0_attn_conv_w, L0_attn_conv_b, L0_attn_dt_bias, L0_attn_A_log, L0_attn_D, L0_attn_norm_w, L0_attn_out_proj_w)
    x = x + _L0_ffn_ref(_L0_cond2_ref(cond_1024, x, L0_cond2_weight_matrix, L0_cond2_W_proj, L0_cond2_b_proj), L0_ffn_w1, L0_ffn_b1, L0_ffn_w2, L0_ffn_b2)
    return x

_drawn_inputs = setup_inputs


def setup_inputs(seed=0):
    import zlib

    import numpy as np

    out = dict(_drawn_inputs(seed))
    spreads = {'L0_cond_gate_b': (0.0, 0.1),
     'L0_cond_time_b': (0.0, 0.1),
     'L0_cond_eb1': (0.0, 0.455),
     'L0_cond_eb2': (0.0, 0.1),
     'L0_cond_sb1': (0.0, 0.318),
     'L0_cond_sb2': (0.0, 0.1),
     'L0_attn_norm_w': (1.0, 0.6),
     'L0_cond2_b_proj': (0.0, 0.8),
     'L0_ffn_b1': (0.0, 0.1),
     'L0_ffn_b2': (0.0, 0.1)}
    factors = {'L0_cond_gate_w': 2.921,
     'L0_attn_in_proj_w': 6.341,
     'L0_attn_conv_w': 7.832,
     'L0_attn_conv_b': 7.108,
     'L0_attn_dt_bias': 8.0,
     'L0_attn_A_log': 26.972,
     'L0_attn_D': 6.036,
     'L0_attn_out_proj_w': 6.329}
    for name, (base, spread) in spreads.items():
        noise = np.random.default_rng([zlib.crc32(name.encode()), seed]).standard_normal(out[name].shape)
        drawn = base * np.exp(spread * noise) if base else spread * noise
        out[name] = jnp.asarray(drawn.astype(out[name].dtype))
    for name, factor in factors.items():
        out[name] = (out[name] * factor).astype(out[name].dtype)
    return out
```

```python
import concourse.bass as bass
from concourse import mybir
from contextlib import ExitStack


class Order:

    def __init__(self, eng, sem):
        self.eng, self.sem, self.count, self.turn, self.per = eng, sem, 0, None, 0

    def step(self, ins):
        self.count += 1
        ins.then_inc(self.sem, 1)
        return self.count

    def wait(self, mark=None):
        mark = self.count if mark is None else mark
        self.eng.wait_ge(self.sem, mark if self.turn is None else self.turn * self.per + mark)

    def link(self, ins):
        self.step(ins)
        self.wait()

    def enter(self, turn, per):
        self.turn, self.per, self.first = turn, per, self.count

    def leave(self, turns):
        assert self.count - self.first == self.per, (self.count - self.first, self.per)
        self.turn, self.count = None, self.first + turns * self.per


def build(nc, x, cond, gate_w, gate_b, time_w, time_b, ew1, eb1, ew2, eb2, sw1, sb1, sw2, sb2,
          in_w, conv_w, conv_b, dt_bias, A_log, D, norm_w, out_w, mix_w, proj_w, proj_b,
          f_w1, f_b1, f_w2, f_b2, out):
    f32 = mybir.dt.float32
    bf16 = mybir.dt.bfloat16
    ALU = mybir.AluOpType
    ACT = mybir.ActivationFunctionType
    AX = mybir.AxisListType

    P = 128
    B, L, DM = x.shape
    E = gate_w.shape[1]
    H = sw1.shape[1]
    HC = H // P
    DI = out_w.shape[1]
    JI = DI // P
    NH = dt_bias.shape[0]
    HD = DI // NH
    CD = conv_w.shape[0]
    JC = CD // P
    KW = conv_w.shape[1]
    F = f_w1.shape[0]
    FC = F // P
    GB = 4
    NG = B // GB
    GT = GB * L
    L3 = L // 3
    EPS = 1e-5
    MAGIC = 1.5 * 2.0 ** 23
    UNITS = (E + 1) * HC
    AHEAD = 2

    ctx = ExitStack()
    with ctx:
        def sb(name, shape, dt=f32):
            return ctx.enter_context(nc.sbuf_tensor(name, shape, dt))

        def sem(name):
            return ctx.enter_context(nc.semaphore(name))

        bank = [ctx.enter_context(nc.psum_tensor(f"bank{i}", [P, 512], f32)) for i in range(8)]

        x_tok = sb("x_tok", [P, B, DM])
        x_T = sb("x_T", [P, B * L])
        c_T = sb("c_T", [P, B * L])
        c_grp = sb("c_grp", [P, GT])
        res = sb("res", [P, B, DM])
        dt_raw = sb("dt_raw", [P, B, NH])
        e_all = x_T[:, :].rearrange("p (b d) -> p b d", d=DM)

        w_up = sb("w_up", [P, E + 1, H])
        w_down = sb("w_down", [P, E + 1, HC, DM])
        rows = sb("rows", [52, P])
        cols = sb("cols", [P, 52])
        C_EB1, C_SB1, C_EB2, C_SB2, C_CB, C_PB, C_NW, C_COND, C_DT = 0, 16, 20, 24, 25, 29, 30, 32, 48
        gate_w_sb = sb("gate_w_sb", [P, 3, E])
        gate_b_sb = sb("gate_b_sb", [B, E])
        time_w_sb = sb("time_w_sb", [P, 2 * E])
        time_b_sb = sb("time_b_sb", [B, 2 * E])
        in_nat = sb("in_nat", [P, 6, DM])
        in_T = sb("in_T", [P, 6 * P])
        conv_w_sb = sb("conv_w_sb", [P, JC, KW])
        dt_bias_sb = sb("dt_bias_sb", [P, NH])
        A_sb = sb("A_sb", [P, NH])
        A_pos = sb("A_pos", [P, NH])
        D_all = sb("D_all", [P, NH])
        D_diag = sb("D_diag", [P, JI, P])
        out_nat = sb("out_nat", [P, DI])
        out_T = sb("out_T", [P, JI, DM])
        mix_sb = sb("mix_sb", [P, 2, P])
        proj_sb = sb("proj_sb", [P, P])
        w1_nat = sb("w1_nat", [P, FC, DM])
        w2_nat = sb("w2_nat", [P, F])
        w1_q = sb("w1_q", [P, FC, DM], bf16)
        w2_q = sb("w2_q", [P, F], bf16)
        w1_qT = sb("w1_qT", [P, F], bf16)
        w2_qT = sb("w2_qT", [P, FC, DM], bf16)
        b1_sb = sb("b1_sb", [P, F])
        b2_sb = sb("b2_sb", [P, DM])

        ident = sb("ident", [P, P])
        identb = sb("identb", [P, P], bf16)
        ident4 = sb("ident4", [P, NH, L])
        ones = sb("ones", [P, P])
        regions = sb("regions", [P, 3])
        part = sb("part", [P, 1])
        lower = sb("lower", [B, E, E])
        minus_half = sb("minus_half", [P, GB])

        agg = sb("agg", [P, B, 3])
        cond_silu = sb("cond_silu", [P, B])
        mod = sb("mod", [B, 2 * E])
        gl = sb("gl", [B, E])
        gmax = sb("gmax", [B, 1])
        gsum = sb("gsum", [B, 1])
        prob = sb("prob", [B, E])
        gt = sb("gt", [B, E, E])
        eq = sb("eq", [B, E, E])
        rank = sb("rank", [B, E])
        wsel = sb("wsel", [B, E])
        wexp = sb("wexp", [B, B, E])
        ones16 = ones[0:B, :]
        wcol = sb("wcol", [P, B, E])
        wm = sb("wm", [P, E, B * L])

        hid = sb("hid", [P, 4, GT])
        part_y = sb("part_y", [P, 2, GT])

        dt_all = sb("dt_all", [P, B, NH])
        dA_all = sb("dA_all", [P, B, NH])
        dt_t = [sb(f"dt_t{i}", [P, B * NH]) for i in range(4)]
        dA_grp = sb("dA_grp", [P, GB * NH])
        z_act = sb("z_act", [P, JI, GT])
        conv = sb("conv", [P, JC, GT])
        xbc = sb("xbc", [P, JC, GT])
        x_dt = sb("x_dt", [P, GB, DI])
        decay = sb("decay", [P, 2, NH * L])
        mixer = sb("mixer", [P, 2, NH * L])
        y_g = sb("y_g", [P, JI, GT])
        y_sq = sb("y_sq", [P, JI, GT])
        y_ms = sb("y_ms", [P, GB])
        y_r = sb("y_r", [P, GB])
        r_grp = sb("r_grp", [P, GB, DM])
        r_T = sb("r_T", [P, GT])
        u_T = sb("u_T", [P, B])
        uw = sb("uw", [B, P])
        e_bias = sb("e_bias", [P, B, P])

        wabs = sb("wabs", [P, 2, 512])
        wsum = sb("wsum", [P, 2])
        wmean = sb("wmean", [P, 2])
        wscale = sb("wscale", [P, 2])
        wtmp = sb("wtmp", [P, 2, 512])
        sq_scr = wm[:, 2, :].rearrange("p (b f) -> p b f", f=F)
        ssq = sb("ssq", [P, 2, GB])
        amax = sb("amax", [P, 2, GB])
        ms = sb("ms", [P, 2, GB])
        rr = sb("rr", [P, 2, GB])
        cl = sb("cl", [P, 2, GB])
        inv = sb("inv", [P, 2, GB])
        qm = sb("qm", [P, 2, GB])
        qk = sb("qk", [P, 2, GB])
        q1_f = sb("q1_f", [P, GT])
        q1 = sb("q1", [P, GT], bf16)
        q1_T = sb("q1_T", [P, GT], bf16)
        h_pre = wm[:, 0, :].rearrange("p (b f) -> p b f", f=F)
        h_act = wm[:, 1, :].rearrange("p (b f) -> p b f", f=F)
        q2_f = wm[:, 3, :].rearrange("p (b f) -> p b f", f=F)
        q2 = sb("q2", [P, GB, F], bf16)
        q2_T = sb("q2_T", [P, GB, F], bf16)
        y_out = sb("y_out", [P, GB, DM])

        names = """x_in shared_in experts_in rows_in gate_in in_in mix_in ffn_in out_sent
            v_order a_order p_order consts
            x_T_psum x_T_ready cols_psum cols_ready agg_psum agg_ready silu_ready gate_psum gl_ready
            prob_exp wexp_ready wcol_psum wcol_ready wm_ready
            up_done gelu_done down_done y_part p_add c_T_done tail_psum tail_done
            in_psum in_ready out_psum out_ready diag_ready u_psum u_ready uw_psum uw_ready eb_psum eb_ready
            abs_done sum_psum wmean_ready w_q_ready w_qT_psum w_qT_ready
            dt_in dt_exp dt_w dt_ln dt_mul
            z_psum z_ready xbc_psum tap_first conv_done xbc_ready xs_T_psum x_dt_ready g_psum bc_psum
            scan_done mix_ready y_psum y_g_ready y_sq_ready m_psum ss_psum ms_ready yr_ready
            r_grp_ready rT_psum rT_ready e_psum e_ready dA_grp_ready
            ssq1 ms1 rr1 q1_ready q1T_psum q1T_ready h_psum h_pre_ready h_act_ready ssq2 ms2 rr2
            q2_ready q2T_psum q2T_ready o_psum y_out_ready""".split()
        s = {n: sem(n) for n in names}

        def col(c, n=1):
            return cols[:, c:c + n]

        def grp(t, g):
            return t[:, bass.ds(g * GB, GB), :].rearrange("p b d -> p (b d)")

        Y_BANK = [4, 5, 4, 5, 6]
        ER = E + 1

        block = ctx.enter_context(nc.Block())

        @block.sync
        def _(sp):
            for g in range(NG):
                sp.dma_start(x_tok[:, g * GB:(g + 1) * GB, :],
                             x[g * GB:(g + 1) * GB, :, :].rearrange("b t d -> t b d")).then_inc(s["x_in"], 16)
            sp.dma_start(w_up[:, 0, :], sw1).then_inc(s["shared_in"], 16)
            sp.dma_start(w_down[:, 0, :, :], sw2.rearrange("(c p) d -> p c d", p=P)).then_inc(s["shared_in"], 16)
            for e in range(E):
                sp.dma_start(w_up[:, 1 + e, :], ew1[e, :, :]).then_inc(s["experts_in"], 16)
                sp.dma_start(w_down[:, 1 + e, :, :],
                             ew2[e, :, :].rearrange("(c p) d -> p c d", p=P)).then_inc(s["experts_in"], 16)
            sp.sem_inc(s["out_sent"], 16)
            with sp.Fori(0, NG) as g:
                sp.wait_ge(s["y_out_ready"], g + 2)
                sp.dma_start(out[bass.ds(g * GB, GB), :, :].rearrange("b t d -> t b d"),
                             y_out[:, :, :]).then_inc(s["out_sent"], 16)
            sp.wait_ge(s["out_sent"], 16 * (NG + 1))

        @block.gpsimd
        def _(pool):
            order = Order(pool, s["p_order"])
            small = ((eb1.rearrange("e (c p) -> (e c) p", p=P), C_EB1),
                     (sb1.rearrange("(c p) -> c p", p=P), C_SB1),
                     (eb2, C_EB2), (sb2.rearrange("(c p) -> c p", p=P), C_SB2),
                     (conv_b.rearrange("(c p) -> c p", p=P), C_CB),
                     (proj_b.rearrange("(c p) -> c p", p=P), C_PB),
                     (norm_w.rearrange("(c p) -> c p", p=P), C_NW), (cond, C_COND),
                     (in_w[6 * P:6 * P + NH, :], C_DT))
            for src, c in small:
                pool.dma_start(rows[c:c + src.shape[0], :], src).then_inc(s["rows_in"], 16)
            assert len(small) == 9

            order.step(pool.memset(ident[:, :], 0.0))
            order.step(pool.memset(regions[:, 0:1], 1.0 / L))
            order.step(pool.memset(regions[:, 1:3], 1.0 / (L - L3)))
            order.step(pool.memset(part[:, :], 1.0 / (L - L3)))
            order.step(pool.memset(lower[:, :, :], 1.0))
            order.step(pool.memset(ones[:, :], 1.0))
            order.step(pool.memset(minus_half[:, :], -0.5))
            order.wait()
            order.step(pool.affine_select(out=ident[:, :], in_=ident[:, :], compare_op=ALU.not_equal, fill=1.0,
                                          base=0, pattern=[[-1, P]], channel_multiplier=1))
            order.step(pool.affine_select(out=part[:, :], in_=part[:, :], compare_op=ALU.is_ge, fill=0.0,
                                          base=-2 * L3, pattern=[[0, 1]], channel_multiplier=1))
            order.step(pool.affine_select(out=regions[:, 1:2], in_=regions[:, 1:2], compare_op=ALU.is_gt, fill=0.0,
                                          base=L3, pattern=[[0, 1]], channel_multiplier=-1))
            order.step(pool.affine_select(out=regions[:, 2:3], in_=regions[:, 2:3], compare_op=ALU.is_ge, fill=0.0,
                                          base=-L3, pattern=[[0, 1]], channel_multiplier=1))
            order.step(pool.affine_select(out=lower[:, :, :], in_=lower[:, :, :], compare_op=ALU.is_gt, fill=0.0,
                                          base=0, pattern=[[1, E], [-1, E]], channel_multiplier=0))
            order.wait()
            order.step(pool.tensor_tensor(regions[:, 1:2], regions[:, 1:2], part[:, :], ALU.add))
            order.step(pool.tensor_copy(identb[:, :], ident[:, :]))
            for h in range(NH):
                order.step(pool.tensor_copy(ident4[:, h, :], ident[:, :]))
            order.wait()
            pool.sem_inc(s["consts"], 1)

            pool.wait_ge(s["wcol_ready"], 1)
            for e in range(E):
                spans = {1: [(0, L3, 1), (L3, 2 * L3, 0), (2 * L3, L, 1)], 2: [(0, L3, 0), (L3, L, 1)]}
                dst = wm[:, e, :].rearrange("p (b t) -> p b t", t=L)
                for lo, hi, on in spans.get(e, [(0, L, 1)]):
                    if on:
                        order.step(pool.tensor_copy(
                            dst[:, :, lo:hi], wcol[:, :, e].unsqueeze(2).broadcast_to([P, B, hi - lo])))
                    else:
                        order.step(pool.memset(dst[:, :, lo:hi], 0.0))
            order.wait()
            pool.sem_inc(s["wm_ready"], 1)

            pool.sem_inc(s["p_add"], 2)
            pool.sem_inc(s["c_T_done"], 1)
            with pool.Fori(0, NG) as g:
                for e in range(E):
                    pool.wait_ge(s["y_part"], ER + g * ER + e + 2)
                    pool.wait_ge(s["p_add"], 2 + g * E + e)
                    pool.tensor_tensor(c_grp[:, :], c_grp[:, :], part_y[:, e % 2, :], ALU.add)\
                        .then_inc(s["p_add"], 1)
                pool.wait_ge(s["p_add"], 2 + (g + 1) * E)
                pool.tensor_copy(c_T[:, bass.ds(g * GT, GT)], c_grp[:, :]).then_inc(s["c_T_done"], 1)
            with pool.Fori(0, NG) as g:
                pool.wait_ge(s["ms_ready"], g + 1)
                pool.tensor_tensor(y_r[:, :], y_ms[:, :], minus_half[:, :], ALU.pow).then_inc(s["yr_ready"], 1)
            with pool.Fori(0, NG) as g:
                for k in range(2):
                    pool.wait_ge(s[f"ms{k + 1}"], g + 1)
                    pool.tensor_tensor(rr[:, k, :], ms[:, k, :], minus_half[:, :], ALU.pow)\
                        .then_inc(s[f"rr{k + 1}"], 1)

        @block.scalar
        def _(act):
            for dst, src in ((gate_w_sb[:, :, :], gate_w.rearrange("(j p) e -> p j e", p=P)),
                             (gate_b_sb[:, :], gate_b.partition_broadcast(B)),
                             (time_w_sb[:, :], time_w),
                             (time_b_sb[:, :], time_b.partition_broadcast(B))):
                act.dma_start(dst, src).then_inc(s["gate_in"], 16)
            for dst, src in ((in_nat[:, :, :], in_w[0:6 * P, :].rearrange("(c p) d -> p c d", p=P)),
                             (conv_w_sb[:, :, :], conv_w.rearrange("(c p) k -> p c k", p=P)),
                             (dt_bias_sb[:, :], dt_bias.partition_broadcast(P)),
                             (A_sb[:, :], A_log.partition_broadcast(P)),
                             (D_all[:, :], D.partition_broadcast(P)),
                             (out_nat[:, :], out_w)):
                act.dma_start(dst, src).then_inc(s["in_in"], 16)
            for dst, src in ((mix_sb[:, :, :], mix_w.rearrange("(k p) c -> p k c", p=P)), (proj_sb[:, :], proj_w)):
                act.dma_start(dst, src).then_inc(s["mix_in"], 16)
            for dst, src in ((w1_nat[:, :, :], f_w1.rearrange("(c p) d -> p c d", p=P)), (w2_nat[:, :], f_w2),
                             (b1_sb[:, :], f_b1.partition_broadcast(P)), (b2_sb[:, :], f_b2.partition_broadcast(P))):
                act.dma_start(dst, src).then_inc(s["ffn_in"], 16)

            for g in range(NG):
                act.wait_ge(s["x_T_psum"], g + 1)
                act.copy(x_T[:, g * GT:(g + 1) * GT], bank[g % 2][:, :]).then_inc(s["x_T_ready"], 1)
            act.wait_ge(s["cols_ready"], 1)
            act.activation(cond_silu[:, :], col(C_COND, B), ACT.Silu).then_inc(s["silu_ready"], 1)
            act.wait_ge(s["gl_ready"], 1)
            act.activation(prob[:, :], gl[:, :], ACT.Exp, bias=gmax[:, 0:1], accum_out=gsum[:, 0:1])\
                .then_inc(s["prob_exp"], 1)

            act.sem_inc(s["gelu_done"], 4)
            with act.Fori(0, NG) as g:
                for i in range(UNITS):
                    e, c = divmod(i, HC)
                    act.wait_ge(s["up_done"], g * UNITS + i + 1)
                    act.wait_ge(s["down_done"], g * UNITS + i + 1)
                    bias = col(C_SB1 + c) if e == 0 else col(C_EB1 + (e - 1) * HC + c)
                    act.activation(hid[:, i % 4, :], bank[i % 4][:, :], ACT.Gelu_apprx_tanh, bias=bias)\
                        .then_inc(s["gelu_done"], 1)

            act.wait_ge(s["u_psum"], 1)
            act.activation(u_T[:, :], bank[3][:, 0:B], ACT.Gelu, bias=col(C_PB)).then_inc(s["u_ready"], 1)
            act.wait_ge(s["ffn_in"], 64)
            act.activation(wabs[:, 0, :], w1_nat[:, :, :].rearrange("p c d -> p (c d)"), ACT.Abs,
                           accum_out=wsum[:, 0:1]).then_inc(s["abs_done"], 1)
            act.activation(wabs[:, 1, :], w2_nat[:, :], ACT.Abs, accum_out=wsum[:, 1:2]).then_inc(s["abs_done"], 1)

            act.wait_ge(s["in_in"], 16 * 6)
            act.activation(A_pos[:, :], A_sb[:, :], ACT.Exp).then_inc(s["dt_exp"], 1)
            act.wait_ge(s["dt_in"], 1)
            act.activation(dt_t[1][:, :], dt_t[0][:, :], ACT.Exp, scale=-1.0).then_inc(s["dt_exp"], 1)
            act.wait_ge(s["dt_w"], 1)
            act.activation(dt_t[3][:, :], dt_t[2][:, :], ACT.Ln).then_inc(s["dt_ln"], 1)
            act.wait_ge(s["dt_mul"], 1)
            act.activation(dA_all[:, :, :].rearrange("p b h -> p (b h)"), dt_t[0][:, :], ACT.Exp, scale=-1.0)\
                .then_inc(s["dt_exp"], 1)

            with act.Fori(0, NG) as g:
                for j in range(JI):
                    act.wait_ge(s["z_psum"], g * JI + j + 1)
                    act.activation(z_act[:, j, :], bank[j][:, :], ACT.Silu).then_inc(s["z_ready"], 1)
                for j in range(JC):
                    act.wait_ge(s["xbc_psum"], g * JC + j + 1)
                    act.activation(conv[:, j, :], bank[2 + j][:, :], ACT.Identity, bias=col(C_CB + j),
                                   scale=conv_w_sb[:, j, KW - 1:KW]).then_inc(s["tap_first"], 1)
                for j in range(JC):
                    act.wait_ge(s["conv_done"], g * JC + j + 1)
                    act.activation(xbc[:, j, :], conv[:, j, :], ACT.Silu).then_inc(s["xbc_ready"], 1)
                for j in range(JI):
                    act.wait_ge(s["y_g_ready"], g * JI + j + 1)
                    act.activation(y_sq[:, j, :], y_g[:, j, :], ACT.Square).then_inc(s["y_sq_ready"], 1)
                act.wait_ge(s["rT_psum"], g + 1)
                act.copy(r_T[:, :], bank[2][:, :]).then_inc(s["rT_ready"], 1)

            with act.Fori(0, NG) as g:
                for b in range(GB):
                    act.activation(sq_scr[:, b, 0:DM], e_all[:, bass.ds(g * GB + b, 1), :].rearrange("p b d -> p (b d)"),
                                   ACT.Square, accum_out=ssq[:, 0, b:b + 1]).then_inc(s["ssq1"], 1)
                act.wait_ge(s["q1T_psum"], g + 1)
                act.copy(q1_T[:, :], bank[0][:, 0:GT // 2].bitcast(bf16)).then_inc(s["q1T_ready"], 1)
                for b in range(GB):
                    act.wait_ge(s["h_pre_ready"], g * GB + b + 1)
                    act.activation(h_act[:, b, :], h_pre[:, b, :], ACT.Gelu).then_inc(s["h_act_ready"], 1)
                for b in range(GB):
                    act.wait_ge(s["h_act_ready"], g * GB + b + 1)
                    act.activation(sq_scr[:, b, :], h_act[:, b, :], ACT.Square,
                                   accum_out=ssq[:, 1, b:b + 1]).then_inc(s["ssq2"], 1)
                for b in range(GB):
                    act.wait_ge(s["q2T_psum"], g * GB + b + 1)
                    act.copy(q2_T[:, b, :], bank[5 + b % 2][:, 0:F // 2].bitcast(bf16)).then_inc(s["q2T_ready"], 1)

        @block.vector
        def _(dve):
            order = Order(dve, s["v_order"])
            v, link = nc.vector, order.link

            dve.wait_ge(s["cols_psum"], 1)
            v.tensor_copy(cols[:, :], bank[6][:, 0:52]).then_inc(s["cols_ready"], 1)
            dve.wait_ge(s["agg_psum"], 1)
            v.tensor_copy(agg[:, :, :].rearrange("p b r -> p (b r)"), bank[5][:, 0:3 * B]).then_inc(s["agg_ready"], 1)
            dve.wait_ge(s["gate_in"], 64)
            dve.wait_ge(s["gate_psum"], 1)
            order.step(v.tensor_tensor(mod[:, :], bank[7][0:B, 16:16 + 2 * E], time_b_sb[:, :], ALU.add))
            link(v.tensor_tensor(gl[:, :], bank[7][0:B, 32:32 + E], gate_b_sb[:, :], ALU.add))
            link(v.scalar_tensor_tensor(out=gl[:, :], in0=mod[:, 0:E], scalar=1.0, in1=gl[:, :],
                                        op0=ALU.add, op1=ALU.mult))
            link(v.tensor_tensor(gl[:, :], gl[:, :], mod[:, E:2 * E], ALU.add))
            v.tensor_reduce(gmax[:, :], gl[:, :], AX.X, ALU.max, negate=True).then_inc(s["gl_ready"], 1)
            dve.wait_ge(s["prob_exp"], 1)
            link(v.reciprocal(gsum[:, :], gsum[:, :]))
            link(v.tensor_scalar(prob[:, :], prob[:, :], gsum[:, 0:1], None, ALU.mult))
            mine = prob[:, :].unsqueeze(2).broadcast_to([B, E, E])
            other = prob[:, :].unsqueeze(1).broadcast_to([B, E, E])
            dve.wait_ge(s["consts"], 1)
            order.step(v.tensor_tensor(gt[:, :, :], other, mine, ALU.is_gt))
            link(v.tensor_tensor(eq[:, :, :], other, mine, ALU.is_equal))
            link(v.tensor_tensor(eq[:, :, :], eq[:, :, :], lower[:, :, :], ALU.mult))
            link(v.tensor_tensor(gt[:, :, :], gt[:, :, :], eq[:, :, :], ALU.add))
            link(v.tensor_reduce(rank[:, :], gt[:, :, :], AX.X, ALU.add))
            link(v.scalar_tensor_tensor(out=wsel[:, :], in0=rank[:, :], scalar=2.0, in1=prob[:, :],
                                        op0=ALU.is_lt, op1=ALU.mult))
            link(v.tensor_reduce(gsum[:, :], wsel[:, :], AX.X, ALU.add))
            link(v.tensor_scalar(gsum[:, :], gsum[:, :], 1e-8, None, ALU.add))
            link(v.reciprocal(gsum[:, :], gsum[:, :]))
            link(v.tensor_scalar(wsel[:, :], wsel[:, :], gsum[:, 0:1], None, ALU.mult))
            v.tensor_tensor(wexp[:, :, :], wsel[:, :].unsqueeze(1).broadcast_to([B, B, E]),
                            ident[0:B, 0:B].unsqueeze(2).broadcast_to([B, B, E]), ALU.mult)\
                .then_inc(s["wexp_ready"], 1)
            dve.wait_ge(s["wcol_psum"], 1)
            v.tensor_copy(wcol[:, :, :].rearrange("p b e -> p (b e)"), bank[4][:, 0:B * E]).then_inc(s["wcol_ready"], 1)

            dve.sem_inc(s["y_part"], ER)
            dve.sem_inc(s["tail_done"], 1)
            dve.wait_ge(s["wm_ready"], 1)
            dve.wait_ge(s["in_in"], 16 * 6)
            with dve.Fori(0, NG) as g:
                dve.wait_ge(s["down_done"], 4 + g * UNITS + HC)
                dve.wait_ge(s["c_T_done"], g + 1)
                v.tensor_scalar(c_grp[:, :], bank[Y_BANK[0]][:, :], col(C_SB2), None, ALU.add)\
                    .then_inc(s["y_part"], 1)
                for e in range(E):
                    dve.wait_ge(s["down_done"], 4 + g * UNITS + HC * (e + 2))
                    dve.wait_ge(s["p_add"], g * E + e + 1)
                    v.scalar_tensor_tensor(out=part_y[:, e % 2, :], in0=bank[Y_BANK[e + 1]][:, :],
                                           scalar=col(C_EB2 + e), in1=wm[:, e, bass.ds(g * GT, GT)],
                                           op0=ALU.add, op1=ALU.mult).then_inc(s["y_part"], 1)
                dve.wait_ge(s["tail_psum"], g + 1)
                v.tensor_tensor(grp(res, g), bank[7][:, :], grp(x_tok, g), ALU.add).then_inc(s["v_order"], 1)
                v.tensor_tensor(dt_raw[:, bass.ds(g * GB, GB), :],
                                bank[5][:, 0:GB * NH].rearrange("p (b h) -> p b h", h=NH),
                                dt_bias_sb[:, :].unsqueeze(1).broadcast_to([P, GB, NH]), ALU.add)\
                    .then_inc(s["tail_done"], 1)
            order.count += NG
            dve.wait_ge(s["tail_done"], NG + 1)
            order.wait()

            raw = dt_raw[:, :, :].rearrange("p b h -> p (b h)")
            dts = dt_all[:, :, :].rearrange("p b h -> p (b h)")
            link(v.tensor_scalar(dts, raw, 0.0, None, ALU.max))
            v.scalar_tensor_tensor(out=dt_t[0][:, :], in0=dts, scalar=2.0, in1=raw,
                                   op0=ALU.mult, op1=ALU.subtract).then_inc(s["dt_in"], 1)
            dve.wait_ge(s["dt_exp"], 2)
            v.tensor_scalar(dt_t[2][:, :], dt_t[1][:, :], 1.0, None, ALU.add).then_inc(s["dt_w"], 1)
            dve.wait_ge(s["dt_w"], 1)
            link(v.scalar_tensor_tensor(out=dt_t[1][:, :], in0=dt_t[2][:, :], scalar=1.0, in1=dt_t[1][:, :],
                                        op0=ALU.subtract, op1=ALU.subtract))
            dve.wait_ge(s["dt_ln"], 1)
            link(v.tensor_tensor(dt_t[3][:, :], dt_t[3][:, :], dt_t[1][:, :], ALU.subtract))
            link(v.tensor_tensor(dts, dts, dt_t[3][:, :], ALU.add))
            v.tensor_tensor(dt_t[0][:, :].rearrange("p (b h) -> p b h", h=NH), dt_all[:, :, :],
                            A_pos[:, :].unsqueeze(1).broadcast_to([P, B, NH]), ALU.mult).then_inc(s["dt_mul"], 1)

            for k in range(2):
                dve.wait_ge(s["in_psum"], k + 1)
                n = 4 * P if k == 0 else 2 * P
                v.tensor_copy(in_T[:, k * 4 * P:k * 4 * P + n], bank[k][:, 0:n]).then_inc(s["in_ready"], 1)
            dve.wait_ge(s["out_psum"], 1)
            for j in range(JI):
                v.tensor_scalar(out_T[:, j, :], bank[2][:, j * P:(j + 1) * P], col(C_NW + j), None, ALU.mult)\
                    .then_inc(s["out_ready"], 1)
            for h in range(NH):
                lo = h % 2 * HD
                v.tensor_scalar(D_diag[lo:lo + HD, h // 2, :], ident[lo:lo + HD, :], D_all[lo:lo + HD, h:h + 1],
                                None, ALU.mult).then_inc(s["diag_ready"], 1)
            dve.wait_ge(s["uw_psum"], 1)
            v.tensor_copy(uw[:, :], bank[4][0:B, 0:P]).then_inc(s["uw_ready"], 1)
            for g in range(NG):
                dve.wait_ge(s["eb_psum"], g + 1)
                v.tensor_copy(e_bias[:, g * GB:(g + 1) * GB, :].rearrange("p b c -> p (b c)"), bank[g][:, :])\
                    .then_inc(s["eb_ready"], 1)
            dve.wait_ge(s["sum_psum"], 1)
            link(v.tensor_scalar(wmean[:, :], bank[5][:, 0:2], 1.0 / (F * DM), 1e-5, ALU.mult, ALU.max))
            link(v.reciprocal(wscale[:, :], wmean[:, :]))
            for k, (nat, q) in enumerate(((w1_nat[:, :, :].rearrange("p c d -> p (c d)"),
                                           w1_q[:, :, :].rearrange("p c d -> p (c d)")),
                                          (w2_nat[:, :], w2_q[:, :]))):
                link(v.tensor_scalar(wtmp[:, k, :], nat, wscale[:, k:k + 1], MAGIC, ALU.mult, ALU.add))
                link(v.tensor_scalar(wtmp[:, k, :], wtmp[:, k, :], MAGIC, 1.0, ALU.subtract, ALU.min))
                v.tensor_scalar(q, wtmp[:, k, :], -1.0, None, ALU.max).then_inc(s["w_q_ready"], 1)
            for k, dst in enumerate((w1_qT[:, :], w2_qT[:, :, :].rearrange("p c d -> p (c d)"))):
                dve.wait_ge(s["w_qT_psum"], k + 1)
                v.tensor_copy(dst, bank[6 + k][:, 0:256].bitcast(bf16)).then_inc(s["w_qT_ready"], 1)
            dve.wait_ge(s["dt_exp"], 3)
            link(v.memset(dA_all[0:1, :, :], 0.0))

            dve.sem_inc(s["e_ready"], 1)
            with dve.Fori(0, NG) as g:
                order.enter(g, JC * (KW - 2) + 1)
                v.tensor_copy(dA_grp[:, :], grp(dA_all, g)).then_inc(s["dA_grp_ready"], 1)
                marks = {}
                for k in range(1, KW):
                    for j in range(JC):
                        if k == 1:
                            dve.wait_ge(s["tap_first"], g * JC + j + 1)
                        else:
                            order.wait(marks[k - 1, j])
                        acc = conv[:, j, :].rearrange("p (b t) -> p b t", t=L)[:, :, k:L]
                        src = bank[2 + j][:, :].rearrange("p (b t) -> p b t", t=L)[:, :, 0:L - k]
                        ins = v.scalar_tensor_tensor(out=acc, in0=src, scalar=conv_w_sb[:, j, KW - 1 - k:KW - k],
                                                     in1=acc, op0=ALU.mult, op1=ALU.add)
                        if k < KW - 1:
                            marks[k, j] = order.step(ins)
                        else:
                            ins.then_inc(s["conv_done"], 1)
                for m in range(2):
                    dve.wait_ge(s["xs_T_psum"], g * 2 + m + 1)
                    dtb = dt_all[:, bass.ds(g * GB + 2 * m, 2), :].rearrange("p b h -> p (b h)")
                    v.tensor_tensor(x_dt[:, 2 * m:2 * m + 2, :].rearrange("p b (h q) -> p (b h) q", q=HD),
                                    bank[2 + m][:, :].rearrange("p (m q) -> p m q", q=HD),
                                    dtb.unsqueeze(2).broadcast_to([P, 2 * NH, HD]),
                                    ALU.mult).then_inc(s["x_dt_ready"], 1)
                dve.wait_ge(s["g_psum"], g + 1)
                for b in range(GB):
                    dve.wait_ge(s["bc_psum"], g * GB + b + 1)
                    if b >= 2:
                        dve.wait_ge(s["mix_ready"], g * GB + b - 1)
                    v.tensor_tensor_scan(out=decay[:, b % 2, :], data0=bank[5 + b % 2][:, :],
                                         data1=ident4[:, :, :].rearrange("p h t -> p (h t)"), initial=0.0,
                                         op0=ALU.mult, op1=ALU.add).then_inc(s["scan_done"], 1)
                    dve.wait_ge(s["scan_done"], g * GB + b + 1)
                    if b >= 2:
                        dve.wait_ge(s["y_psum"], g * GB + b - 1)
                    v.tensor_tensor(mixer[:, b % 2, :].rearrange("p (h t) -> p h t", t=L),
                                    decay[:, b % 2, :].rearrange("p (h t) -> p h t", t=L),
                                    bank[4][:, b * L:(b + 1) * L].unsqueeze(1).broadcast_to([P, NH, L]),
                                    ALU.mult).then_inc(s["mix_ready"], 1)
                dve.wait_ge(s["z_ready"], (g + 1) * JI)
                dve.wait_ge(s["y_psum"], (g + 1) * GB)
                for j in range(JI):
                    v.tensor_tensor(y_g[:, j, :], bank[j][:, :], z_act[:, j, :], ALU.mult)\
                        .then_inc(s["y_g_ready"], 1)
                dve.wait_ge(s["ss_psum"], g + 1)
                v.tensor_scalar(y_ms[:, :], bank[6][:, 0:GB], 1.0 / DI, EPS, ALU.mult, ALU.add)\
                    .then_inc(s["ms_ready"], 1)
                dve.wait_ge(s["yr_ready"], g + 1)
                for b in range(GB):
                    v.scalar_tensor_tensor(out=r_grp[:, b, :], in0=bank[7][:, b * DM:(b + 1) * DM],
                                           scalar=y_r[:, b:b + 1],
                                           in1=res[:, bass.ds(g * GB + b, 1), :].rearrange("p b d -> p (b d)"),
                                           op0=ALU.mult, op1=ALU.add).then_inc(s["r_grp_ready"], 1)
                dve.wait_ge(s["r_grp_ready"], (g + 1) * GB)
                order.step(v.tensor_tensor(res[:, bass.ds(g * GB, GB), :], r_grp[:, :, :],
                                           b2_sb[:, :].unsqueeze(1).broadcast_to([P, GB, DM]), ALU.add))
                dve.wait_ge(s["e_psum"], g + 1)
                v.tensor_tensor(grp(e_all, g), bank[3][:, :], grp(e_bias, g), ALU.add).then_inc(s["e_ready"], 1)
                order.leave(NG)

            dve.sem_inc(s["y_out_ready"], 1)

            def scales(k):
                v.tensor_scalar(ms[:, k, :], ssq[:, k, :], 1.0 / (DM, F)[k], EPS, ALU.mult, ALU.add)\
                    .then_inc(s[f"ms{k + 1}"], 1)
                dve.wait_ge(s[f"rr{k + 1}"], g + 1)
                link(v.tensor_tensor(cl[:, k, :], amax[:, k, :], rr[:, k, :], ALU.mult))
                link(v.tensor_scalar(cl[:, k, :], cl[:, k, :], 1e-5, None, ALU.max))
                order.step(v.tensor_scalar(qk[:, k, :], cl[:, k, :], 1.0 / 127.0, wmean[:, k:k + 1], ALU.mult, ALU.mult))
                link(v.reciprocal(inv[:, k, :], cl[:, k, :]))
                link(v.scalar_tensor_tensor(out=qm[:, k, :], in0=inv[:, k, :], scalar=127.0, in1=rr[:, k, :],
                                            op0=ALU.mult, op1=ALU.mult))

            dve.wait_ge(s["e_ready"], NG + 1)
            with dve.Fori(0, NG) as g:
                order.enter(g, 1 + 5 + GB + GB + 5 + GB)
                order.step(v.tensor_reduce(amax[:, 0, :], e_all[:, bass.ds(g * GB, GB), :], AX.X, ALU.max,
                                           apply_absolute_value=True))
                dve.wait_ge(s["ssq1"], (g + 1) * GB)
                dve.wait_ge(s["y_out_ready"], g + 1)
                scales(0)
                for b in range(GB):
                    order.step(v.tensor_scalar(q1_f[:, b * DM:(b + 1) * DM],
                                               e_all[:, bass.ds(g * GB + b, 1), :].rearrange("p b d -> p (b d)"),
                                               qm[:, 0, b:b + 1], MAGIC, ALU.mult, ALU.add))
                order.wait()
                v.tensor_scalar(q1[:, :], q1_f[:, :], MAGIC, None, ALU.subtract).then_inc(s["q1_ready"], 1)
                for b in range(GB):
                    dve.wait_ge(s["h_psum"], g * GB + b + 1)
                    v.scalar_tensor_tensor(out=h_pre[:, b, :], in0=bank[1 + b][:, :], scalar=qk[:, 0, b:b + 1],
                                           in1=b1_sb[:, :], op0=ALU.mult, op1=ALU.add).then_inc(s["h_pre_ready"], 1)
                for b in range(GB):
                    dve.wait_ge(s["h_act_ready"], g * GB + b + 1)
                    order.step(v.tensor_reduce(amax[:, 1, b:b + 1], h_act[:, b, :], AX.X, ALU.max,
                                               apply_absolute_value=True))
                dve.wait_ge(s["ssq2"], (g + 1) * GB)
                scales(1)
                for b in range(GB):
                    link(v.tensor_scalar(q2_f[:, b, :], h_act[:, b, :], qm[:, 1, b:b + 1], MAGIC, ALU.mult, ALU.add))
                    v.tensor_scalar(q2[:, b, :], q2_f[:, b, :], MAGIC, None, ALU.subtract).then_inc(s["q2_ready"], 1)
                dve.wait_ge(s["o_psum"], g + 1)
                dve.wait_ge(s["out_sent"], g * 16 + 16)
                for b in range(GB):
                    ins = v.scalar_tensor_tensor(out=y_out[:, b, :], in0=bank[7][:, b * DM:(b + 1) * DM],
                                                 scalar=qk[:, 1, b:b + 1],
                                                 in1=res[:, bass.ds(g * GB + b, 1), :].rearrange("p b d -> p (b d)"),
                                                 op0=ALU.mult, op1=ALU.add)
                ins.then_inc(s["y_out_ready"], 1)
                order.leave(NG)

        @block.tensor
        def _(pe):
            mm, tr = pe.matmul, pe.transpose

            pe.wait_ge(s["consts"], 1)
            pe.wait_ge(s["x_in"], 16 * NG)
            for g in range(NG):
                if g >= 2:
                    pe.wait_ge(s["x_T_ready"], g - 1)
                for b in range(GB):
                    ins = tr(bank[g % 2][:, b * L:(b + 1) * L], x_tok[:, g * GB + b, :], ident[:, :])
                ins.then_inc(s["x_T_psum"], 1)
            pe.wait_ge(s["rows_in"], 16 * 9)
            tr(bank[6][:, 0:52], rows[:, :], ident[0:52, 0:52]).then_inc(s["cols_psum"], 1)
            for b in range(B):
                ins = mm(bank[5][:, 3 * b:3 * b + 3], x_tok[:, b, :], regions[:, :], start=True, stop=True)
            ins.then_inc(s["agg_psum"], 1)
            pe.wait_ge(s["silu_ready"], 1)
            pe.wait_ge(s["gate_in"], 64)
            mm(bank[7][0:B, 16:16 + 2 * E], cond_silu[:, :], time_w_sb[:, :], start=True, stop=True)
            pe.wait_ge(s["agg_ready"], 1)
            for j in range(3):
                ins = mm(bank[7][0:B, 32:32 + E], agg[:, :, j], gate_w_sb[:, j, :], start=(j == 0), stop=(j == 2))
            ins.then_inc(s["gate_psum"], 1)
            pe.wait_ge(s["wexp_ready"], 1)
            mm(bank[4][:, 0:B * E], ones[0:B, :], wexp[:, :, :].rearrange("k b e -> k (b e)"), start=True, stop=True)\
                .then_inc(s["wcol_psum"], 1)

            pe.sem_inc(s["down_done"], 4)
            pe.wait_ge(s["shared_in"], 32)
            pe.wait_ge(s["x_T_ready"], NG)
            pe.wait_ge(s["wcol_ready"], 1)
            with pe.Fori(0, NG) as g:
                for i in range(UNITS + AHEAD):
                    if i < UNITS:
                        e, c = divmod(i, HC)
                        if i == HC:
                            pe.wait_ge(s["experts_in"], 16 * 2 * E)
                        pe.wait_ge(s["gelu_done"], g * UNITS + i + 1)
                        mm(bank[i % 4][:, :], w_up[:, e, c * P:(c + 1) * P], x_T[:, bass.ds(g * GT, GT)],
                           start=True, stop=True).then_inc(s["up_done"], 1)
                    if i >= AHEAD:
                        k = i - AHEAD
                        e, c = divmod(k, HC)
                        if c == 0:
                            last = {0: 3, 1: 4, 2: ER + 1, 3: ER + 2, 4: 5}[e]
                            pe.wait_ge(s["y_part"], g * ER + last)
                            if e == 1:
                                pe.wait_ge(s["tail_done"], g + 1)
                        pe.wait_ge(s["gelu_done"], 4 + g * UNITS + k + 1)
                        mm(bank[Y_BANK[e]][:, :], w_down[:, e, c, :], hid[:, k % 4, :],
                           start=(c == 0), stop=(c == HC - 1)).then_inc(s["down_done"], 1)
                pe.wait_ge(s["p_add"], 2 + (g + 1) * E)
                pe.wait_ge(s["y_part"], ER + g * ER + 4)
                for b in range(GB):
                    tr(bank[7][:, b * DM:(b + 1) * DM], c_grp[:, b * L:(b + 1) * L], ident[:, :])
                for b in range(GB):
                    ins = mm(bank[5][:, b * NH:(b + 1) * NH], c_grp[:, b * L:(b + 1) * L], col(C_DT, NH),
                             start=True, stop=True)
                ins.then_inc(s["tail_psum"], 1)

            pe.wait_ge(s["in_in"], 16 * 6)
            pe.wait_ge(s["gelu_done"], 4 + NG * UNITS)
            for c in range(6):
                ins = tr(bank[c // 4][:, c % 4 * P:(c % 4 + 1) * P], in_nat[:, c, :], ident[:, :])
                if c in (3, 5):
                    ins.then_inc(s["in_psum"], 1)
            for j in range(JI):
                ins = tr(bank[2][:, j * P:(j + 1) * P], out_nat[:, j * P:(j + 1) * P], ident[:, :])
            ins.then_inc(s["out_psum"], 1)
            pe.wait_ge(s["mix_in"], 32)
            mm(bank[3][:, 0:B], proj_sb[:, :], col(C_COND, B), start=True, stop=True).then_inc(s["u_psum"], 1)
            pe.wait_ge(s["u_ready"], 1)
            pe.wait_ge(s["y_part"], ER + NG * ER)
            pe.wait_ge(s["tail_done"], NG + 1)
            mm(bank[4][0:B, 0:P], u_T[:, :], mix_sb[:, 0, :], start=True, stop=True).then_inc(s["uw_psum"], 1)
            pe.wait_ge(s["abs_done"], 2)
            mm(bank[5][:, 0:2], ones[:, :], wsum[:, :], start=True, stop=True).then_inc(s["sum_psum"], 1)
            pe.wait_ge(s["uw_ready"], 1)
            for g in range(NG):
                if g < 2:
                    pe.wait_ge(s["in_ready"], g + 1)
                elif g == 2:
                    pe.wait_ge(s["out_ready"], JI)
                for b in range(GB):
                    bb = g * GB + b
                    ins = mm(bank[g][:, b * P:(b + 1) * P], ident[0:B, bb:bb + 1].broadcast_to([B, P]), uw[:, :],
                             start=True, stop=True)
                ins.then_inc(s["eb_psum"], 1)
            for k, (q, bk) in enumerate(((w1_q, 6), (w2_q, 7))):
                pe.wait_ge(s["w_q_ready"], k + 1)
                for c in range(FC):
                    src = q[:, c, :] if k == 0 else q[:, c * P:(c + 1) * P]
                    ins = tr(bank[bk][:, c * P // 2:(c + 1) * P // 2].bitcast(bf16), src, identb[:, :])
                ins.then_inc(s["w_qT_psum"], 1)
            pe.wait_ge(s["w_qT_ready"], 2)
            pe.wait_ge(s["eb_ready"], NG)
            pe.wait_ge(s["diag_ready"], NH)

            def inputs(g, j):
                return xbc[:, j, :]

            with pe.Fori(0, NG) as g:
                tokens = c_T[:, bass.ds(g * GT, GT)]
                for j in range(JI):
                    mm(bank[j][:, :], in_T[:, j * P:(j + 1) * P], tokens, start=True, stop=True)\
                        .then_inc(s["z_psum"], 1)
                for j in range(JC):
                    if j == 1:
                        pe.wait_ge(s["e_ready"], g + 1)
                    mm(bank[2 + j][:, :], in_T[:, DI + j * P:DI + (j + 1) * P], tokens, start=True, stop=True)\
                        .then_inc(s["xbc_psum"], 1)
                for j in range(JI):
                    pe.wait_ge(s["z_ready"], g * JI + j + 1)
                    pe.wait_ge(s["xbc_ready"], g * JC + j + 1)
                    mm(bank[j][:, :], D_diag[:, j, :], xbc[:, j, :], start=True, stop=False)
                for b in range(GB):
                    for j in range(JI):
                        ins = tr(bank[2 + b // 2][:, (b % 2 * JI + j) * P:(b % 2 * JI + j + 1) * P],
                                 xbc[:, j, b * L:(b + 1) * L], ident[:, :])
                    if b % 2:
                        ins.then_inc(s["xs_T_psum"], 1)
                pe.wait_ge(s["xbc_ready"], (g + 1) * JC)
                for b in range(GB):
                    ins = mm(bank[4][:, b * L:(b + 1) * L], xbc[:, JI, b * L:(b + 1) * L],
                             xbc[:, JI + 1, b * L:(b + 1) * L], start=True, stop=True)
                ins.then_inc(s["g_psum"], 1)

                def spread(b):
                    if b >= 2:
                        pe.wait_ge(s["scan_done"], g * GB + b - 1)
                    for h in range(NH):
                        ins = mm(bank[5 + b % 2][:, h * L:(h + 1) * L],
                                 dA_grp[:, b * NH + h:b * NH + h + 1].broadcast_to([P, P]), ident[:, :],
                                 start=True, stop=True)
                    ins.then_inc(s["bc_psum"], 1)

                pe.wait_ge(s["dA_grp_ready"], g + 1)
                spread(0)
                spread(1)
                for b in range(GB):
                    pe.wait_ge(s["mix_ready"], g * GB + b + 1)
                    pe.wait_ge(s["x_dt_ready"], g * 2 + b // 2 + 1)
                    for h in range(NH):
                        lo = h % 2 * HD
                        ins = mm(bank[h // 2][lo:lo + HD, b * L:(b + 1) * L], x_dt[:, b, h * HD:(h + 1) * HD],
                                 mixer[:, b % 2, h * L:(h + 1) * L], start=False, stop=(b == GB - 1))
                    ins.then_inc(s["y_psum"], 1)
                    if b + 2 < GB:
                        spread(b + 2)
                pe.wait_ge(s["y_g_ready"], (g + 1) * JI)
                for b in range(GB):
                    for j in range(JI):
                        mm(bank[7][:, b * DM:(b + 1) * DM], y_g[:, j, b * L:(b + 1) * L], out_T[:, j, :],
                           start=(j == 0), stop=(j == JI - 1))
                pe.wait_ge(s["y_sq_ready"], (g + 1) * JI)
                for b in range(GB):
                    for j in range(JI):
                        ins = mm(bank[6][:, b:b + 1], y_sq[:, j, b * L:(b + 1) * L], ones[:, 0:1],
                                 start=(j == 0), stop=(j == JI - 1))
                ins.then_inc(s["ss_psum"], 1)
                pe.wait_ge(s["r_grp_ready"], (g + 1) * GB)
                for b in range(GB):
                    ins = tr(bank[2][:, b * L:(b + 1) * L], r_grp[:, b, :], ident[:, :])
                ins.then_inc(s["rT_psum"], 1)
                pe.wait_ge(s["rT_ready"], g + 1)
                for b in range(GB):
                    ins = mm(bank[3][:, b * P:(b + 1) * P], r_T[:, b * L:(b + 1) * L], mix_sb[:, 1, :],
                             start=True, stop=True)
                ins.then_inc(s["e_psum"], 1)

            with pe.Fori(0, NG) as g:
                pe.wait_ge(s["q1_ready"], g + 1)
                for b in range(GB):
                    ins = tr(bank[0][:, b * L // 2:(b + 1) * L // 2].bitcast(bf16), q1[:, b * DM:(b + 1) * DM],
                             identb[:, :])
                ins.then_inc(s["q1T_psum"], 1)
                pe.wait_ge(s["q1T_ready"], g + 1)
                for b in range(GB):
                    mm(bank[1 + b][:, :], q1_T[:, b * L:(b + 1) * L], w1_qT[:, :], start=True, stop=True)\
                        .then_inc(s["h_psum"], 1)
                pe.wait_ge(s["y_out_ready"], g + 1)
                for b in range(GB):
                    pe.wait_ge(s["q2_ready"], g * GB + b + 1)
                    if b >= 2:
                        pe.wait_ge(s["q2T_ready"], g * GB + b - 1)
                    for c in range(FC):
                        ins = tr(bank[5 + b % 2][:, c * L // 2:(c + 1) * L // 2].bitcast(bf16),
                                 q2[:, b, c * P:(c + 1) * P], identb[:, :])
                    ins.then_inc(s["q2T_psum"], 1)
                for b in range(GB):
                    pe.wait_ge(s["q2T_ready"], g * GB + b + 1)
                    for c in range(FC):
                        ins = mm(bank[7][:, b * DM:(b + 1) * DM], q2_T[:, b, c * L:(c + 1) * L], w2_qT[:, c, :],
                                 start=(c == 0), stop=(c == FC - 1))
                ins.then_inc(s["o_psum"], 1)

    return nc


_INS = ["x", "cond_1024", "L0_cond_gate_w", "L0_cond_gate_b", "L0_cond_time_w", "L0_cond_time_b", "L0_cond_ew1",
        "L0_cond_eb1", "L0_cond_ew2", "L0_cond_eb2", "L0_cond_sw1", "L0_cond_sb1", "L0_cond_sw2", "L0_cond_sb2",
        "L0_attn_in_proj_w", "L0_attn_conv_w", "L0_attn_conv_b", "L0_attn_dt_bias", "L0_attn_A_log", "L0_attn_D",
        "L0_attn_norm_w", "L0_attn_out_proj_w", "L0_cond2_weight_matrix", "L0_cond2_W_proj", "L0_cond2_b_proj",
        "L0_ffn_w1", "L0_ffn_b1", "L0_ffn_w2", "L0_ffn_b2"]


def kernel(**inputs):
    import numpy as _np
    import concourse.bacc as _bacc
    from concourse import mybir as _mybir
    from concourse.bass_utils import run_bass_kernel_spmd as _run

    nc = _bacc.Bacc("TRN2", target_bir_lowering=False, num_devices=1)
    arrays, args = {}, []
    for name in _INS:
        a = _np.ascontiguousarray(inputs[name])
        arrays[f"in_{name}"] = a
        args.append(nc.dram_tensor(f"in_{name}", a.shape, _mybir.dt.from_np(a.dtype), kind="ExternalInput").ap())
    args.append(nc.dram_tensor("out_dram", inputs["x"].shape, _mybir.dt.float32, kind="ExternalOutput").ap())
    build(nc, *args)
    r = _run(nc, [arrays], core_ids=[0])
    return r.results[0]["out_dram"]
```

```python
import concourse.bass as bass
from concourse import mybir
from contextlib import ExitStack


class Order:

    def __init__(self, eng, sem):
        self.eng, self.sem, self.count, self.turn, self.per = eng, sem, 0, None, 0

    def step(self, ins):
        self.count += 1
        ins.then_inc(self.sem, 1)
        return self.count

    def wait(self, mark=None):
        mark = self.count if mark is None else mark
        self.eng.wait_ge(self.sem, mark if self.turn is None else self.turn * self.per + mark)

    def link(self, ins):
        self.step(ins)
        self.wait()

    def enter(self, turn, per):
        self.turn, self.per, self.first = turn, per, self.count

    def leave(self, turns):
        assert self.count - self.first == self.per, (self.count - self.first, self.per)
        self.turn, self.count = None, self.first + turns * self.per


class Stage:

    def __init__(self, eng, sem, per):
        self.eng, self.sem, self.per, self.base, self.n = eng, sem, per, None, per

    def group(self, g):
        assert self.n == self.per, (self.n, self.per)
        self.base, self.n = g * self.per, 0

    def step(self, ins):
        self.n += 1
        ins.then_inc(self.sem, 1)
        return self.n

    def wait(self, mark=None):
        self.eng.wait_ge(self.sem, self.base + (self.n if mark is None else mark))

    def link(self, ins):
        self.step(ins)
        self.wait()


def build(nc, x, cond, gate_w, gate_b, time_w, time_b, ew1, eb1, ew2, eb2, sw1, sb1, sw2, sb2,
          in_w, conv_w, conv_b, dt_bias, A_log, D, norm_w, out_w, mix_w, proj_w, proj_b,
          f_w1, f_b1, f_w2, f_b2, out):
    f32 = mybir.dt.float32
    bf16 = mybir.dt.bfloat16
    f16 = mybir.dt.float16
    ALU = mybir.AluOpType
    ACT = mybir.ActivationFunctionType
    AX = mybir.AxisListType

    P = 128
    B, L, DM = x.shape
    E = gate_w.shape[1]
    H = sw1.shape[1]
    HC = H // P
    DI = out_w.shape[1]
    JI = DI // P
    NH = dt_bias.shape[0]
    HD = DI // NH
    CD = conv_w.shape[0]
    JC = CD // P
    KW = conv_w.shape[1]
    F = f_w1.shape[0]
    FC = F // P
    GB = 4
    NG = B // GB
    GT = GB * L
    L3 = L // 3
    EPS = 1e-5
    MAGIC = 1.5 * 2.0 ** 23
    K = 2
    U = GB * K
    XS, WS, CS, IS = 8.0, 1024.0, 8.0, 64.0

    ctx = ExitStack()
    with ctx:
        def sb(name, shape, dt=f32):
            return ctx.enter_context(nc.sbuf_tensor(name, shape, dt))

        def sem(name):
            return ctx.enter_context(nc.semaphore(name))

        bank = [ctx.enter_context(nc.psum_tensor(f"bank{i}", [P, 512], f32)) for i in range(8)]

        x_tok = sb("x_tok", [P, B, DM])
        x_hi = sb("x_hi", [P, B * L], f16)
        x_lo = sb("x_lo", [P, B * L], f16)
        c_hi = sb("c_hi", [P, B * L], f16)
        c_lo = sb("c_lo", [P, B * L], f16)
        c_grp = sb("c_grp", [P, GB, DM])
        res = sb("res", [P, B, DM])
        dt_raw = sb("dt_raw", [P, B, NH])

        up_nat = sb("up_nat", [P, E + 1, H])
        up_hi = sb("up_hi", [P, (E + 1) * H], f16)
        up_lo = sb("up_lo", [P, (E + 1) * H], f16)
        down = sb("down", [P, (E + 1) * HC * DM])
        eb1_rows = sb("eb1_rows", [E, H])
        b2_rows = sb("b2_rows", [E + 1, DM])
        rows = sb("rows", [27, P])
        cols = sb("cols", [P, 27])
        C_SB1, C_CB, C_PB, C_NW, C_COND, C_END = 0, 4, 8, 9, 11, 27
        gate_w_sb = sb("gate_w_sb", [P, 3, E])
        gate_b_sb = sb("gate_b_sb", [B, E])
        time_w_sb = sb("time_w_sb", [P, 2 * E])
        time_b_sb = sb("time_b_sb", [B, 2 * E])
        in_nat = sb("in_nat", [P, 6, DM])
        in_nat_dt = sb("in_nat_dt", [NH, DM])
        TAP0 = DI + NH
        in_hi = sb("in_hi", [P, TAP0 + KW * CD], f16)
        in_lo = sb("in_lo", [P, TAP0 + KW * CD], f16)
        conv_w_sb = sb("conv_w_sb", [P, JC, KW])
        dt_bias_sb = sb("dt_bias_sb", [P, NH])
        A_sb = sb("A_sb", [P, NH])
        A_pos = sb("A_pos", [P, NH])
        D_all = sb("D_all", [P, NH])
        D_col = sb("D_col", [P, JI])
        out_nat = sb("out_nat", [P, DI])
        out_T = sb("out_T", [P, JI, DM])
        mix_sb = sb("mix_sb", [P, 2, P])
        proj_sb = sb("proj_sb", [P, P])
        w1_nat = sb("w1_nat", [P, FC, DM])
        w2_nat = sb("w2_nat", [P, F])
        w1_q = sb("w1_q", [P, FC, DM], bf16)
        w2_q = sb("w2_q", [P, F], bf16)
        w1_qT = sb("w1_qT", [P, F], bf16)
        w2_qT = sb("w2_qT", [P, FC, DM], bf16)
        b1_sb = sb("b1_sb", [P, F])
        b2_sb = sb("b2_sb", [P, DM])

        ident = sb("ident", [P, P])
        identb = sb("identb", [P, P], bf16)
        ident4 = sb("ident4", [P, NH, L])
        ones = sb("ones", [P, P])
        regions = sb("regions", [P, 3])
        part = sb("part", [P, 1])
        lower = sb("lower", [B, E, E])
        number = sb("number", [B, 2, E])
        mask = sb("mask", [P, E + 1])
        mask_T = sb("mask_T", [E + 1, P])
        minus_half = sb("minus_half", [P, GB])

        agg = sb("agg", [P, B, 3])
        cond_silu = sb("cond_silu", [P, B])
        mod = sb("mod", [B, 2 * E])
        gl = sb("gl", [B, E])
        gmax = sb("gmax", [B, 1])
        gsum = sb("gsum", [B, 1])
        prob = sb("prob", [B, E])
        gt = sb("gt", [B, E, E])
        eq = sb("eq", [B, E, E])
        rank = sb("rank", [B, E])
        pick = sb("pick", [B, K, E])
        w_all = sb("w_all", [B, E + 1])
        sent = sb("sent", [B, K * E + K])
        spread = sb("spread", [B, B, K * E + K])
        picked = sb("picked", [B, K, E])
        w_tok = sb("w_tok", [P, B * K, E])
        w_slot = sb("w_slot", [P, B, K])
        offset = sb("offset", [1, B * K], mybir.dt.int32)
        pick_T = sb("pick_T", [E, K, B])
        w_T = sb("w_T", [E + 1, B])
        w_mask_T = sb("w_mask_T", [E + 1, GB, L])
        slot_bias = sb("slot_bias", [P, B, K, HC])

        hid_s = sb("hid_s", [P, HC, GT])
        pre = sb("pre", [P, 2, HC * L])
        hid = sb("hid", [P, 4, HC * L])

        dt_all = sb("dt_all", [P, B, NH])
        dA_all = sb("dA_all", [P, B, NH])
        dt_t = [sb(f"dt_t{i}", [P, B * NH]) for i in range(4)]
        dA_rest = sb("dA_rest", [P, 2, B * NH])
        dA_parts = sb("dA_parts", [P, 3, B * NH], bf16)
        dA_grp = sb("dA_grp", [P, 3, GB * NH], bf16)
        ffn_work = sb("ffn_work", [P, 4, 2048])
        z_act = sb("z_act", [P, JI, GT])
        xD = sb("xD", [P, JI, GT])
        xbc = sb("xbc", [P, JC, GT])
        x_dt = sb("x_dt", [P, GB, DI])
        decay = sb("decay", [P, 2, NH * L])
        mixer = sb("mixer", [P, 2, NH * L])
        y_g = sb("y_g", [P, JI, GT])
        y_sq = sb("y_sq", [P, JI, GT])
        y_ms = sb("y_ms", [P, GB])
        y_r = sb("y_r", [P, GB])
        r_grp = sb("r_grp", [P, GB, DM])
        r_T = sb("r_T", [P, GT])
        u_T = sb("u_T", [P, B])
        uw = sb("uw", [B, P])
        e_bias = hid_s[:, :, :].rearrange("p c (b d) -> p (c b) d", d=P)

        e_all = up_nat[:, 0:E, :].rearrange("p e (b d) -> p (e b) d", d=DM)
        in_taps = ffn_work[:, 0, :].rearrange("p (k n) -> p k n", k=KW)
        wabs = ffn_work[:, 2, 0:1024].rearrange("p (k n) -> p k n", k=2)
        wsum = sb("wsum", [P, 2])
        wmean = sb("wmean", [P, 2])
        wscale = sb("wscale", [P, 2])
        wtmp = ffn_work[:, 1, 0:1024].rearrange("p (k n) -> p k n", k=2)
        sq_scr = ffn_work[:, 2, :].rearrange("p (b f) -> p b f", f=F)
        ssq = sb("ssq", [P, 2, GB])
        amax = sb("amax", [P, 2, GB])
        ms = sb("ms", [P, 2, GB])
        rr = sb("rr", [P, 2, GB])
        cl = sb("cl", [P, 2, GB])
        inv = sb("inv", [P, 2, GB])
        qm = sb("qm", [P, 2, GB])
        qk = sb("qk", [P, 2, GB])
        q1_f = sb("q1_f", [P, GT])
        q1 = sb("q1", [P, GT], bf16)
        q1_T = sb("q1_T", [P, GT], bf16)
        h_pre = ffn_work[:, 0, :].rearrange("p (b f) -> p b f", f=F)
        h_act = ffn_work[:, 1, :].rearrange("p (b f) -> p b f", f=F)
        q2_f = ffn_work[:, 3, :].rearrange("p (b f) -> p b f", f=F)
        halves = hid[:, :, :].rearrange("p u n -> p (u n)").bitcast(bf16).rearrange("p (k b f) -> p k b f", k=2, f=F)
        q2, q2_T = halves[:, 0], halves[:, 1]
        y_out = sb("y_out", [P, GB, DM])

        names = """x_in shared_in experts_in rows_in gate_in in_in mix_in ffn_in out_sent
            v_order a_order p_order consts
            x_T_psum x_hi_ready x_lo_ready cols_psum cols_ready agg_psum agg_ready silu_ready gate_psum gl_ready
            prob_exp spread_ready sent_psum sent_ready gate_T_psum gate_T_ready slot_bias_psum slot_bias_ready
            w_slot_ready w_mask_T_ready up_hi_ready up_lo_ready
            up_s_done up_done pre_done gelu_s_done gelu_done down_s_done down_done y_s_copied y_added
            c_T_psum c_hi_ready c_lo_ready res_ready dt_psum
            in_psum in_hi_ready in_ready out_psum out_ready D_col_ready in_taps_ready u_psum u_ready uw_psum uw_ready eb_psum eb_ready
            abs_done sum_psum wmean_ready w_q_ready w_qT_psum w_qT_ready
            dt_in dt_exp dt_w dt_ln dt_mul
            z_psum z_ready xbc_psum xbc_ready xD_ready res_b2_ready v_b v_c dA_ready xs_T_psum x_dt_ready g_psum bc_psum
            scan_done mix_ready y_psum y_g_ready y_sq_ready m_psum ss_psum ms_ready yr_ready
            r_grp_ready rT_psum rT_ready e_psum e_ready dA_grp_ready
            ssq1 ms1 rr1 q1_ready q1T_psum q1T_ready h_psum h_pre_ready h_act_ready ssq2 ms2 rr2
            q2_ready q2T_psum q2T_ready o_psum y_out_ready""".split()
        s = {n: sem(n) for n in names}

        ROWS = 8

        def col(c, n=1):
            return cols[:, c:c + n]

        def in_part(k):
            return slice(TAP0 + (k - 1) * CD, TAP0 + k * CD) if k else slice(0, TAP0)

        def grp(t, g):
            return t[:, bass.ds(g * GB, GB), :].rearrange("p b d -> p (b d)")

        block = ctx.enter_context(nc.Block())

        @block.sync
        def _(sp):
            for g in range(NG):
                sp.dma_start(x_tok[:, g * GB:(g + 1) * GB, :],
                             x[g * GB:(g + 1) * GB, :, :].rearrange("b t d -> t b d")).then_inc(s["x_in"], 16)
            HD2 = HC * DM
            sp.dma_start(up_nat[:, E, :], sw1).then_inc(s["shared_in"], 16)
            sp.dma_start(down[:, E * HD2:(E + 1) * HD2].rearrange("p (c d) -> p c d", d=DM),
                         sw2.rearrange("(c p) d -> p c d", p=P)).then_inc(s["shared_in"], 16)
            for e in range(E):
                sp.dma_start(up_nat[:, e, :], ew1[e, :, :]).then_inc(s["experts_in"], 16)
                sp.dma_start(down[:, e * HD2:(e + 1) * HD2].rearrange("p (c d) -> p c d", d=DM),
                             ew2[e, :, :].rearrange("(c p) d -> p c d", p=P)).then_inc(s["experts_in"], 16)
            sp.sem_inc(s["out_sent"], 16)
            with sp.Fori(0, NG) as g:
                sp.wait_ge(s["y_out_ready"], g + 2)
                sp.dma_start(out[bass.ds(g * GB, GB), :, :].rearrange("b t d -> t b d"),
                             y_out[:, :, :]).then_inc(s["out_sent"], 16)
            sp.wait_ge(s["out_sent"], 16 * (NG + 1))

        @block.gpsimd
        def _(pool):
            order = Order(pool, s["p_order"])
            small = ((rows, sb1.rearrange("(c p) -> c p", p=P), C_SB1),
                     (rows, conv_b.rearrange("(c p) -> c p", p=P), C_CB),
                     (rows, proj_b.rearrange("(c p) -> c p", p=P), C_PB),
                     (rows, norm_w.rearrange("(c p) -> c p", p=P), C_NW), (rows, cond, C_COND),
                     (eb1_rows, eb1, 0), (b2_rows, eb2, 0), (b2_rows, sb2.rearrange("(c p) -> c p", p=P), E))
            for dst, src, c in small:
                pool.dma_start(dst[c:c + src.shape[0], :], src).then_inc(s["rows_in"], 16)
            assert len(small) == ROWS

            order.step(pool.memset(ident[:, :], 0.0))
            order.step(pool.memset(mask[:, :], 1.0))
            order.step(pool.memset(part[:, :], 1.0))
            order.step(pool.memset(lower[:, :, :], 1.0))
            order.step(pool.memset(ones[:, :], 1.0))
            order.step(pool.memset(minus_half[:, :], -0.5))
            for e in range(E):
                order.step(pool.memset(number[:, :, e:e + 1], float(e)))
            order.step(pool.memset(w_all[:, :], 1.0))
            order.wait()
            order.step(pool.affine_select(out=ident[:, :], in_=ident[:, :], compare_op=ALU.not_equal, fill=1.0,
                                          base=0, pattern=[[-1, P]], channel_multiplier=1))
            order.step(pool.affine_select(out=part[:, :], in_=part[:, :], compare_op=ALU.is_ge, fill=0.0,
                                          base=-2 * L3, pattern=[[0, 1]], channel_multiplier=1))
            order.step(pool.affine_select(out=mask[:, 1:2], in_=mask[:, 1:2], compare_op=ALU.is_gt, fill=0.0,
                                          base=L3, pattern=[[0, 1]], channel_multiplier=-1))
            order.step(pool.affine_select(out=mask[:, 2:3], in_=mask[:, 2:3], compare_op=ALU.is_ge, fill=0.0,
                                          base=-L3, pattern=[[0, 1]], channel_multiplier=1))
            order.step(pool.affine_select(out=lower[:, :, :], in_=lower[:, :, :], compare_op=ALU.is_gt, fill=0.0,
                                          base=0, pattern=[[1, E], [-1, E]], channel_multiplier=0))
            order.wait()
            order.step(pool.tensor_tensor(mask[:, 1:2], mask[:, 1:2], part[:, :], ALU.add))
            order.wait()
            order.step(pool.tensor_scalar(regions[:, 0:1], mask[:, 0:1], 1.0 / L, None, ALU.mult))
            order.step(pool.tensor_scalar(regions[:, 1:3], mask[:, 1:3], 1.0 / (L - L3), None, ALU.mult))
            order.wait()
            pool.sem_inc(s["consts"], 1)
            order.step(pool.tensor_copy(identb[:, :], ident[:, :]))
            for h in range(NH):
                order.step(pool.tensor_copy(ident4[:, h, :], ident[:, :]))
            order.wait()
            pool.sem_inc(s["consts"], 1)

            pool.wait_ge(s["in_in"], 16 * 7)
            for k in range(KW):
                pool.tensor_tensor(in_taps[:, k, :].rearrange("p (c d) -> p c d", d=DM), in_nat[:, JI:, :],
                                   conv_w_sb[:, :, KW - 1 - k:KW - k].broadcast_to([P, JC, DM]), ALU.mult)\
                    .then_inc(s["in_taps_ready"], 1)

            def bias_weights(g):
                pool.tensor_tensor(w_mask_T[:, :, :], w_T[:, bass.ds(g * GB, GB)].unsqueeze(2).broadcast_to([E + 1, GB, L]),
                                   mask_T[:, :].unsqueeze(1).broadcast_to([E + 1, GB, L]), ALU.mult)\
                    .then_inc(s["w_mask_T_ready"], 1)

            def residual(g):
                pool.wait_ge(s["y_added"], (g + 2) * GB)
                pool.tensor_tensor(grp(res, g), c_grp[:, :, :].rearrange("p b d -> p (b d)"), grp(x_tok, g), ALU.add)\
                    .then_inc(s["res_ready"], 1)

            pool.wait_ge(s["gate_T_ready"], 1)
            bias_weights(0)
            with pool.Fori(0, NG - 1) as g:
                pool.wait_ge(s["down_s_done"], g + 1)
                bias_weights(g + 1)
                residual(g)
            residual(NG - 1)

            pool.wait_ge(s["D_col_ready"], 1)

            def times_D(g):
                pool.wait_ge(s["xbc_ready"], g * JC + JI)
                pool.wait_ge(s["y_g_ready"], (g + 1) * JI)
                pool.tensor_tensor(xD[:, :, :], xbc[:, 0:JI, :], D_col[:, :].unsqueeze(2).broadcast_to([P, JI, GT]),
                                   ALU.mult).then_inc(s["xD_ready"], 1)

            def norm_power(g):
                pool.wait_ge(s["ms_ready"], g + 1)
                pool.tensor_tensor(y_r[:, :], y_ms[:, :], minus_half[:, :], ALU.pow).then_inc(s["yr_ready"], 1)

            def add_b2(g):
                pool.wait_ge(s["r_grp_ready"], (g + 1) * GB)
                pool.tensor_tensor(res[:, bass.ds(g * GB, GB), :], r_grp[:, :, :],
                                   b2_sb[:, :].unsqueeze(1).broadcast_to([P, GB, DM]), ALU.add)\
                    .then_inc(s["res_b2_ready"], 1)

            def quant_power(g, k):
                pool.wait_ge(s[f"ms{k + 1}"], g + 1)
                pool.tensor_tensor(rr[:, k, :], ms[:, k, :], minus_half[:, :], ALU.pow)\
                    .then_inc(s[f"rr{k + 1}"], 1)

            def pool_turn(i, ssm=True, ffn=True):
                if ffn:
                    quant_power(i - 1, 0)
                if ssm:
                    times_D(i)
                    norm_power(i)
                if ffn:
                    quant_power(i - 1, 1)
                if ssm:
                    add_b2(i)

            pool.sem_inc(s["xD_ready"], 1)
            pool.sem_inc(s["res_b2_ready"], 1)
            pool_turn(0, ffn=False)
            with pool.Fori(1, NG) as i:
                pool_turn(i)
            pool_turn(NG, ssm=False)

        @block.scalar
        def _(act):
            for dst, src in ((gate_w_sb[:, :, :], gate_w.rearrange("(j p) e -> p j e", p=P)),
                             (gate_b_sb[:, :], gate_b.partition_broadcast(B)),
                             (time_w_sb[:, :], time_w),
                             (time_b_sb[:, :], time_b.partition_broadcast(B))):
                act.dma_start(dst, src).then_inc(s["gate_in"], 16)
            for dst, src in ((in_nat[:, :, :], in_w[0:6 * P, :].rearrange("(c p) d -> p c d", p=P)),
                             (in_nat_dt[:, :], in_w[6 * P:6 * P + NH, :]),
                             (conv_w_sb[:, :, :], conv_w.rearrange("(c p) k -> p c k", p=P)),
                             (dt_bias_sb[:, :], dt_bias.partition_broadcast(P)),
                             (A_sb[:, :], A_log.partition_broadcast(P)),
                             (D_all[:, :], D.partition_broadcast(P)),
                             (out_nat[:, :], out_w)):
                act.dma_start(dst, src).then_inc(s["in_in"], 16)
            for dst, src in ((mix_sb[:, :, :], mix_w.rearrange("(k p) c -> p k c", p=P)), (proj_sb[:, :], proj_w)):
                act.dma_start(dst, src).then_inc(s["mix_in"], 16)
            for dst, src in ((w1_nat[:, :, :], f_w1.rearrange("(c p) d -> p c d", p=P)), (w2_nat[:, :], f_w2),
                             (b1_sb[:, :], f_b1.partition_broadcast(P)), (b2_sb[:, :], f_b2.partition_broadcast(P))):
                act.dma_start(dst, src).then_inc(s["ffn_in"], 16)

            for g in range(NG):
                act.wait_ge(s["x_T_psum"], g + 1)
                act.activation(x_hi[:, g * GT:(g + 1) * GT], bank[g % 2][:, :], ACT.Copy, scale=XS)\
                    .then_inc(s["x_hi_ready"], 1)
            act.wait_ge(s["cols_ready"], 1)
            act.activation(cond_silu[:, :], col(C_COND, B), ACT.Silu).then_inc(s["silu_ready"], 1)
            for e in (E, *range(E)):
                if e == E:
                    act.wait_ge(s["shared_in"], 32)
                elif e == 0:
                    act.wait_ge(s["gl_ready"], 1)
                    act.activation(prob[:, :], gl[:, :], ACT.Exp, bias=gmax[:, 0:1], accum_out=gsum[:, 0:1])\
                        .then_inc(s["prob_exp"], 1)
                    act.wait_ge(s["experts_in"], 16 * 2 * E)
                act.activation(up_hi[:, e * H:(e + 1) * H], up_nat[:, e, :], ACT.Copy, scale=WS)\
                    .then_inc(s["up_hi_ready"], 1)

            act.sem_inc(s["gelu_done"], 2)
            act.sem_inc(s["y_s_copied"], 1)

            def shared_gelu(g, c):
                act.wait_ge(s["up_s_done"], g * HC + c + 1)
                act.activation(hid_s[:, c, :], bank[c % 3][:, :], ACT.Gelu_apprx_tanh, bias=col(C_SB1 + c),
                               scale=1.0 / (XS * WS)).then_inc(s["gelu_s_done"], 1)

            def slot_gelu(g, u):
                act.wait_ge(s["pre_done"], g * U + u + 1)
                act.wait_ge(s["down_done"], g * U + u + 1)
                act.activation(hid[:, u % 4, :], pre[:, u % 2, :], ACT.Gelu_apprx_tanh).then_inc(s["gelu_done"], 1)

            def copy_shared(g, first):
                act.wait_ge(s["down_s_done"], g + 1)
                if not first:
                    act.wait_ge(s["c_T_psum"], g)
                    act.wait_ge(s["res_ready"], g)
                act.copy(c_grp[:, :, :].rearrange("p b d -> p (b d)"), bank[3][:, :]).then_inc(s["y_s_copied"], 1)

            def first_parts(g):
                act.wait_ge(s["c_T_psum"], g + 1)
                act.activation(c_hi[:, bass.ds(g * GT, GT)], bank[6][:, :], ACT.Copy, scale=CS)\
                    .then_inc(s["c_hi_ready"], 1)

            def act_group(g, more):
                for u in range(2, U):
                    slot_gelu(g, u)
                if more:
                    act.wait_ge(s["down_s_done"], g + 1)
                    for c in range(HC):
                        shared_gelu(g + 1, c)
                    slot_gelu(g + 1, 0)
                    slot_gelu(g + 1, 1)
                first_parts(g)
                if more:
                    copy_shared(g + 1, False)

            for c in range(HC):
                shared_gelu(0, c)
            slot_gelu(0, 0)
            slot_gelu(0, 1)
            copy_shared(0, True)
            with act.Fori(0, NG - 1) as g:
                act_group(g, True)
            act_group(NG - 1, False)

            act.wait_ge(s["in_in"], 16 * 7)
            for k in range(KW + 1):
                act.wait_ge(s["in_psum"], k + 1)
                at = in_part(k)
                act.activation(in_hi[:, at], bank[k % 2][:, 0:at.stop - at.start], ACT.Copy, scale=IS)\
                    .then_inc(s["in_hi_ready"], 1)
            act.wait_ge(s["u_psum"], 1)
            act.activation(u_T[:, :], bank[3][:, 0:B], ACT.Gelu, bias=col(C_PB)).then_inc(s["u_ready"], 1)
            act.wait_ge(s["ffn_in"], 64)
            act.activation(wabs[:, 0, :], w1_nat[:, :, :].rearrange("p c d -> p (c d)"), ACT.Abs,
                           accum_out=wsum[:, 0:1]).then_inc(s["abs_done"], 1)
            act.activation(wabs[:, 1, :], w2_nat[:, :], ACT.Abs, accum_out=wsum[:, 1:2]).then_inc(s["abs_done"], 1)

            act.activation(A_pos[:, :], A_sb[:, :], ACT.Exp).then_inc(s["dt_exp"], 1)
            act.wait_ge(s["dt_in"], 1)
            act.activation(dt_t[1][:, :], dt_t[0][:, :], ACT.Exp, scale=-1.0).then_inc(s["dt_exp"], 1)
            act.wait_ge(s["dt_w"], 1)
            act.activation(dt_t[3][:, :], dt_t[2][:, :], ACT.Ln).then_inc(s["dt_ln"], 1)
            act.wait_ge(s["dt_mul"], 1)
            act.activation(dA_all[:, :, :].rearrange("p b h -> p (b h)"), dt_t[0][:, :], ACT.Exp, scale=-1.0)\
                .then_inc(s["dt_exp"], 1)

            def silu_x(g, j):
                act.wait_ge(s["xbc_psum"], g * JC + j + 1)
                if j < JI:
                    act.wait_ge(s["xs_T_psum"], (g + 1) * 2)
                    act.wait_ge(s["xD_ready"], g + 1)
                else:
                    act.wait_ge(s["g_psum"], g + 1)
                act.activation(xbc[:, j, :], bank[j % 2][:, :], ACT.Silu, bias=col(C_CB + j),
                               scale=1.0 / (CS * IS)).then_inc(s["xbc_ready"], 1)

            def silu_z(g, j):
                act.wait_ge(s["z_psum"], g * JI + j + 1)
                act.wait_ge(s["y_g_ready"], (g + 1) * JI)
                act.activation(z_act[:, j, :], bank[j][:, :], ACT.Silu, scale=1.0 / (CS * IS)).then_inc(s["z_ready"], 1)

            def squares(g):
                for j in range(JI):
                    act.wait_ge(s["y_g_ready"], (g + 1) * JI + j + 1)
                    act.activation(y_sq[:, j, :], y_g[:, j, :], ACT.Square).then_inc(s["y_sq_ready"], 1)

            def copy_r_T(g):
                act.wait_ge(s["rT_psum"], g + 1)
                act.copy(r_T[:, :], bank[2][:, :]).then_inc(s["rT_ready"], 1)

            def squares_1(g):
                act.wait_ge(s["e_ready"], g + 2)
                for b in range(GB):
                    act.activation(sq_scr[:, b, 0:DM], e_all[:, bass.ds(g * GB + b, 1), :].rearrange("p b d -> p (b d)"),
                                   ACT.Square, accum_out=ssq[:, 0, b:b + 1]).then_inc(s["ssq1"], 1)

            def copy_q1_T(g):
                act.wait_ge(s["q1T_psum"], g + 1)
                act.copy(q1_T[:, :], bank[7][:, 0:GT // 2].bitcast(bf16)).then_inc(s["q1T_ready"], 1)

            def gelu(g, b):
                act.wait_ge(s["h_pre_ready"], g * GB + b + 1)
                act.activation(h_act[:, b, :], h_pre[:, b, :], ACT.Gelu).then_inc(s["h_act_ready"], 1)

            def squares_2(g, b):
                act.wait_ge(s["h_act_ready"], g * GB + b + 1)
                act.activation(sq_scr[:, b, :], h_act[:, b, :], ACT.Square,
                               accum_out=ssq[:, 1, b:b + 1]).then_inc(s["ssq2"], 1)

            def copy_q2_T(g, b):
                act.wait_ge(s["q2T_psum"], g * GB + b + 1)
                act.copy(q2_T[:, b, :], bank[5 + b % 2][:, 0:F // 2].bitcast(bf16)).then_inc(s["q2T_ready"], 1)

            def act_turn(i, proj=True, ssm=True, ffn=True):
                if ffn:
                    squares_1(i - 1)
                if proj:
                    silu_x(i + 1, 0)
                if ffn:
                    copy_q1_T(i - 1)
                if proj:
                    silu_x(i + 1, 1)
                if ffn:
                    gelu(i - 1, 0)
                    gelu(i - 1, 1)
                if ssm:
                    squares(i)
                if ffn:
                    gelu(i - 1, 2)
                    gelu(i - 1, 3)
                    for b in range(GB):
                        squares_2(i - 1, b)
                if proj:
                    silu_x(i + 1, 2)
                    silu_x(i + 1, 3)
                    for j in range(JI):
                        silu_z(i + 1, j)
                if ffn:
                    copy_q2_T(i - 1, 0)
                    copy_q2_T(i - 1, 1)
                if ssm:
                    copy_r_T(i)
                if ffn:
                    copy_q2_T(i - 1, 2)
                    copy_q2_T(i - 1, 3)

            act.sem_inc(s["z_ready"], JI)
            act_turn(-1, ssm=False, ffn=False)
            act_turn(0, ffn=False)
            with act.Fori(1, NG - 1) as i:
                act_turn(i)
            act_turn(NG - 1, proj=False)
            act_turn(NG, proj=False, ssm=False)

        @block.vector
        def _(dve):
            order = Order(dve, s["v_order"])
            v, link = nc.vector, order.link

            for g in range(NG):
                dve.wait_ge(s["x_hi_ready"], g + 1)
                at = slice(g * GT, (g + 1) * GT)
                v.scalar_tensor_tensor(out=x_lo[:, at], in0=bank[g % 2][:, :], scalar=XS, in1=x_hi[:, at],
                                       op0=ALU.mult, op1=ALU.subtract).then_inc(s["x_lo_ready"], 1)
            dve.wait_ge(s["cols_psum"], 1)
            v.tensor_copy(cols[:, :], bank[6][:, 0:C_END]).then_inc(s["cols_ready"], 1)
            dve.wait_ge(s["agg_psum"], 1)
            v.tensor_copy(agg[:, :, :].rearrange("p b r -> p (b r)"), bank[5][:, 0:3 * B]).then_inc(s["agg_ready"], 1)
            dve.wait_ge(s["gate_in"], 64)
            dve.wait_ge(s["gate_psum"], 1)
            order.step(v.tensor_tensor(mod[:, :], bank[7][0:B, 16:16 + 2 * E], time_b_sb[:, :], ALU.add))
            link(v.tensor_tensor(gl[:, :], bank[7][0:B, 32:32 + E], gate_b_sb[:, :], ALU.add))
            link(v.scalar_tensor_tensor(out=gl[:, :], in0=mod[:, 0:E], scalar=1.0, in1=gl[:, :],
                                        op0=ALU.add, op1=ALU.mult))
            link(v.tensor_tensor(gl[:, :], gl[:, :], mod[:, E:2 * E], ALU.add))
            v.tensor_reduce(gmax[:, :], gl[:, :], AX.X, ALU.max, negate=True).then_inc(s["gl_ready"], 1)
            dve.wait_ge(s["prob_exp"], 1)
            link(v.reciprocal(gsum[:, :], gsum[:, :]))
            link(v.tensor_scalar(prob[:, :], prob[:, :], gsum[:, 0:1], None, ALU.mult))
            mine = prob[:, :].unsqueeze(2).broadcast_to([B, E, E])
            other = prob[:, :].unsqueeze(1).broadcast_to([B, E, E])
            dve.wait_ge(s["consts"], 2)
            order.step(v.tensor_tensor(gt[:, :, :], other, mine, ALU.is_gt))
            link(v.tensor_tensor(eq[:, :, :], other, mine, ALU.is_equal))
            link(v.tensor_tensor(eq[:, :, :], eq[:, :, :], lower[:, :, :], ALU.mult))
            link(v.tensor_tensor(gt[:, :, :], gt[:, :, :], eq[:, :, :], ALU.add))
            link(v.tensor_reduce(rank[:, :], gt[:, :, :], AX.X, ALU.add))
            link(v.scalar_tensor_tensor(out=w_all[:, 0:E], in0=rank[:, :], scalar=float(K), in1=prob[:, :],
                                        op0=ALU.is_lt, op1=ALU.mult))
            link(v.tensor_reduce(gsum[:, :], w_all[:, 0:E], AX.X, ALU.add))
            link(v.tensor_scalar(gsum[:, :], gsum[:, :], 1e-8, None, ALU.add))
            link(v.reciprocal(gsum[:, :], gsum[:, :]))
            order.step(v.tensor_scalar(w_all[:, 0:E], w_all[:, 0:E], gsum[:, 0:1], None, ALU.mult))
            for k in range(K):
                order.step(v.tensor_scalar(pick[:, k, :], rank[:, :], float(k), None, ALU.is_equal))
            order.wait()
            order.step(v.tensor_tensor(sent[:, 0:K * E].rearrange("b (k e) -> b k e", e=E), pick[:, :, :],
                                       w_all[:, 0:E].unsqueeze(1).broadcast_to([B, K, E]), ALU.mult))
            link(v.tensor_tensor(picked[:, :, :], pick[:, :, :], number[:, :, :], ALU.mult))
            link(v.tensor_reduce(sent[:, K * E:], picked[:, :, :], AX.X, ALU.add))
            link(v.tensor_scalar(sent[:, K * E:], sent[:, K * E:], float(E - 1), float(H), ALU.min, ALU.mult))
            v.tensor_tensor(spread[:, :, :], sent[:, :].unsqueeze(1).broadcast_to([B, B, K * E + K]),
                            ident[0:B, 0:B].unsqueeze(2).broadcast_to([B, B, K * E + K]), ALU.mult)\
                .then_inc(s["spread_ready"], 1)
            dve.wait_ge(s["sent_psum"], 1)
            got = bank[4][:, 0:B * (K * E + K)].rearrange("p (b n) -> p b n", n=K * E + K)
            order.step(v.tensor_copy(offset[:, :].rearrange("p (b k) -> p b k", k=K), got[0:1, :, K * E:]))
            for k in range(K):
                ins = v.tensor_tensor(w_tok[:, :, :].rearrange("p (b k) e -> p b k e", k=K)[:, :, k, :],
                                      got[:, :, k * E:(k + 1) * E],
                                      mask[:, 0:E].unsqueeze(1).broadcast_to([P, B, E]), ALU.mult)
                order.step(ins)
            order.wait()
            dve.sem_inc(s["sent_ready"], 1)
            v.tensor_reduce(w_slot[:, :, :].rearrange("p b k -> p (b k)"), w_tok[:, :, :], AX.X, ALU.add)\
                .then_inc(s["w_slot_ready"], 1)
            dve.wait_ge(s["gate_T_psum"], 1)
            order.step(v.tensor_copy(pick_T[:, :, :].rearrange("e k b -> e (k b)"), bank[6][0:E, 0:K * B]))
            order.step(v.tensor_copy(w_T[:, :], bank[6][0:E + 1, 64:64 + B]))
            order.step(v.tensor_copy(mask_T[:, :], bank[6][0:E + 1, 128:256]))
            order.wait()
            dve.sem_inc(s["gate_T_ready"], 1)
            for n, e in enumerate((E, *range(E))):
                dve.wait_ge(s["up_hi_ready"], n + 1)
                v.scalar_tensor_tensor(out=up_lo[:, e * H:(e + 1) * H], in0=up_nat[:, e, :], scalar=WS,
                                       in1=up_hi[:, e * H:(e + 1) * H], op0=ALU.mult, op1=ALU.subtract)\
                    .then_inc(s["up_lo_ready"], 1)
            dve.wait_ge(s["slot_bias_psum"], 1)
            link(v.tensor_copy(slot_bias[:, :, :, :].rearrange("p b k c -> p c k b"),
                               bank[7][:, 0:HC * K * B].rearrange("p (c k b) -> p c k b", k=K, b=B)))

            dve.sem_inc(s["c_lo_ready"], 1)
            dve.sem_inc(s["y_added"], GB)

            def slot_pre(g, u):
                dve.wait_ge(s["up_done"], g * U + u + 1)
                dve.wait_ge(s["gelu_done"], g * U + u + 1)
                bias = slot_bias[:, :, :, :].rearrange("p b k c -> p (b k) c")[:, bass.ds(g * U + u, 1), :]
                v.scalar_tensor_tensor(out=pre[:, u % 2, :].rearrange("p (c t) -> p c t", t=L),
                                       in0=bank[(u + 1) % 3][:, :].rearrange("p (c t) -> p c t", t=L),
                                       scalar=1.0 / (XS * WS),
                                       in1=bias.rearrange("p o c -> p (o c)").unsqueeze(2).broadcast_to([P, HC, L]),
                                       op0=ALU.mult, op1=ALU.add).then_inc(s["pre_done"], 1)

            def add_slots(g):
                dve.wait_ge(s["y_s_copied"], g + 2)
                dve.wait_ge(s["down_done"], 4 + (g + 1) * U)
                marks = []
                for k in range(K):
                    for b in range(GB):
                        if k:
                            dve.wait_ge(s["v_order"], v0 + g * GB + b + 1)
                        w = w_slot[:, bass.ds(g * GB + b, 1), k]
                        ins = v.scalar_tensor_tensor(out=c_grp[:, b, :], in0=bank[4 + k][:, b * DM:(b + 1) * DM],
                                                     scalar=w, in1=c_grp[:, b, :], op0=ALU.mult, op1=ALU.add)
                        ins.then_inc(s["y_added"] if k else s["v_order"], 1)

            def second_parts(g):
                dve.wait_ge(s["c_hi_ready"], g + 1)
                v.scalar_tensor_tensor(out=c_lo[:, bass.ds(g * GT, GT)], in0=bank[6][:, :], scalar=CS,
                                       in1=c_hi[:, bass.ds(g * GT, GT)], op0=ALU.mult, op1=ALU.subtract)\
                    .then_inc(s["c_lo_ready"], 1)

            def vector_group(g, more):
                for u in range(2, U):
                    slot_pre(g, u)
                if more:
                    slot_pre(g + 1, 0)
                    slot_pre(g + 1, 1)
                add_slots(g)
                second_parts(g)

            v0 = order.count
            slot_pre(0, 0)
            slot_pre(0, 1)
            with dve.Fori(0, NG - 1) as g:
                vector_group(g, True)
            vector_group(NG - 1, False)
            order.count += NG * GB

            for k in range(KW + 1):
                dve.wait_ge(s["in_hi_ready"], k + 1)
                at = in_part(k)
                v.scalar_tensor_tensor(out=in_lo[:, at], in0=bank[k % 2][:, 0:at.stop - at.start], scalar=IS,
                                       in1=in_hi[:, at], op0=ALU.mult, op1=ALU.subtract).then_inc(s["in_ready"], 1)

            dve.wait_ge(s["dt_psum"], 1)
            link(v.scalar_tensor_tensor(out=dt_raw[:, :, :], in0=bank[7][:, 0:B * NH].rearrange("p (b h) -> p b h", h=NH),
                                        scalar=1.0 / (CS * IS),
                                        in1=dt_bias_sb[:, :].unsqueeze(1).broadcast_to([P, B, NH]),
                                        op0=ALU.mult, op1=ALU.add))

            raw = dt_raw[:, :, :].rearrange("p b h -> p (b h)")
            dts = dt_all[:, :, :].rearrange("p b h -> p (b h)")
            link(v.tensor_scalar(dts, raw, 0.0, None, ALU.max))
            v.scalar_tensor_tensor(out=dt_t[0][:, :], in0=dts, scalar=2.0, in1=raw,
                                   op0=ALU.mult, op1=ALU.subtract).then_inc(s["dt_in"], 1)
            dve.wait_ge(s["dt_exp"], 2)
            v.tensor_scalar(dt_t[2][:, :], dt_t[1][:, :], 1.0, None, ALU.add).then_inc(s["dt_w"], 1)
            dve.wait_ge(s["dt_w"], 1)
            link(v.scalar_tensor_tensor(out=dt_t[1][:, :], in0=dt_t[2][:, :], scalar=1.0, in1=dt_t[1][:, :],
                                        op0=ALU.subtract, op1=ALU.subtract))
            dve.wait_ge(s["dt_ln"], 1)
            link(v.tensor_tensor(dt_t[3][:, :], dt_t[3][:, :], dt_t[1][:, :], ALU.subtract))
            link(v.tensor_tensor(dts, dts, dt_t[3][:, :], ALU.add))
            v.tensor_tensor(dt_t[0][:, :].rearrange("p (b h) -> p b h", h=NH), dt_all[:, :, :],
                            A_pos[:, :].unsqueeze(1).broadcast_to([P, B, NH]), ALU.mult).then_inc(s["dt_mul"], 1)

            dve.wait_ge(s["out_psum"], 1)
            for j in range(JI):
                v.tensor_scalar(out_T[:, j, :], bank[2][:, j * P:(j + 1) * P], col(C_NW + j), None, ALU.mult)\
                    .then_inc(s["out_ready"], 1)
            for h in range(NH):
                lo = h % 2 * HD
                order.step(v.tensor_copy(D_col[lo:lo + HD, h // 2:h // 2 + 1], D_all[lo:lo + HD, h:h + 1]))
            order.wait()
            dve.sem_inc(s["D_col_ready"], 1)
            dve.wait_ge(s["uw_psum"], 1)
            v.tensor_copy(uw[:, :], bank[4][0:B, 0:P]).then_inc(s["uw_ready"], 1)
            for g in range(NG):
                dve.wait_ge(s["eb_psum"], g + 1)
                v.tensor_copy(e_bias[:, g * GB:(g + 1) * GB, :].rearrange("p b c -> p (b c)"), bank[g][:, :])\
                    .then_inc(s["eb_ready"], 1)
            dve.wait_ge(s["sum_psum"], 1)
            link(v.tensor_scalar(wmean[:, :], bank[5][:, 0:2], 1.0 / (F * DM), 1e-5, ALU.mult, ALU.max))
            link(v.reciprocal(wscale[:, :], wmean[:, :]))
            for k, (nat, q) in enumerate(((w1_nat[:, :, :].rearrange("p c d -> p (c d)"),
                                           w1_q[:, :, :].rearrange("p c d -> p (c d)")),
                                          (w2_nat[:, :], w2_q[:, :]))):
                link(v.tensor_scalar(wtmp[:, k, :], nat, wscale[:, k:k + 1], MAGIC, ALU.mult, ALU.add))
                link(v.tensor_scalar(wtmp[:, k, :], wtmp[:, k, :], MAGIC, 1.0, ALU.subtract, ALU.min))
                v.tensor_scalar(q, wtmp[:, k, :], -1.0, None, ALU.max).then_inc(s["w_q_ready"], 1)
            for k, dst in enumerate((w1_qT[:, :], w2_qT[:, :, :].rearrange("p c d -> p (c d)"))):
                dve.wait_ge(s["w_qT_psum"], k + 1)
                v.tensor_copy(dst, bank[6 - k][:, 0:256].bitcast(bf16)).then_inc(s["w_qT_ready"], 1)
            dve.wait_ge(s["dt_exp"], 3)
            link(v.memset(dA_all[0:1, :, :], 0.0))
            rest = dA_all[:, :, :].rearrange("p b h -> p (b h)")
            for k in range(3):
                link(v.tensor_copy(dA_parts[:, k, :], rest))
                if k < 2:
                    link(v.tensor_tensor(dA_rest[:, k, :], rest, dA_parts[:, k, :], ALU.subtract))
                    rest = dA_rest[:, k, :]
            dve.wait_ge(s["eb_ready"], NG)

            own_b = Stage(dve, s["v_b"], JI)
            own_c = Stage(dve, s["v_c"], 1 + 5 + GB + GB + 5 + GB)
            dve.sem_inc(s["e_ready"], 1)
            dve.sem_inc(s["y_g_ready"], JI)
            dve.sem_inc(s["y_out_ready"], 1)

            def group_decays(g):
                dve.wait_ge(s["bc_psum"], g * GB + GB)
                v.tensor_copy(dA_grp[:, :, :], dA_parts[:, :, bass.ds(g * GB * NH, GB * NH)])\
                    .then_inc(s["dA_grp_ready"], 1)

            def x_times_dt(g):
                for m in range(2):
                    dve.wait_ge(s["xs_T_psum"], g * 2 + 2 + m + 1)
                    dtb = dt_all[:, bass.ds(g * GB + 2 * m, 2), :].rearrange("p b h -> p (b h)")
                    v.tensor_tensor(x_dt[:, 2 * m:2 * m + 2, :].rearrange("p b (h q) -> p (b h) q", q=HD),
                                    bank[2 + m][:, :].rearrange("p (m q) -> p m q", q=HD),
                                    dtb.unsqueeze(2).broadcast_to([P, 2 * NH, HD]),
                                    ALU.mult).then_inc(s["x_dt_ready"], 1)

            def scan(g, b):
                dve.wait_ge(s["bc_psum"], g * GB + GB + b + 1)
                if b >= 2:
                    dve.wait_ge(s["mix_ready"], g * GB + b - 1)
                v.tensor_tensor_scan(out=decay[:, b % 2, :], data0=bank[5 + b % 2][:, :],
                                     data1=ident4[:, :, :].rearrange("p h t -> p (h t)"), initial=0.0,
                                     op0=ALU.mult, op1=ALU.add).then_inc(s["scan_done"], 1)

            def mix(g, b):
                dve.wait_ge(s["scan_done"], g * GB + b + 1)
                if b == 0:
                    dve.wait_ge(s["g_psum"], g + 2)
                if b >= 2:
                    dve.wait_ge(s["y_psum"], g * GB + b - 1)
                v.tensor_tensor(mixer[:, b % 2, :].rearrange("p (h t) -> p h t", t=L),
                                decay[:, b % 2, :].rearrange("p (h t) -> p h t", t=L),
                                bank[4][:, b * L:(b + 1) * L].unsqueeze(1).broadcast_to([P, NH, L]),
                                ALU.mult).then_inc(s["mix_ready"], 1)

            def gate_y(g):
                own_b.group(g)
                dve.wait_ge(s["z_ready"], (g + 2) * JI)
                dve.wait_ge(s["xD_ready"], g + 2)
                dve.wait_ge(s["y_psum"], (g + 1) * GB)
                for j in range(JI):
                    own_b.step(v.tensor_tensor(y_g[:, j, :], bank[2 + j][:, :], xD[:, j, :], ALU.add))
                for j in range(JI):
                    own_b.wait(j + 1)
                    v.tensor_tensor(y_g[:, j, :], y_g[:, j, :], z_act[:, j, :], ALU.mult)\
                        .then_inc(s["y_g_ready"], 1)

            def mean_square(g):
                dve.wait_ge(s["ss_psum"], g + 1)
                v.tensor_scalar(y_ms[:, :], bank[7][:, 0:GB], 1.0 / DI, EPS, ALU.mult, ALU.add)\
                    .then_inc(s["ms_ready"], 1)

            def add_residual(g):
                dve.wait_ge(s["yr_ready"], g + 1)
                dve.wait_ge(s["res_b2_ready"], g + 1)
                for b in range(GB):
                    v.scalar_tensor_tensor(out=r_grp[:, b, :], in0=bank[4][:, b * DM:(b + 1) * DM],
                                           scalar=y_r[:, b:b + 1],
                                           in1=res[:, bass.ds(g * GB + b, 1), :].rearrange("p b d -> p (b d)"),
                                           op0=ALU.mult, op1=ALU.add).then_inc(s["r_grp_ready"], 1)

            def mixed(g):
                dve.wait_ge(s["e_psum"], g + 1)
                v.tensor_tensor(grp(e_all, g), bank[3][:, :], grp(e_bias, g), ALU.add).then_inc(s["e_ready"], 1)

            def largest_1(g):
                own_c.group(g)
                dve.wait_ge(s["e_ready"], g + 2)
                own_c.step(v.tensor_reduce(amax[:, 0, :], e_all[:, bass.ds(g * GB, GB), :], AX.X, ALU.max,
                                           apply_absolute_value=True))

            def mean_squares(g, k):
                dve.wait_ge(s[f"ssq{k + 1}"], (g + 1) * GB)
                v.tensor_scalar(ms[:, k, :], ssq[:, k, :], 1.0 / (DM, F)[k], EPS, ALU.mult, ALU.add)\
                    .then_inc(s[f"ms{k + 1}"], 1)

            def scales(g, k):
                if k == 0:
                    dve.wait_ge(s["y_out_ready"], g + 1)
                dve.wait_ge(s[f"rr{k + 1}"], g + 1)
                link = own_c.link
                link(v.tensor_tensor(cl[:, k, :], amax[:, k, :], rr[:, k, :], ALU.mult))
                link(v.tensor_scalar(cl[:, k, :], cl[:, k, :], 1e-5, None, ALU.max))
                own_c.step(v.tensor_scalar(qk[:, k, :], cl[:, k, :], 1.0 / 127.0, wmean[:, k:k + 1], ALU.mult, ALU.mult))
                link(v.reciprocal(inv[:, k, :], cl[:, k, :]))
                link(v.scalar_tensor_tensor(out=qm[:, k, :], in0=inv[:, k, :], scalar=127.0, in1=rr[:, k, :],
                                            op0=ALU.mult, op1=ALU.mult))

            def round_1(g):
                for b in range(GB):
                    own_c.step(v.tensor_scalar(q1_f[:, b * DM:(b + 1) * DM],
                                               e_all[:, bass.ds(g * GB + b, 1), :].rearrange("p b d -> p (b d)"),
                                               qm[:, 0, b:b + 1], MAGIC, ALU.mult, ALU.add))
                own_c.wait()
                v.tensor_scalar(q1[:, :], q1_f[:, :], MAGIC, None, ALU.subtract).then_inc(s["q1_ready"], 1)

            def scale_h(g, b):
                dve.wait_ge(s["h_psum"], g * GB + b + 1)
                v.scalar_tensor_tensor(out=h_pre[:, b, :], in0=bank[5 + b % 2][:, :], scalar=qk[:, 0, b:b + 1],
                                       in1=b1_sb[:, :], op0=ALU.mult, op1=ALU.add).then_inc(s["h_pre_ready"], 1)

            def largest_2(g, b):
                dve.wait_ge(s["h_act_ready"], g * GB + b + 1)
                own_c.step(v.tensor_reduce(amax[:, 1, b:b + 1], h_act[:, b, :], AX.X, ALU.max,
                                           apply_absolute_value=True))

            def round_2(g):
                marks = []
                for b in range(GB):
                    marks.append(own_c.step(v.tensor_scalar(q2_f[:, b, :], h_act[:, b, :], qm[:, 1, b:b + 1], MAGIC,
                                                            ALU.mult, ALU.add)))
                    if b:
                        own_c.wait(marks[b - 1])
                        v.tensor_scalar(q2[:, b - 1, :], q2_f[:, b - 1, :], MAGIC, None, ALU.subtract)\
                            .then_inc(s["q2_ready"], 1)
                own_c.wait()
                v.tensor_scalar(q2[:, GB - 1, :], q2_f[:, GB - 1, :], MAGIC, None, ALU.subtract)\
                    .then_inc(s["q2_ready"], 1)

            def output(g):
                dve.wait_ge(s["o_psum"], g + 1)
                dve.wait_ge(s["out_sent"], g * 16 + 16)
                dve.wait_ge(s["res_b2_ready"], g + 2)
                for b in range(GB):
                    ins = v.scalar_tensor_tensor(out=y_out[:, b, :], in0=bank[7][:, b * DM:(b + 1) * DM],
                                                 scalar=qk[:, 1, b:b + 1],
                                                 in1=res[:, bass.ds(g * GB + b, 1), :].rearrange("p b d -> p (b d)"),
                                                 op0=ALU.mult, op1=ALU.add)
                ins.then_inc(s["y_out_ready"], 1)

            def vector_turn(i, ssm=True, ffn=True):
                if ffn:
                    largest_1(i - 1)
                    mean_squares(i - 1, 0)
                if ssm:
                    group_decays(i)
                    x_times_dt(i)
                    scan(i, 0)
                    mix(i, 0)
                if ffn:
                    scales(i - 1, 0)
                    round_1(i - 1)
                if ssm:
                    for b in range(1, GB):
                        scan(i, b)
                        mix(i, b)
                if ffn:
                    scale_h(i - 1, 0)
                    scale_h(i - 1, 1)
                if ssm:
                    gate_y(i)
                if ffn:
                    scale_h(i - 1, 2)
                    scale_h(i - 1, 3)
                    for b in range(GB):
                        largest_2(i - 1, b)
                if ssm:
                    mean_square(i)
                if ffn:
                    mean_squares(i - 1, 1)
                if ssm:
                    add_residual(i)
                if ffn:
                    scales(i - 1, 1)
                    round_2(i - 1)
                if ssm:
                    mixed(i)
                if ffn:
                    output(i - 1)

            vector_turn(0, ffn=False)
            with dve.Fori(1, NG) as i:
                vector_turn(i)
            vector_turn(NG, ssm=False)

        @block.tensor
        def _(pe):
            mm, tr = pe.matmul, pe.transpose

            pe.wait_ge(s["consts"], 1)
            pe.wait_ge(s["x_in"], 16 * NG)
            for g in range(NG):
                if g >= 2:
                    pe.wait_ge(s["x_lo_ready"], g - 1)
                for b in range(GB):
                    ins = tr(bank[g % 2][:, b * L:(b + 1) * L], x_tok[:, g * GB + b, :], ident[:, :])
                ins.then_inc(s["x_T_psum"], 1)
            for b in range(B):
                ins = mm(bank[5][:, 3 * b:3 * b + 3], x_tok[:, b, :], regions[:, :], start=True, stop=True)
            ins.then_inc(s["agg_psum"], 1)
            pe.wait_ge(s["rows_in"], 16 * ROWS)
            tr(bank[6][:, 0:C_END], rows[:, :], ident[0:C_END, 0:C_END]).then_inc(s["cols_psum"], 1)
            pe.wait_ge(s["silu_ready"], 1)
            pe.wait_ge(s["gate_in"], 64)
            mm(bank[7][0:B, 16:16 + 2 * E], cond_silu[:, :], time_w_sb[:, :], start=True, stop=True)
            pe.wait_ge(s["agg_ready"], 1)
            for j in range(3):
                ins = mm(bank[7][0:B, 32:32 + E], agg[:, :, j], gate_w_sb[:, j, :], start=(j == 0), stop=(j == 2))
            ins.then_inc(s["gate_psum"], 1)

            def three(dst, w_hi, w_lo, m_hi, m_lo):
                mm(dst, w_hi, m_hi, start=True, stop=False)
                mm(dst, w_hi, m_lo, start=False, stop=False)
                return mm(dst, w_lo, m_hi, start=False, stop=True)

            def shared_up(g, c, first=False):
                if c == 3:
                    pe.wait_ge(s["gelu_s_done"], g * HC + 1)
                elif not first:
                    pe.wait_ge(s["pre_done"], g * U - 2 + c)
                w = slice(E * H + c * P, E * H + (c + 1) * P)
                at = bass.ds(g * GT, GT)
                three(bank[c % 3][:, :], up_hi[:, w], up_lo[:, w], x_hi[:, at], x_lo[:, at])\
                    .then_inc(s["up_s_done"], 1)

            def shared_down(g):
                pe.wait_ge(s["y_s_copied"], g + 1)
                pe.wait_ge(s["gelu_s_done"], (g + 1) * HC)
                pe.wait_ge(s["w_mask_T_ready"], g + 1)
                for b in range(GB):
                    dst = bank[3][:, b * DM:(b + 1) * DM]
                    mm(dst, w_mask_T[:, b, :], b2_rows[:, :], start=True, stop=False)
                    for c in range(HC):
                        ins = mm(dst, hid_s[:, c, b * L:(b + 1) * L], down[:, E * H + c * DM:E * H + (c + 1) * DM],
                                 start=False, stop=(c == HC - 1))
                ins.then_inc(s["down_s_done"], 1)

            def slot_up(g, u, e_at):
                if u < 3:
                    pe.wait_ge(s["gelu_s_done"], g * HC + u + 2)
                else:
                    pe.wait_ge(s["pre_done"], g * U + u - 2)
                at = bass.ds(g * GT + u // K * L, L)
                for c in range(HC):
                    w = bass.ds(e_at + c * P, P)
                    ins = three(bank[(u + 1) % 3][:, c * L:(c + 1) * L], up_hi[:, w], up_lo[:, w],
                                x_hi[:, at], x_lo[:, at])
                ins.then_inc(s["up_done"], 1)

            def slot_down(g, u, e_at):
                if u < K:
                    pe.wait_ge(s["y_added"], (g + 1) * GB)
                pe.wait_ge(s["gelu_done"], 2 + g * U + u + 1)
                b, k = divmod(u, K)
                for c in range(HC):
                    ins = mm(bank[4 + k][:, b * DM:(b + 1) * DM], hid[:, u % 4, c * L:(c + 1) * L],
                             down[:, bass.ds(e_at + c * DM, DM)], start=(c == 0), stop=(c == HC - 1))
                ins.then_inc(s["down_done"], 1)

            def transpose_c(g):
                pe.wait_ge(s["y_added"], (g + 2) * GB)
                pe.wait_ge(s["c_lo_ready"], g + 1)
                for b in range(GB):
                    ins = tr(bank[6][:, b * L:(b + 1) * L], c_grp[:, b, :], ident[:, :])
                ins.then_inc(s["c_T_psum"], 1)

            def slot_experts(first, n):
                _, values = nc.values_load_multi_w_load_instructions(
                    offset[0:1, bass.ds(first, n)], engines=(mybir.EngineType.PE,), min_val=0, max_val=(E - 1) * H,
                    skip_runtime_bounds_check_because="the gate keeps the offsets within the weights")
                return values

            pe.wait_ge(s["spread_ready"], 1)
            mm(bank[4][:, 0:B * (K * E + K)], ones[0:B, :], spread[:, :, :].rearrange("k b e -> k (b e)"),
               start=True, stop=True).then_inc(s["sent_psum"], 1)
            pe.wait_ge(s["cols_ready"], 1)
            for k in range(K):
                tr(bank[6][0:E, k * B:(k + 1) * B], pick[:, k, :], ident[0:B, 0:B])
            tr(bank[6][0:E + 1, 64:64 + B], w_all[:, :], ident[0:B, 0:B])
            tr(bank[6][0:E + 1, 128:256], mask[:, :], ident[:, :]).then_inc(s["gate_T_psum"], 1)
            pe.wait_ge(s["gate_T_ready"], 1)
            for c in range(HC):
                ins = mm(bank[7][:, c * K * B:(c + 1) * K * B], eb1_rows[:, c * P:(c + 1) * P],
                         pick_T[:, :, :].rearrange("e k b -> e (k b)"), start=True, stop=True)
            ins.then_inc(s["slot_bias_psum"], 1)

            pe.sem_inc(s["down_done"], 4)
            pe.wait_ge(s["x_lo_ready"], NG)
            pe.wait_ge(s["up_lo_ready"], 1)
            for c in range(HC):
                shared_up(0, c, True)
            pe.wait_ge(s["sent_ready"], 1)
            pe.wait_ge(s["up_lo_ready"], E + 1)
            e_at = slot_experts(0, K)
            slot_up(0, 0, e_at[0])
            slot_up(0, 1, e_at[1])
            shared_down(0)

            def tensor_group(g, more):
                e_at = slot_experts(g * U, U)
                for u in range(2, U):
                    slot_up(g, u, e_at[u])
                    slot_down(g, u - 2, e_at[u - 2])
                if more:
                    shared_up(g + 1, 0)
                slot_down(g, U - 2, e_at[U - 2])
                if more:
                    shared_up(g + 1, 1)
                slot_down(g, U - 1, e_at[U - 1])
                if more:
                    shared_up(g + 1, 2)
                    shared_up(g + 1, 3)
                    e_next = slot_experts((g + 1) * U, K)
                    slot_up(g + 1, 0, e_next[0])
                    slot_up(g + 1, 1, e_next[1])
                transpose_c(g)
                if more:
                    shared_down(g + 1)

            with pe.Fori(0, NG - 1) as g:
                tensor_group(g, True)
            tensor_group(NG - 1, False)

            pe.wait_ge(s["in_in"], 16 * 7)
            for j in range(JI):
                tr(bank[0][:, j * P:(j + 1) * P], in_nat[:, j, :], ident[:, :])
            tr(bank[0][:, DI:DI + NH], in_nat_dt[:, :], ident[0:NH, 0:NH]).then_inc(s["in_psum"], 1)
            pe.wait_ge(s["in_taps_ready"], KW)
            for k in range(1, KW + 1):
                if k >= 2:
                    pe.wait_ge(s["in_ready"], k - 1)
                for c in range(JC):
                    ins = tr(bank[k % 2][:, c * P:(c + 1) * P], in_taps[:, k - 1, c * P:(c + 1) * P], ident[:, :])
                ins.then_inc(s["in_psum"], 1)
            for j in range(JI):
                ins = tr(bank[2][:, j * P:(j + 1) * P], out_nat[:, j * P:(j + 1) * P], ident[:, :])
            ins.then_inc(s["out_psum"], 1)
            pe.wait_ge(s["mix_in"], 32)
            mm(bank[3][:, 0:B], proj_sb[:, :], col(C_COND, B), start=True, stop=True).then_inc(s["u_psum"], 1)
            pe.wait_ge(s["u_ready"], 1)
            pe.wait_ge(s["in_ready"], KW + 1)
            pe.wait_ge(s["c_lo_ready"], NG + 1)
            for b in range(B):
                at = slice(b * L, (b + 1) * L)
                w = slice(DI, DI + NH)
                ins = three(bank[7][:, b * NH:(b + 1) * NH], c_hi[:, at], c_lo[:, at], in_hi[:, w], in_lo[:, w])
            ins.then_inc(s["dt_psum"], 1)
            mm(bank[4][0:B, 0:P], u_T[:, :], mix_sb[:, 0, :], start=True, stop=True).then_inc(s["uw_psum"], 1)
            pe.wait_ge(s["abs_done"], 2)
            mm(bank[5][:, 0:2], ones[:, :], wsum[:, :], start=True, stop=True).then_inc(s["sum_psum"], 1)
            pe.wait_ge(s["uw_ready"], 1)
            for g in range(NG):
                if g == 2:
                    pe.wait_ge(s["out_ready"], JI)
                for b in range(GB):
                    bb = g * GB + b
                    ins = mm(bank[g][:, b * P:(b + 1) * P], ident[0:B, bb:bb + 1].broadcast_to([B, P]), uw[:, :],
                             start=True, stop=True)
                ins.then_inc(s["eb_psum"], 1)
            for k, (q, bk) in enumerate(((w1_q, 6), (w2_q, 5))):
                pe.wait_ge(s["w_q_ready"], k + 1)
                for c in range(FC):
                    src = q[:, c, :] if k == 0 else q[:, c * P:(c + 1) * P]
                    ins = tr(bank[bk][:, c * P // 2:(c + 1) * P // 2].bitcast(bf16), src, identb[:, :])
                ins.then_inc(s["w_qT_psum"], 1)
            pe.wait_ge(s["w_qT_ready"], 2)
            pe.wait_ge(s["eb_ready"], NG)
            pe.wait_ge(s["dt_in"], 1)

            def conv_proj(g, j):
                if j < 2:
                    pe.wait_ge(s["z_ready"], g * JI + j + 1)
                else:
                    pe.wait_ge(s["xbc_ready"], g * JC + j - 1)
                dst = bank[j % 2][:, :].rearrange("p (b t) -> p b t", t=L)
                hi = c_hi[:, bass.ds(g * GT, GT)].rearrange("p (b t) -> p b t", t=L)
                lo = c_lo[:, bass.ds(g * GT, GT)].rearrange("p (b t) -> p b t", t=L)
                for k in range(KW):
                    w = slice(TAP0 + k * CD + j * P, TAP0 + k * CD + (j + 1) * P)
                    to, of = slice(k, L), slice(0, L - k)
                    mm(dst[:, :, to], in_hi[:, w], hi[:, :, of], start=(k == 0), stop=False)
                    mm(dst[:, :, to], in_hi[:, w], lo[:, :, of], start=False, stop=False)
                    ins = mm(dst[:, :, to], in_lo[:, w], hi[:, :, of], start=False, stop=(k == KW - 1))
                ins.then_inc(s["xbc_psum"], 1)

            def z_proj(g, j):
                pe.wait_ge(s["xbc_ready"], g * JC + 2 + j + 1)
                w, at = slice(j * P, (j + 1) * P), bass.ds(g * GT, GT)
                three(bank[j][:, :], in_hi[:, w], in_lo[:, w], c_hi[:, at], c_lo[:, at]).then_inc(s["z_psum"], 1)

            def transpose_x(g):
                pe.wait_ge(s["xbc_ready"], g * JC + JI)
                pe.wait_ge(s["e_ready"], g + 1)
                for b in range(GB):
                    for j in range(JI):
                        ins = tr(bank[2 + b // 2][:, (b % 2 * JI + j) * P:(b % 2 * JI + j + 1) * P],
                                 xbc[:, j, b * L:(b + 1) * L], ident[:, :])
                    if b % 2:
                        ins.then_inc(s["xs_T_psum"], 1)

            def c_dot_b(g):
                pe.wait_ge(s["xbc_ready"], (g + 1) * JC)
                for b in range(GB):
                    ins = mm(bank[4][:, b * L:(b + 1) * L], xbc[:, JI, b * L:(b + 1) * L],
                             xbc[:, JI + 1, b * L:(b + 1) * L], start=True, stop=True)
                ins.then_inc(s["g_psum"], 1)

            def spread_decays(g, b):
                if b == 0:
                    pe.wait_ge(s["dA_grp_ready"], g + 1)
                if b >= 2:
                    pe.wait_ge(s["scan_done"], g * GB + b - 1)
                for h in range(NH):
                    for k in range(3):
                        ins = mm(bank[5 + b % 2][:, h * L:(h + 1) * L],
                                 dA_grp[:, k, b * NH + h:b * NH + h + 1].broadcast_to([P, P]), identb[:, :],
                                 start=(k == 0), stop=(k == 2))
                ins.then_inc(s["bc_psum"], 1)

            def heads(g, b):
                pe.wait_ge(s["mix_ready"], g * GB + b + 1)
                pe.wait_ge(s["x_dt_ready"], g * 2 + 2)
                for h in range(NH):
                    lo = h % 2 * HD
                    ins = mm(bank[2 + h // 2][lo:lo + HD, b * L:(b + 1) * L], x_dt[:, b, h * HD:(h + 1) * HD],
                             mixer[:, b % 2, h * L:(h + 1) * L], start=True, stop=True)
                ins.then_inc(s["y_psum"], 1)

            def out_proj(g):
                pe.wait_ge(s["y_g_ready"], (g + 2) * JI)
                for b in range(GB):
                    for j in range(JI):
                        mm(bank[4][:, b * DM:(b + 1) * DM], y_g[:, j, b * L:(b + 1) * L], out_T[:, j, :],
                           start=(j == 0), stop=(j == JI - 1))

            def sum_squares(g):
                pe.wait_ge(s["y_sq_ready"], (g + 1) * JI)
                for b in range(GB):
                    for j in range(JI):
                        ins = mm(bank[7][:, b:b + 1], y_sq[:, j, b * L:(b + 1) * L], ones[:, 0:1],
                                 start=(j == 0), stop=(j == JI - 1))
                ins.then_inc(s["ss_psum"], 1)

            def transpose_r(g):
                pe.wait_ge(s["r_grp_ready"], (g + 1) * GB)
                for b in range(GB):
                    ins = tr(bank[2][:, b * L:(b + 1) * L], r_grp[:, b, :], ident[:, :])
                ins.then_inc(s["rT_psum"], 1)

            def mix_product(g):
                pe.wait_ge(s["rT_ready"], g + 1)
                for b in range(GB):
                    ins = mm(bank[3][:, b * P:(b + 1) * P], r_T[:, b * L:(b + 1) * L], mix_sb[:, 1, :],
                             start=True, stop=True)
                ins.then_inc(s["e_psum"], 1)

            def transpose_q1(g):
                pe.wait_ge(s["q1_ready"], g + 1)
                pe.wait_ge(s["y_out_ready"], g + 1)
                for b in range(GB):
                    ins = tr(bank[7][:, b * L // 2:(b + 1) * L // 2].bitcast(bf16), q1[:, b * DM:(b + 1) * DM],
                             identb[:, :])
                ins.then_inc(s["q1T_psum"], 1)

            def ffn_up(g, b):
                pe.wait_ge(s["q1T_ready"], g + 1)
                if b >= 2:
                    pe.wait_ge(s["h_pre_ready"], g * GB + b - 1)
                mm(bank[5 + b % 2][:, :], q1_T[:, b * L:(b + 1) * L], w1_qT[:, :], start=True, stop=True)\
                    .then_inc(s["h_psum"], 1)

            def transpose_q2(g, b):
                pe.wait_ge(s["q2_ready"], g * GB + b + 1)
                if b >= 2:
                    pe.wait_ge(s["q2T_ready"], g * GB + b - 1)
                for c in range(FC):
                    ins = tr(bank[5 + b % 2][:, c * L // 2:(c + 1) * L // 2].bitcast(bf16),
                             q2[:, b, c * P:(c + 1) * P], identb[:, :])
                ins.then_inc(s["q2T_psum"], 1)

            def ffn_down(g):
                for b in range(GB):
                    pe.wait_ge(s["q2T_ready"], g * GB + b + 1)
                    for c in range(FC):
                        ins = mm(bank[7][:, b * DM:(b + 1) * DM], q2_T[:, b, c * L:(c + 1) * L], w2_qT[:, c, :],
                                 start=(c == 0), stop=(c == FC - 1))
                ins.then_inc(s["o_psum"], 1)

            def tensor_turn(i, proj=True, ssm=True, ffn=True):
                if ssm:
                    transpose_x(i)
                    c_dot_b(i)
                    spread_decays(i, 0)
                    spread_decays(i, 1)
                if proj:
                    conv_proj(i + 1, 0)
                if ssm:
                    heads(i, 0)
                    spread_decays(i, 2)
                if ffn:
                    transpose_q1(i - 1)
                if ssm:
                    heads(i, 1)
                    spread_decays(i, 3)
                if proj:
                    conv_proj(i + 1, 1)
                if ssm:
                    heads(i, 2)
                    heads(i, 3)
                if ffn:
                    ffn_up(i - 1, 0)
                    ffn_up(i - 1, 1)
                if proj:
                    conv_proj(i + 1, 2)
                if ffn:
                    ffn_up(i - 1, 2)
                    ffn_up(i - 1, 3)
                if ssm:
                    out_proj(i)
                if proj:
                    conv_proj(i + 1, 3)
                if ssm:
                    sum_squares(i)
                if proj:
                    for j in range(JI):
                        z_proj(i + 1, j)
                if ffn:
                    transpose_q2(i - 1, 0)
                    transpose_q2(i - 1, 1)
                if ssm:
                    transpose_r(i)
                if ffn:
                    transpose_q2(i - 1, 2)
                    transpose_q2(i - 1, 3)
                if ssm:
                    mix_product(i)
                if ffn:
                    ffn_down(i - 1)

            pe.sem_inc(s["xs_T_psum"], 2)
            pe.sem_inc(s["g_psum"], 1)
            pe.sem_inc(s["bc_psum"], GB)
            tensor_turn(-1, ssm=False, ffn=False)
            tensor_turn(0, ffn=False)
            with pe.Fori(1, NG - 1) as i:
                tensor_turn(i)
            tensor_turn(NG - 1, proj=False)
            tensor_turn(NG, proj=False, ssm=False)

    return nc


_INS = ["x", "cond_1024", "L0_cond_gate_w", "L0_cond_gate_b", "L0_cond_time_w", "L0_cond_time_b", "L0_cond_ew1",
        "L0_cond_eb1", "L0_cond_ew2", "L0_cond_eb2", "L0_cond_sw1", "L0_cond_sb1", "L0_cond_sw2", "L0_cond_sb2",
        "L0_attn_in_proj_w", "L0_attn_conv_w", "L0_attn_conv_b", "L0_attn_dt_bias", "L0_attn_A_log", "L0_attn_D",
        "L0_attn_norm_w", "L0_attn_out_proj_w", "L0_cond2_weight_matrix", "L0_cond2_W_proj", "L0_cond2_b_proj",
        "L0_ffn_w1", "L0_ffn_b1", "L0_ffn_w2", "L0_ffn_b2"]


def kernel(**inputs):
    import numpy as _np
    import concourse.bacc as _bacc
    from concourse import mybir as _mybir
    from concourse.bass_utils import run_bass_kernel_spmd as _run

    nc = _bacc.Bacc("TRN2", target_bir_lowering=False, num_devices=1)
    arrays, args = {}, []
    for name in _INS:
        a = _np.ascontiguousarray(inputs[name])
        arrays[f"in_{name}"] = a
        args.append(nc.dram_tensor(f"in_{name}", a.shape, _mybir.dt.from_np(a.dtype), kind="ExternalInput").ap())
    args.append(nc.dram_tensor("out_dram", inputs["x"].shape, _mybir.dt.float32, kind="ExternalOutput").ap())
    build(nc, *args)
    r = _run(nc, [arrays], core_ids=[0])
    return r.results[0]["out_dram"]
```

```python
import concourse.bass as bass
from concourse import mybir
from contextlib import ExitStack


class Order:

    def __init__(self, eng, sem):
        self.eng, self.sem, self.count, self.turn, self.per = eng, sem, 0, None, 0

    def step(self, ins):
        self.count += 1
        ins.then_inc(self.sem, 1)
        return self.count

    def wait(self, mark=None):
        mark = self.count if mark is None else mark
        self.eng.wait_ge(self.sem, mark if self.turn is None else self.turn * self.per + mark)

    def link(self, ins):
        self.step(ins)
        self.wait()

    def enter(self, turn, per):
        self.turn, self.per, self.first = turn, per, self.count

    def leave(self, turns):
        assert self.count - self.first == self.per, (self.count - self.first, self.per)
        self.turn, self.count = None, self.first + turns * self.per


class Stage:

    def __init__(self, eng, sem, per):
        self.eng, self.sem, self.per, self.base, self.n = eng, sem, per, None, per

    def group(self, g):
        assert self.n == self.per, (self.n, self.per)
        self.base, self.n = g * self.per, 0

    def resume(self, g):
        self.base = g * self.per

    def step(self, ins):
        self.n += 1
        ins.then_inc(self.sem, 1)
        return self.n

    def wait(self, mark=None):
        self.eng.wait_ge(self.sem, self.base + (self.n if mark is None else mark))

    def link(self, ins):
        self.step(ins)
        self.wait()


def build(nc, x, cond, gate_w, gate_b, time_w, time_b, ew1, eb1, ew2, eb2, sw1, sb1, sw2, sb2,
          in_w, conv_w, conv_b, dt_bias, A_log, D, norm_w, out_w, mix_w, proj_w, proj_b,
          f_w1, f_b1, f_w2, f_b2, out):
    f32 = mybir.dt.float32
    bf16 = mybir.dt.bfloat16
    f16 = mybir.dt.float16
    ALU = mybir.AluOpType
    ACT = mybir.ActivationFunctionType
    AX = mybir.AxisListType

    P = 128
    B, L, DM = x.shape
    E = gate_w.shape[1]
    H = sw1.shape[1]
    HC = H // P
    DI = out_w.shape[1]
    JI = DI // P
    NH = dt_bias.shape[0]
    HD = DI // NH
    CD = conv_w.shape[0]
    JC = CD // P
    KW = conv_w.shape[1]
    F = f_w1.shape[0]
    FC = F // P
    GB = 4
    NG = B // GB
    GT = GB * L
    L3 = L // 3
    EPS = 1e-5
    MAGIC = 1.5 * 2.0 ** 23
    K = 2
    U = GB * K
    XS, WS, CS, IS = 8.0, 1024.0, 8.0, 64.0

    ctx = ExitStack()
    with ctx:
        def sb(name, shape, dt=f32):
            return ctx.enter_context(nc.sbuf_tensor(name, shape, dt))

        def sem(name):
            return ctx.enter_context(nc.semaphore(name))

        bank = [ctx.enter_context(nc.psum_tensor(f"bank{i}", [P, 512], f32)) for i in range(8)]

        x_tok = sb("x_tok", [P, B, DM])
        x_hi = sb("x_hi", [P, B * L], f16)
        x_lo = sb("x_lo", [P, B * L], f16)
        c_hi = sb("c_hi", [P, B * L], f16)
        c_lo = sb("c_lo", [P, B * L], f16)
        c_grp = sb("c_grp", [P, GB, DM])
        res = sb("res", [P, B, DM])
        dt_raw = sb("dt_raw", [P, B, NH])

        up_nat = sb("up_nat", [P, E + 1, H])
        up_hi = sb("up_hi", [P, (E + 1) * H], f16)
        up_lo = sb("up_lo", [P, (E + 1) * H], f16)
        down = sb("down", [P, (E + 1) * HC * DM])
        eb1_rows = sb("eb1_rows", [E, H])
        b2_rows = sb("b2_rows", [E + 1, DM])
        C_SB1 = 0
        C_CB = C_SB1 + HC
        C_PB = C_CB + JC
        C_NW = C_PB + 1
        C_COND = C_NW + JI
        C_END = C_COND + B
        rows = sb("rows", [C_END, P])
        cols = sb("cols", [P, C_END])
        gate_w_sb = sb("gate_w_sb", [P, 3, E])
        gate_b_sb = sb("gate_b_sb", [B, E])
        time_w_sb = sb("time_w_sb", [P, 2 * E])
        time_b_sb = sb("time_b_sb", [B, 2 * E])
        in_nat = sb("in_nat", [P, 6, DM])
        in_nat_dt = sb("in_nat_dt", [NH, DM])
        TAP0 = DI + NH
        in_hi = sb("in_hi", [P, TAP0 + KW * CD], f16)
        in_lo = sb("in_lo", [P, TAP0 + KW * CD], f16)
        conv_w_sb = sb("conv_w_sb", [P, JC, KW])
        dt_bias_sb = sb("dt_bias_sb", [P, NH])
        A_sb = sb("A_sb", [P, NH])
        A_pos = sb("A_pos", [P, NH])
        D_all = sb("D_all", [P, NH])
        D_col = sb("D_col", [P, JI])
        out_nat = sb("out_nat", [P, DI])
        out_T = sb("out_T", [P, JI, DM])
        mix_sb = sb("mix_sb", [P, 2, P])
        proj_sb = sb("proj_sb", [P, P])
        w1_nat = sb("w1_nat", [P, FC, DM])
        w2_nat = sb("w2_nat", [P, F])
        w1_q = sb("w1_q", [P, FC, DM], bf16)
        w2_q = sb("w2_q", [P, F], bf16)
        w1_qT = sb("w1_qT", [P, F], bf16)
        w2_qT = sb("w2_qT", [P, FC, DM], bf16)
        b1_sb = sb("b1_sb", [P, F])
        b2_sb = sb("b2_sb", [P, DM])

        ident = sb("ident", [P, P])
        identb = sb("identb", [P, P], bf16)
        ident4 = sb("ident4", [P, NH, L])
        ones = sb("ones", [P, P])
        zeros = sb("zeros", [P, P], bf16)
        part = sb("part", [P, 1])
        lower = sb("lower", [B, E, E])
        number = sb("number", [B, 2, E])
        mask = sb("mask", [P, E + 1])
        mask_T = sb("mask_T", [E + 1, P])
        minus_half = sb("minus_half", [P, GB])

        thirds = sb("thirds", [P, B, 3])
        agg = sb("agg", [P, 3, B])
        cond_silu = sb("cond_silu", [P, B])
        mod = sb("mod", [B, 2 * E])
        gl = sb("gl", [B, E])
        gmax = sb("gmax", [B, 1])
        gsum = sb("gsum", [B, 1])
        prob = sb("prob", [B, E])
        gt = sb("gt", [B, E, E])
        eq = sb("eq", [B, E, E])
        rank = sb("rank", [B, E])
        pick = sb("pick", [B, K, E])
        w_all = sb("w_all", [B, E + 1])
        sent = sb("sent", [B, K * E + K])
        spread = sb("spread", [B, B, K * E + K])
        picked = sb("picked", [B, K, E])
        w_tok = sb("w_tok", [P, B * K, E])
        w_slot = sb("w_slot", [P, B, K])
        offset = sb("offset", [1, B * K], mybir.dt.int32)
        pick_T = sb("pick_T", [E, K, B])
        w_T = sb("w_T", [E + 1, B])
        w_mask_T = sb("w_mask_T", [E + 1, GB, L])
        slot_bias = sb("slot_bias", [P, B, K, HC])

        hid_s = sb("hid_s", [P, HC, GT])
        pre = sb("pre", [P, 2, HC * L])
        hid = sb("hid", [P, 4, HC * L])

        dt_all = sb("dt_all", [P, B, NH])
        dA_all = sb("dA_all", [P, B, NH])
        dt_t = [sb(f"dt_t{i}", [P, B * NH]) for i in range(4)]
        dA_rest = sb("dA_rest", [P, 2, B * NH])
        dA_parts = sb("dA_parts", [P, 3, B * NH], bf16)
        ffn_work = sb("ffn_work", [P, 4, GB * F])
        z_act = sb("z_act", [P, JI, GT])
        xD = sb("xD", [P, JI, GT])
        in_tap = xD[:, 0, :].rearrange("p (c d) -> p c d", d=DM)
        xbc = sb("xbc", [P, JC, GT])
        x_dt = sb("x_dt", [P, GB, DI])
        decay = sb("decay", [P, 2, NH * L])
        mixer = sb("mixer", [P, 2, NH * L])
        y_g = sb("y_g", [P, JI, GT])
        y_sq = sb("y_sq", [P, JI, GT])
        y_ms = sb("y_ms", [P, GB])
        y_r = sb("y_r", [P, GB])
        r_grp = sb("r_grp", [P, GB, DM])
        r_T = sb("r_T", [P, GT])
        u_T = sb("u_T", [P, B])
        uw = sb("uw", [B, P])
        uw_rest = sb("uw_rest", [B, 2, P])
        uw_parts = sb("uw_parts", [P, 3, P], bf16)

        e_all = up_nat[:, 0:E, :].rearrange("p e (b d) -> p (e b) d", d=DM)
        wabs = ffn_work[:, 3, 0:1024].rearrange("p (k n) -> p k n", k=2)
        wsum = sb("wsum", [P, 2])
        wmean = sb("wmean", [P, 2])
        wscale = sb("wscale", [P, 2])
        wtmp = ffn_work[:, 3, 1024:2048].rearrange("p (k n) -> p k n", k=2)
        sq_scr = ffn_work[:, 2, :].rearrange("p (b f) -> p b f", f=F)
        ssq = sb("ssq", [P, 2, GB])
        amax = sb("amax", [P, 2, GB])
        ms = sb("ms", [P, 2, GB])
        rr = sb("rr", [P, 2, GB])
        cl = sb("cl", [P, 2, GB])
        inv = sb("inv", [P, 2, GB])
        qm = sb("qm", [P, 2, GB])
        qk = sb("qk", [P, 2, GB])
        q1_f = sb("q1_f", [P, GT])
        q1 = sb("q1", [P, GT], bf16)
        q1_T = sb("q1_T", [P, GT], bf16)
        h_pre = ffn_work[:, 0, :].rearrange("p (b f) -> p b f", f=F)
        h_act = ffn_work[:, 1, :].rearrange("p (b f) -> p b f", f=F)
        q2_f = ffn_work[:, 3, :].rearrange("p (b f) -> p b f", f=F)
        halves = hid[:, :, :].rearrange("p u n -> p (u n)").bitcast(bf16).rearrange("p (k b f) -> p k b f", k=2, f=F)
        q2, q2_T = halves[:, 0], halves[:, 1]
        y_out = sb("y_out", [P, GB, DM])

        names = """proj_in thirds_ready bias_in down_s_in downs_in ident_ready shared_in experts_in rows_in gate_in
            in_in mix_in ffn_in out_sent v_order p_order consts x_T_psum x_hi_ready x_lo_ready cols_psum
            cols_ready agg_ready silu_ready gate_psum gl_ready prob_exp spread_ready sent_psum sent_ready
            gate_T_psum gate_T_ready slot_bias_psum slot_bias_ready w_mask_T_ready up_hi_ready up_lo_ready
            up_s_done up_done pre_done gelu_s_done gelu_done down_s_done down_done y_s_copied y_added c_T_psum
            c_hi_ready c_lo_ready res_ready dt_psum in_psum in_hi_ready in_ready out_psum out_ready in_tap_ready
            u_psum u_ready uw_psum uw_ready abs_done sum_psum wmean_ready w_q_ready w_qT_psum w_qT_ready dt_in
            dt_exp dt_w dt_ln dt_mul z_psum z_ready xbc_psum xbc_ready xD_ready res_b2_ready out_proj_psum v_b
            v_last v_c dA_ready xs_T_psum x_dt_ready g_psum bc_psum scan_done mix_ready y_psum y_g_ready
            y_sq_ready ss_psum ms_ready yr_ready r_grp_ready rT_psum rT_ready e_psum e_ready ssq1 ms1 rr1
            q1_ready q1T_psum q1T_ready h_psum h_pre_ready h_act_ready ssq2 ms2 rr2 q2_ready q2T_psum q2T_ready
            q2_f_ready o_psum y_out_ready""".split()
        s = {n: sem(n) for n in names}
        x_in = [sem(f"x_in{g}") for g in range(NG)]

        X_BANK = (7, 4, 5, 3)
        ROWS = 5

        def col(c, n=1):
            return cols[:, c:c + n]

        def in_part(k):
            return slice(0, TAP0) if k is None else bass.ds(TAP0 + k * CD, CD)

        def ffn_bank(g, b):
            return bank[b % 2] if last(g) else bank[5 + b % 2]

        def q1_bank(g):
            return bank[4] if last(g) else bank[0] if isinstance(g, int) else bank[7]

        def last(g):
            return isinstance(g, int) and g == NG - 1

        def grp(t, g):
            return t[:, bass.ds(g * GB, GB), :].rearrange("p b d -> p (b d)")

        block = ctx.enter_context(nc.Block())

        @block.sync
        def _(sp):
            for g in range(NG):
                sp.dma_start(x_tok[:, g * GB:(g + 1) * GB, :],
                             x[g * GB:(g + 1) * GB, :, :].rearrange("b t d -> t b d")).then_inc(x_in[g], 16)
            sp.dma_start(proj_sb[:, :], proj_w).then_inc(s["proj_in"], 16)
            sp.dma_start(up_nat[:, E, :], sw1).then_inc(s["shared_in"], 16)
            sp.dma_start(up_nat[:, 0:E, :], ew1.rearrange("e d h -> d e h")).then_inc(s["experts_in"], 16)
            sp.dma_start(down[:, E * H:].rearrange("p (c d) -> p c d", d=DM),
                         sw2.rearrange("(c p) d -> p c d", p=P)).then_inc(s["down_s_in"], 16)
            sp.dma_start(down[:, 0:E * H].rearrange("p (c d) -> p c d", d=DM),
                         ew2.rearrange("e (c p) d -> p (e c) d", p=P)).then_inc(s["downs_in"], 16)
            for dst, src in ((eb1_rows[:, :], eb1), (b2_rows[0:E, :], eb2),
                             (b2_rows[E:E + 1, :], sb2.rearrange("(c p) -> c p", p=P))):
                sp.dma_start(dst, src).then_inc(s["bias_in"], 16)
            for dst, src in ((in_nat[:, :, :], in_w[0:6 * P, :].rearrange("(c p) d -> p c d", p=P)),
                             (in_nat_dt[:, :], in_w[6 * P:6 * P + NH, :]),
                             (conv_w_sb[:, :, :], conv_w.rearrange("(c p) k -> p c k", p=P)),
                             (dt_bias_sb[:, :], dt_bias.partition_broadcast(P)),
                             (A_sb[:, :], A_log.partition_broadcast(P)),
                             (D_all[:, :], D.partition_broadcast(P)),
                             (out_nat[:, :], out_w)):
                sp.dma_start(dst, src).then_inc(s["in_in"], 16)
            for dst, src in ((w1_nat[:, :, :], f_w1.rearrange("(c p) d -> p c d", p=P)), (w2_nat[:, :], f_w2),
                             (b1_sb[:, :], f_b1.partition_broadcast(P)), (b2_sb[:, :], f_b2.partition_broadcast(P))):
                sp.dma_start(dst, src).then_inc(s["ffn_in"], 16)
            sp.sem_inc(s["out_sent"], 16)
            with sp.Fori(0, NG) as g:
                sp.wait_ge(s["y_out_ready"], g + 2)
                sp.dma_start(out[bass.ds(g * GB, GB), :, :].rearrange("b t d -> t b d"),
                             y_out[:, :, :]).then_inc(s["out_sent"], 16)
            sp.wait_ge(s["out_sent"], 16 * (NG + 1))

        @block.gpsimd
        def _(pool):
            order = Order(pool, s["p_order"])
            order.link(pool.memset(ident[:, :], 0.0))
            order.link(pool.affine_select(out=ident[:, :], in_=ident[:, :], compare_op=ALU.not_equal, fill=1.0,
                                          base=0, pattern=[[-1, P]], channel_multiplier=1))
            pool.sem_inc(s["ident_ready"], 1)
            for dst, src in ((gate_w_sb[:, :, :], gate_w.rearrange("(j p) e -> p j e", p=P)),
                             (gate_b_sb[:, :], gate_b.partition_broadcast(B)),
                             (time_w_sb[:, :], time_w),
                             (time_b_sb[:, :], time_b.partition_broadcast(B))):
                pool.dma_start(dst, src).then_inc(s["gate_in"], 16)
            pool.dma_start(mix_sb[:, :, :], mix_w.rearrange("(k p) c -> p k c", p=P)).then_inc(s["mix_in"], 16)

            order.step(pool.memset(mask[:, :], 1.0))
            order.step(pool.memset(part[:, :], 1.0))
            order.step(pool.memset(lower[:, :, :], 1.0))
            order.step(pool.memset(ones[:, :], 1.0))
            order.step(pool.memset(minus_half[:, :], -0.5))
            for e in range(E):
                order.step(pool.memset(number[:, :, e:e + 1], float(e)))
            order.step(pool.memset(w_all[:, :], 1.0))
            order.step(pool.memset(zeros[:, :], 0.0))
            order.step(pool.memset(uw_parts[:, :, :], 0.0))
            order.wait()
            order.step(pool.affine_select(out=part[:, :], in_=part[:, :], compare_op=ALU.is_ge, fill=0.0,
                                          base=-2 * L3, pattern=[[0, 1]], channel_multiplier=1))
            order.step(pool.affine_select(out=mask[:, 1:2], in_=mask[:, 1:2], compare_op=ALU.is_gt, fill=0.0,
                                          base=L3, pattern=[[0, 1]], channel_multiplier=-1))
            order.step(pool.affine_select(out=mask[:, 2:3], in_=mask[:, 2:3], compare_op=ALU.is_ge, fill=0.0,
                                          base=-L3, pattern=[[0, 1]], channel_multiplier=1))
            order.step(pool.affine_select(out=lower[:, :, :], in_=lower[:, :, :], compare_op=ALU.is_gt, fill=0.0,
                                          base=0, pattern=[[1, E], [-1, E]], channel_multiplier=0))
            order.wait()
            order.link(pool.tensor_tensor(mask[:, 1:2], mask[:, 1:2], part[:, :], ALU.add))
            pool.sem_inc(s["consts"], 1)
            order.step(pool.tensor_copy(identb[:, :], ident[:, :]))
            for h in range(NH):
                order.step(pool.tensor_copy(ident4[:, h, :], ident[:, :]))
            order.wait()
            pool.sem_inc(s["consts"], 1)

            def bias_weights(g):
                pool.tensor_tensor(w_mask_T[:, :, :], w_T[:, bass.ds(g * GB, GB)].unsqueeze(2).broadcast_to([E + 1, GB, L]),
                                   mask_T[:, :].unsqueeze(1).broadcast_to([E + 1, GB, L]), ALU.mult)\
                    .then_inc(s["w_mask_T_ready"], 1)

            def residual(g):
                pool.wait_ge(s["y_added"], (g + 2) * GB)
                pool.tensor_tensor(grp(res, g), c_grp[:, :, :].rearrange("p b d -> p (b d)"), grp(x_tok, g), ALU.add)\
                    .then_inc(s["res_ready"], 1)

            def times_tap(k):
                pool.tensor_tensor(in_tap[:, :, :], in_nat[:, JI:, :],
                                   conv_w_sb[:, :, bass.ds(k, 1)].broadcast_to([P, JC, DM]), ALU.mult)\
                    .then_inc(s["in_tap_ready"], 1)

            pool.wait_ge(s["gate_T_ready"], 1)
            bias_weights(0)
            pool.wait_ge(s["in_in"], 16 * 7)
            times_tap(0)
            with pool.Fori(0, NG - 1) as g:
                pool.wait_ge(s["down_s_done"], g + 1)
                bias_weights(g + 1)
                residual(g)
                pool.wait_ge(s["in_psum"], g + 2)
                times_tap(g + 1)
            pool.wait_ge(s["wmean_ready"], 1)
            for k, (nat, q) in enumerate(((w1_nat[:, :, :].rearrange("p c d -> p (c d)"),
                                           w1_q[:, :, :].rearrange("p c d -> p (c d)")),
                                          (w2_nat[:, :], w2_q[:, :]))):
                order.link(pool.tensor_scalar(wtmp[:, k, :], nat, wscale[:, k:k + 1], MAGIC, ALU.mult, ALU.add))
                order.link(pool.tensor_scalar(wtmp[:, k, :], wtmp[:, k, :], MAGIC, 1.0, ALU.subtract, ALU.min))
                pool.tensor_scalar(q, wtmp[:, k, :], -1.0, None, ALU.max).then_inc(s["w_q_ready"], 1)
            residual(NG - 1)

            pool.wait_ge(s["out_ready"], 1)

            def times_D(g):
                pool.wait_ge(s["xbc_ready"], g * JC + JI)
                pool.wait_ge(s["y_g_ready"], (g + 1) * JI)
                pool.tensor_tensor(xD[:, :, :], xbc[:, 0:JI, :], D_col[:, :].unsqueeze(2).broadcast_to([P, JI, GT]),
                                   ALU.mult).then_inc(s["xD_ready"], 1)

            def norm_power(g):
                pool.wait_ge(s["ms_ready"], g + 1)
                pool.tensor_tensor(y_r[:, :], y_ms[:, :], minus_half[:, :], ALU.pow).then_inc(s["yr_ready"], 1)

            def add_b2(g):
                pool.wait_ge(s["r_grp_ready"], (g + 1) * GB)
                pool.tensor_tensor(res[:, bass.ds(g * GB, GB), :], r_grp[:, :, :],
                                   b2_sb[:, :].unsqueeze(1).broadcast_to([P, GB, DM]), ALU.add)\
                    .then_inc(s["res_b2_ready"], 1)

            def quant_power(g, k):
                pool.wait_ge(s[f"ms{k + 1}"], g + 1)
                pool.tensor_tensor(rr[:, k, :], ms[:, k, :], minus_half[:, :], ALU.pow)\
                    .then_inc(s[f"rr{k + 1}"], 1)

            def quant_power_half(g, half):
                pool.wait_ge(s["ms2"], g + half + 1)
                at = slice(2 * half, 2 * half + 2)
                pool.tensor_tensor(rr[:, 1, at], ms[:, 1, at], minus_half[:, at], ALU.pow).then_inc(s["rr2"], 1)

            def pool_turn(i, ssm=True, ffn=True):
                if ffn:
                    quant_power(i - 1, 0)
                if ssm:
                    times_D(i)
                    norm_power(i)
                if ffn:
                    quant_power(i - 1, 1)
                if ssm:
                    add_b2(i)

            pool.sem_inc(s["xD_ready"], 1)
            pool.sem_inc(s["res_b2_ready"], 1)
            pool_turn(0, ffn=False)
            with pool.Fori(1, NG - 1) as i:
                pool_turn(i)
            quant_power(NG - 2, 0)
            times_D(NG - 1)
            norm_power(NG - 1)
            quant_power(NG - 2, 1)
            add_b2(NG - 1)
            quant_power(NG - 1, 0)
            quant_power_half(NG - 1, 0)
            quant_power_half(NG - 1, 1)

        @block.scalar
        def _(act):
            small = ((cond, C_COND), (sb1.rearrange("(c p) -> c p", p=P), C_SB1),
                     (conv_b.rearrange("(c p) -> c p", p=P), C_CB), (proj_b.rearrange("(c p) -> c p", p=P), C_PB),
                     (norm_w.rearrange("(c p) -> c p", p=P), C_NW))
            for src, c in small:
                act.dma_start(rows[c:c + src.shape[0], :], src).then_inc(s["rows_in"], 16)
            assert len(small) == ROWS

            for g in range(NG):
                if g == NG - 1:
                    act.wait_ge(s["shared_in"], 16)
                    act.activation(up_hi[:, E * H:], up_nat[:, E, :], ACT.Copy, scale=WS).then_inc(s["up_hi_ready"], 1)
                act.wait_ge(s["thirds_ready"], g + 1)
                act.activation(x_hi[:, g * GT:(g + 1) * GT], bank[X_BANK[g]][:, :], ACT.Copy, scale=XS)\
                    .then_inc(s["x_hi_ready"], 1)
            act.wait_ge(s["cols_ready"], 1)
            act.activation(cond_silu[:, :], col(C_COND, B), ACT.Silu).then_inc(s["silu_ready"], 1)
            act.wait_ge(s["gl_ready"], 1)
            act.activation(prob[:, :], gl[:, :], ACT.Exp, bias=gmax[:, 0:1], accum_out=gsum[:, 0:1])\
                .then_inc(s["prob_exp"], 1)
            act.wait_ge(s["u_psum"], 1)
            act.activation(u_T[:, :], bank[7][:, 0:B], ACT.Gelu, bias=col(C_PB)).then_inc(s["u_ready"], 1)
            act.wait_ge(s["experts_in"], 16)
            for e in range(E):
                act.activation(up_hi[:, e * H:(e + 1) * H], up_nat[:, e, :], ACT.Copy, scale=WS)\
                    .then_inc(s["up_hi_ready"], 1)
            act.sem_inc(s["gelu_done"], 2)
            act.sem_inc(s["y_s_copied"], 1)

            def shared_gelu(g, c):
                act.wait_ge(s["up_s_done"], g * HC + c + 1)
                act.activation(hid_s[:, c, :], bank[c % 3][:, :], ACT.Gelu_apprx_tanh, bias=col(C_SB1 + c),
                               scale=1.0 / (XS * WS)).then_inc(s["gelu_s_done"], 1)

            def slot_gelu(g, u):
                act.wait_ge(s["pre_done"], g * U + u + 1)
                act.wait_ge(s["down_done"], g * U + u + 1)
                act.activation(hid[:, u % 4, :], pre[:, u % 2, :], ACT.Gelu_apprx_tanh).then_inc(s["gelu_done"], 1)

            def copy_shared(g, first):
                act.wait_ge(s["down_s_done"], g + 1)
                if not first:
                    act.wait_ge(s["c_T_psum"], g)
                    act.wait_ge(s["res_ready"], g)
                act.copy(c_grp[:, :, :].rearrange("p b d -> p (b d)"), bank[3][:, :]).then_inc(s["y_s_copied"], 1)

            def first_parts(g):
                act.wait_ge(s["c_T_psum"], g + 1)
                act.activation(c_hi[:, bass.ds(g * GT, GT)], bank[6][:, :], ACT.Copy, scale=CS)\
                    .then_inc(s["c_hi_ready"], 1)

            def in_first(k, n):
                act.wait_ge(s["in_psum"], n)
                at = in_part(k)
                act.activation(in_hi[:, at], bank[7][:, 0:TAP0 if k is None else CD], ACT.Copy, scale=IS)\
                    .then_inc(s["in_hi_ready"], 1)

            def act_group(g, more):
                for u in range(2, U):
                    slot_gelu(g, u)
                if more:
                    act.wait_ge(s["down_s_done"], g + 1)
                    for c in range(HC):
                        shared_gelu(g + 1, c)
                    slot_gelu(g + 1, 0)
                    slot_gelu(g + 1, 1)
                in_first(g, g + 2)
                first_parts(g)
                if more:
                    copy_shared(g + 1, False)

            for c in range(HC):
                shared_gelu(0, c)
            slot_gelu(0, 0)
            slot_gelu(0, 1)
            in_first(None, 1)
            act.wait_ge(s["ffn_in"], 64)
            act.activation(wabs[:, 0, :], w1_nat[:, :, :].rearrange("p c d -> p (c d)"), ACT.Abs,
                           accum_out=wsum[:, 0:1]).then_inc(s["abs_done"], 1)
            act.activation(wabs[:, 1, :], w2_nat[:, :], ACT.Abs, accum_out=wsum[:, 1:2]).then_inc(s["abs_done"], 1)
            copy_shared(0, True)
            with act.Fori(0, NG - 1) as g:
                act_group(g, True)
            act_group(NG - 1, False)

            act.sem_inc(s["e_ready"], 1)
            act.sem_inc(s["z_ready"], JI)
            for k, dst in enumerate((w1_qT[:, :], w2_qT[:, :, :].rearrange("p c d -> p (c d)"))):
                act.wait_ge(s["w_qT_psum"], k + 1)
                act.copy(dst, bank[6 - k][:, 0:256].bitcast(bf16)).then_inc(s["w_qT_ready"], 1)

            act.activation(A_pos[:, :], A_sb[:, :], ACT.Exp).then_inc(s["dt_exp"], 1)
            act.wait_ge(s["dt_in"], 1)
            act.activation(dt_t[1][:, :], dt_t[0][:, :], ACT.Exp, scale=-1.0).then_inc(s["dt_exp"], 1)
            act.wait_ge(s["dt_w"], 1)
            act.activation(dt_t[3][:, :], dt_t[2][:, :], ACT.Ln).then_inc(s["dt_ln"], 1)
            act.wait_ge(s["dt_mul"], 1)
            act.activation(dA_all[:, :, :].rearrange("p b h -> p (b h)"), dt_t[0][:, :], ACT.Exp, scale=-1.0)\
                .then_inc(s["dt_exp"], 1)

            def silu_x(g, j):
                act.wait_ge(s["xbc_psum"], g * JC + j + 1)
                if j < JI:
                    act.wait_ge(s["xs_T_psum"], (g + 1) * 2)
                    act.wait_ge(s["xD_ready"], g + 1)
                else:
                    act.wait_ge(s["g_psum"], g + 1)
                act.activation(xbc[:, j, :], bank[j % 2][:, :], ACT.Silu, bias=col(C_CB + j),
                               scale=1.0 / (CS * IS)).then_inc(s["xbc_ready"], 1)

            def silu_z(g, j):
                act.wait_ge(s["z_psum"], g * JI + j + 1)
                act.wait_ge(s["y_g_ready"], (g + 1) * JI)
                act.activation(z_act[:, j, :], bank[j][:, :], ACT.Silu, scale=1.0 / (CS * IS)).then_inc(s["z_ready"], 1)

            def squares(g):
                for j in range(JI):
                    act.wait_ge(s["y_g_ready"], (g + 1) * JI + j + 1)
                    act.activation(y_sq[:, j, :], y_g[:, j, :], ACT.Square).then_inc(s["y_sq_ready"], 1)

            def copy_r_T(g):
                act.wait_ge(s["rT_psum"], g + 1)
                act.copy(r_T[:, :], bank[2][:, :]).then_inc(s["rT_ready"], 1)

            def copy_e(g):
                act.wait_ge(s["e_psum"], g + 1)
                act.copy(grp(e_all, g), bank[3][:, :]).then_inc(s["e_ready"], 1)

            def squares_1(g):
                for b in range(GB):
                    act.activation(sq_scr[:, b, 0:DM], e_all[:, bass.ds(g * GB + b, 1), :].rearrange("p b d -> p (b d)"),
                                   ACT.Square, accum_out=ssq[:, 0, b:b + 1]).then_inc(s["ssq1"], 1)

            def copy_q1_T(g):
                act.wait_ge(s["q1T_psum"], g + 1)
                act.copy(q1_T[:, :], q1_bank(g)[:, 0:GT // 2].bitcast(bf16)).then_inc(s["q1T_ready"], 1)

            def gelu(g, b):
                act.wait_ge(s["h_pre_ready"], g * GB + b + 1)
                act.activation(h_act[:, b, :], h_pre[:, b, :], ACT.Gelu).then_inc(s["h_act_ready"], 1)

            def squares_2(g, b):
                act.wait_ge(s["h_act_ready"], g * GB + b + 1)
                act.activation(sq_scr[:, b, :], h_act[:, b, :], ACT.Square,
                               accum_out=ssq[:, 1, b:b + 1]).then_inc(s["ssq2"], 1)

            def whole_2(g, b):
                act.wait_ge(s["q2_f_ready"], b + 1)
                act.activation(q2[:, b, :], q2_f[:, b, :], ACT.Copy, bias=-MAGIC).then_inc(s["q2_ready"], 1)

            def copy_q2_T(g, b):
                act.wait_ge(s["q2T_psum"], g * GB + b + 1)
                act.copy(q2_T[:, b, :], ffn_bank(g, b)[:, 0:F // 2].bitcast(bf16)).then_inc(s["q2T_ready"], 1)

            def act_turn(i, proj=True, ssm=True, ffn=True):
                if proj:
                    silu_x(i + 1, 0)
                if ffn:
                    copy_q1_T(i - 1)
                if proj:
                    silu_x(i + 1, 1)
                if ffn:
                    gelu(i - 1, 0)
                    gelu(i - 1, 1)
                if ssm:
                    squares(i)
                if ffn:
                    gelu(i - 1, 2)
                    gelu(i - 1, 3)
                    for b in range(GB):
                        squares_2(i - 1, b)
                if proj:
                    silu_x(i + 1, 2)
                    silu_x(i + 1, 3)
                    for j in range(JI):
                        silu_z(i + 1, j)
                if ssm:
                    copy_r_T(i)
                if ffn:
                    copy_q2_T(i - 1, 0)
                    copy_q2_T(i - 1, 1)
                if ssm:
                    copy_e(i)
                    act.wait_ge(s["e_ready"], i + 2)
                if ffn:
                    copy_q2_T(i - 1, 2)
                    copy_q2_T(i - 1, 3)
                if ssm:
                    squares_1(i)

            act_turn(-1, ssm=False, ffn=False)
            act_turn(0, ffn=False)
            with act.Fori(1, NG - 1) as i:
                act_turn(i)
            f, m = NG - 2, NG - 1
            copy_q1_T(f)
            squares(m)
            for b in range(GB):
                gelu(f, b)
            for b in range(GB - 1):
                squares_2(f, b)
            copy_r_T(m)
            squares_2(f, GB - 1)
            copy_e(m)
            act.wait_ge(s["e_ready"], m + 2)
            squares_1(m)
            copy_q2_T(f, 0)
            copy_q2_T(f, 1)
            copy_q1_T(m)
            gelu(m, 0)
            copy_q2_T(f, 2)
            copy_q2_T(f, 3)
            gelu(m, 1)
            for b in range(2):
                squares_2(m, b)
            for b in range(2, GB):
                gelu(m, b)
            for b in range(2, GB):
                squares_2(m, b)
            whole_2(m, 0)
            whole_2(m, 1)
            copy_q2_T(m, 0)
            copy_q2_T(m, 1)
            whole_2(m, 2)
            whole_2(m, 3)
            copy_q2_T(m, 2)
            copy_q2_T(m, 3)

        @block.vector
        def _(dve):
            order = Order(dve, s["v_order"])
            v, link = nc.vector, order.link

            def exact_parts(whole, rest, parts, n):
                for k in range(3):
                    link(v.tensor_copy(parts[0:n, k, :], whole))
                    if k < 2:
                        link(v.tensor_tensor(rest[0:n, k, :], whole, parts[0:n, k, :], ALU.subtract))
                        whole = rest[0:n, k, :]

            def x_second(g):
                dve.wait_ge(s["x_hi_ready"], g + 1)
                at = slice(g * GT, (g + 1) * GT)
                v.scalar_tensor_tensor(out=x_lo[:, at], in0=bank[X_BANK[g]][:, :], scalar=XS, in1=x_hi[:, at],
                                       op0=ALU.mult, op1=ALU.subtract).then_inc(s["x_lo_ready"], 1)

            def up_second(e, n):
                dve.wait_ge(s["up_hi_ready"], n)
                v.scalar_tensor_tensor(out=up_lo[:, e * H:(e + 1) * H], in0=up_nat[:, e, :], scalar=WS,
                                       in1=up_hi[:, e * H:(e + 1) * H], op0=ALU.mult, op1=ALU.subtract)\
                    .then_inc(s["up_lo_ready"], 1)

            for g in range(NG):
                dve.wait_ge(s["x_T_psum"], g + 1)
                tokens = bank[X_BANK[g]][:, :].rearrange("p (b t) -> p b t", t=L)
                order.step(v.tensor_reduce(thirds[:, g * GB:(g + 1) * GB, 0:2],
                                           tokens[:, :, 0:2 * L3].rearrange("p b (r t) -> p b r t", t=L3), AX.X, ALU.add))
                v.tensor_reduce(thirds[:, g * GB:(g + 1) * GB, 2:3], tokens[:, :, 2 * L3:], AX.X, ALU.add)\
                    .then_inc(s["thirds_ready"], 1)
            dve.wait_ge(s["thirds_ready"], NG)
            order.wait()
            order.step(v.tensor_tensor(agg[:, 1, :], thirds[:, :, 0], thirds[:, :, 2], ALU.add))
            link(v.tensor_tensor(agg[:, 2, :], thirds[:, :, 1], thirds[:, :, 2], ALU.add))
            link(v.tensor_tensor(agg[:, 0, :], agg[:, 2, :], thirds[:, :, 0], ALU.add))
            order.step(v.tensor_scalar(agg[:, 0, :], agg[:, 0, :], 1.0 / L, None, ALU.mult))
            link(v.tensor_scalar(agg[:, 1:3, :], agg[:, 1:3, :], 1.0 / (L - L3), None, ALU.mult))
            dve.sem_inc(s["agg_ready"], 1)
            dve.wait_ge(s["cols_psum"], 1)
            v.tensor_copy(cols[:, :], bank[6][:, 0:C_END]).then_inc(s["cols_ready"], 1)
            x_second(0)
            up_second(E, 1)
            dve.wait_ge(s["gate_in"], 64)
            dve.wait_ge(s["gate_psum"], 1)
            order.step(v.tensor_tensor(mod[:, :], bank[6][0:B, 64:64 + 2 * E], time_b_sb[:, :], ALU.add))
            link(v.tensor_tensor(gl[:, :], bank[6][0:B, 96:96 + E], gate_b_sb[:, :], ALU.add))
            link(v.scalar_tensor_tensor(out=gl[:, :], in0=mod[:, 0:E], scalar=1.0, in1=gl[:, :],
                                        op0=ALU.add, op1=ALU.mult))
            link(v.tensor_tensor(gl[:, :], gl[:, :], mod[:, E:2 * E], ALU.add))
            v.tensor_reduce(gmax[:, :], gl[:, :], AX.X, ALU.max, negate=True).then_inc(s["gl_ready"], 1)
            dve.wait_ge(s["prob_exp"], 1)
            link(v.reciprocal(gsum[:, :], gsum[:, :]))
            link(v.tensor_scalar(prob[:, :], prob[:, :], gsum[:, 0:1], None, ALU.mult))
            mine = prob[:, :].unsqueeze(2).broadcast_to([B, E, E])
            other = prob[:, :].unsqueeze(1).broadcast_to([B, E, E])
            dve.wait_ge(s["consts"], 1)
            order.step(v.tensor_tensor(gt[:, :, :], other, mine, ALU.is_gt))
            link(v.tensor_tensor(eq[:, :, :], other, mine, ALU.is_equal))
            link(v.tensor_tensor(eq[:, :, :], eq[:, :, :], lower[:, :, :], ALU.mult))
            link(v.tensor_tensor(gt[:, :, :], gt[:, :, :], eq[:, :, :], ALU.add))
            link(v.tensor_reduce(rank[:, :], gt[:, :, :], AX.X, ALU.add))
            link(v.scalar_tensor_tensor(out=w_all[:, 0:E], in0=rank[:, :], scalar=float(K), in1=prob[:, :],
                                        op0=ALU.is_lt, op1=ALU.mult))
            link(v.tensor_reduce(gsum[:, :], w_all[:, 0:E], AX.X, ALU.add))
            link(v.tensor_scalar(gsum[:, :], gsum[:, :], 1e-8, None, ALU.add))
            link(v.reciprocal(gsum[:, :], gsum[:, :]))
            order.step(v.tensor_scalar(w_all[:, 0:E], w_all[:, 0:E], gsum[:, 0:1], None, ALU.mult))
            for k in range(K):
                order.step(v.tensor_scalar(pick[:, k, :], rank[:, :], float(k), None, ALU.is_equal))
            order.wait()
            order.step(v.tensor_tensor(sent[:, 0:K * E].rearrange("b (k e) -> b k e", e=E), pick[:, :, :],
                                       w_all[:, 0:E].unsqueeze(1).broadcast_to([B, K, E]), ALU.mult))
            link(v.tensor_tensor(picked[:, :, :], pick[:, :, :], number[:, :, :], ALU.mult))
            link(v.tensor_reduce(sent[:, K * E:], picked[:, :, :], AX.X, ALU.add))
            link(v.tensor_scalar(sent[:, K * E:], sent[:, K * E:], float(E - 1), float(H), ALU.min, ALU.mult))
            v.tensor_tensor(spread[:, :, :], sent[:, :].unsqueeze(1).broadcast_to([B, B, K * E + K]),
                            ident[0:B, 0:B].unsqueeze(2).broadcast_to([B, B, K * E + K]), ALU.mult)\
                .then_inc(s["spread_ready"], 1)
            dve.wait_ge(s["sent_psum"], 1)
            got = bank[6][:, 0:B * (K * E + K)].rearrange("p (b n) -> p b n", n=K * E + K)
            order.step(v.tensor_copy(offset[:, :].rearrange("p (b k) -> p b k", k=K), got[0:1, :, K * E:]))
            for k in range(K):
                order.step(v.tensor_tensor(w_tok[:, :, :].rearrange("p (b k) e -> p b k e", k=K)[:, :, k, :],
                                           got[:, :, k * E:(k + 1) * E],
                                           mask[:, 0:E].unsqueeze(1).broadcast_to([P, B, E]), ALU.mult))
            order.wait()
            dve.sem_inc(s["sent_ready"], 1)
            order.step(v.tensor_reduce(w_slot[:, :, :].rearrange("p b k -> p (b k)"), w_tok[:, :, :], AX.X, ALU.add))
            dve.wait_ge(s["gate_T_psum"], 1)
            order.step(v.tensor_copy(pick_T[:, :, :].rearrange("e k b -> e (k b)"), bank[7][0:E, 0:K * B]))
            order.step(v.tensor_copy(w_T[:, :], bank[7][0:E + 1, 64:64 + B]))
            order.step(v.tensor_copy(mask_T[:, :], bank[7][0:E + 1, 128:256]))
            order.wait()
            dve.sem_inc(s["gate_T_ready"], 1)
            for e in range(E):
                up_second(e, e + 2)
            dve.wait_ge(s["slot_bias_psum"], 1)
            link(v.tensor_copy(slot_bias[:, :, :, :].rearrange("p b k c -> p c k b"),
                               bank[6][:, 0:HC * K * B].rearrange("p (c k b) -> p c k b", k=K, b=B)))
            dve.sem_inc(s["slot_bias_ready"], 1)
            dve.wait_ge(s["uw_psum"], 1)
            link(v.tensor_copy(uw[:, :], bank[7][0:B, 0:P]))
            dve.sem_inc(s["uw_ready"], 1)
            dve.sem_inc(s["c_lo_ready"], 1)
            dve.sem_inc(s["y_added"], GB)

            def slot_pre(g, u):
                dve.wait_ge(s["up_done"], g * U + u + 1)
                dve.wait_ge(s["gelu_done"], g * U + u + 1)
                bias = slot_bias[:, :, :, :].rearrange("p b k c -> p (b k) c")[:, bass.ds(g * U + u, 1), :]
                v.scalar_tensor_tensor(out=pre[:, u % 2, :].rearrange("p (c t) -> p c t", t=L),
                                       in0=bank[(u + 1) % 3][:, :].rearrange("p (c t) -> p c t", t=L),
                                       scalar=1.0 / (XS * WS),
                                       in1=bias.rearrange("p o c -> p (o c)").unsqueeze(2).broadcast_to([P, HC, L]),
                                       op0=ALU.mult, op1=ALU.add).then_inc(s["pre_done"], 1)

            def add_slots(g):
                dve.wait_ge(s["y_s_copied"], g + 2)
                for k in range(K):
                    dve.wait_ge(s["down_done"], 4 + (g + 1) * U - K + k + 1)
                    for b in range(GB):
                        if k:
                            dve.wait_ge(s["v_order"], order_start + g * GB + b + 1)
                        w = w_slot[:, bass.ds(g * GB + b, 1), k]
                        v.scalar_tensor_tensor(out=c_grp[:, b, :], in0=bank[4 + k][:, b * DM:(b + 1) * DM],
                                               scalar=w, in1=c_grp[:, b, :], op0=ALU.mult, op1=ALU.add)\
                            .then_inc(s["y_added"] if k else s["v_order"], 1)

            def second_parts(g):
                dve.wait_ge(s["c_hi_ready"], g + 1)
                v.scalar_tensor_tensor(out=c_lo[:, bass.ds(g * GT, GT)], in0=bank[6][:, :], scalar=CS,
                                       in1=c_hi[:, bass.ds(g * GT, GT)], op0=ALU.mult, op1=ALU.subtract)\
                    .then_inc(s["c_lo_ready"], 1)

            def in_second(k, n):
                dve.wait_ge(s["in_hi_ready"], n)
                at = in_part(k)
                v.scalar_tensor_tensor(out=in_lo[:, at], in0=bank[7][:, 0:TAP0 if k is None else CD], scalar=IS,
                                       in1=in_hi[:, at], op0=ALU.mult, op1=ALU.subtract).then_inc(s["in_ready"], 1)

            def vector_group(g, more):
                for u in range(2, U):
                    slot_pre(g, u)
                add_slots(g)
                if more:
                    slot_pre(g + 1, 0)
                    slot_pre(g + 1, 1)
                in_second(g, g + 2)
                second_parts(g)

            for g in range(1, NG):
                x_second(g)
            slot_pre(0, 0)
            slot_pre(0, 1)
            in_second(None, 1)
            dve.wait_ge(s["out_psum"], 1)
            for j in range(JI):
                order.step(v.tensor_scalar(out_T[:, j, :], bank[6][:, j * P:(j + 1) * P], col(C_NW + j), None, ALU.mult))
            for h in range(NH):
                lo = h % 2 * HD
                order.step(v.tensor_copy(D_col[lo:lo + HD, h // 2:h // 2 + 1], D_all[lo:lo + HD, h:h + 1]))
            order.wait()
            dve.sem_inc(s["out_ready"], 1)
            dve.wait_ge(s["sum_psum"], 1)
            link(v.tensor_scalar(wmean[:, :], bank[7][:, 0:2], 1.0 / (F * DM), 1e-5, ALU.mult, ALU.max))
            link(v.reciprocal(wscale[:, :], wmean[:, :]))
            dve.sem_inc(s["wmean_ready"], 1)
            exact_parts(uw[:, :], uw_rest, uw_parts, B)
            order_start = order.count
            with dve.Fori(0, NG - 1) as g:
                vector_group(g, True)
            vector_group(NG - 1, False)
            order.count += NG * GB

            dve.wait_ge(s["dt_psum"], 1)
            link(v.scalar_tensor_tensor(out=dt_raw[:, :, :], in0=bank[7][:, 0:B * NH].rearrange("p (b h) -> p b h", h=NH),
                                        scalar=1.0 / (CS * IS),
                                        in1=dt_bias_sb[:, :].unsqueeze(1).broadcast_to([P, B, NH]),
                                        op0=ALU.mult, op1=ALU.add))

            raw = dt_raw[:, :, :].rearrange("p b h -> p (b h)")
            dts = dt_all[:, :, :].rearrange("p b h -> p (b h)")
            link(v.tensor_scalar(dts, raw, 0.0, None, ALU.max))
            v.scalar_tensor_tensor(out=dt_t[0][:, :], in0=dts, scalar=2.0, in1=raw,
                                   op0=ALU.mult, op1=ALU.subtract).then_inc(s["dt_in"], 1)
            dve.wait_ge(s["dt_exp"], 2)
            v.tensor_scalar(dt_t[2][:, :], dt_t[1][:, :], 1.0, None, ALU.add).then_inc(s["dt_w"], 1)
            dve.wait_ge(s["dt_w"], 1)
            link(v.scalar_tensor_tensor(out=dt_t[1][:, :], in0=dt_t[2][:, :], scalar=1.0, in1=dt_t[1][:, :],
                                        op0=ALU.subtract, op1=ALU.subtract))
            dve.wait_ge(s["dt_ln"], 1)
            link(v.tensor_tensor(dt_t[3][:, :], dt_t[3][:, :], dt_t[1][:, :], ALU.subtract))
            link(v.tensor_tensor(dts, dts, dt_t[3][:, :], ALU.add))
            v.tensor_tensor(dt_t[0][:, :].rearrange("p (b h) -> p b h", h=NH), dt_all[:, :, :],
                            A_pos[:, :].unsqueeze(1).broadcast_to([P, B, NH]), ALU.mult).then_inc(s["dt_mul"], 1)

            dve.wait_ge(s["dt_exp"], 3)
            link(v.memset(dA_all[0:1, :, :], 0.0))
            exact_parts(dA_all[:, :, :].rearrange("p b h -> p (b h)"), dA_rest, dA_parts, P)
            dve.sem_inc(s["dA_ready"], 1)

            own_b = Stage(dve, s["v_b"], JI)
            own_c = Stage(dve, s["v_c"], 1 + 5 + GB + GB + 5 + GB)
            own_last = Stage(dve, s["v_last"], 1 + 5 + GB + GB + 2 * 5)
            dve.sem_inc(s["y_g_ready"], JI)
            dve.sem_inc(s["y_out_ready"], 1)

            def x_times_dt(g):
                for m in range(2):
                    dve.wait_ge(s["xs_T_psum"], g * 2 + 2 + m + 1)
                    dtb = dt_all[:, bass.ds(g * GB + 2 * m, 2), :].rearrange("p b h -> p (b h)")
                    v.tensor_tensor(x_dt[:, 2 * m:2 * m + 2, :].rearrange("p b (h q) -> p (b h) q", q=HD),
                                    bank[2 + m][:, :].rearrange("p (m q) -> p m q", q=HD),
                                    dtb.unsqueeze(2).broadcast_to([P, 2 * NH, HD]),
                                    ALU.mult).then_inc(s["x_dt_ready"], 1)

            def scan(g, b):
                dve.wait_ge(s["bc_psum"], g * GB + b + 1)
                if b >= 2:
                    dve.wait_ge(s["mix_ready"], g * GB + b - 1)
                v.tensor_tensor_scan(out=decay[:, b % 2, :], data0=bank[5 + b % 2][:, :],
                                     data1=ident4[:, :, :].rearrange("p h t -> p (h t)"), initial=0.0,
                                     op0=ALU.mult, op1=ALU.add).then_inc(s["scan_done"], 1)

            def mix(g, b):
                dve.wait_ge(s["scan_done"], g * GB + b + 1)
                if b == 0:
                    dve.wait_ge(s["g_psum"], g + 2)
                if b >= 2:
                    dve.wait_ge(s["y_psum"], g * GB + b - 1)
                v.tensor_tensor(mixer[:, b % 2, :].rearrange("p (h t) -> p h t", t=L),
                                decay[:, b % 2, :].rearrange("p (h t) -> p h t", t=L),
                                bank[4][:, b * L:(b + 1) * L].unsqueeze(1).broadcast_to([P, NH, L]),
                                ALU.mult).then_inc(s["mix_ready"], 1)

            def gate_y(g):
                own_b.group(g)
                dve.wait_ge(s["z_ready"], (g + 2) * JI)
                dve.wait_ge(s["xD_ready"], g + 2)
                dve.wait_ge(s["y_psum"], (g + 1) * GB)
                for j in range(JI):
                    own_b.step(v.tensor_tensor(y_g[:, j, :], bank[2 + j][:, :], xD[:, j, :], ALU.add))
                for j in range(JI):
                    own_b.wait(j + 1)
                    v.tensor_tensor(y_g[:, j, :], y_g[:, j, :], z_act[:, j, :], ALU.mult)\
                        .then_inc(s["y_g_ready"], 1)

            def mean_square(g):
                dve.wait_ge(s["ss_psum"], g + 1)
                v.tensor_scalar(y_ms[:, :], bank[7][:, 0:GB], 1.0 / DI, EPS, ALU.mult, ALU.add)\
                    .then_inc(s["ms_ready"], 1)

            def add_residual(g):
                dve.wait_ge(s["out_proj_psum"], g + 1)
                dve.wait_ge(s["yr_ready"], g + 1)
                dve.wait_ge(s["res_b2_ready"], g + 1)
                for b in range(GB):
                    v.scalar_tensor_tensor(out=r_grp[:, b, :], in0=bank[4][:, b * DM:(b + 1) * DM],
                                           scalar=y_r[:, b:b + 1],
                                           in1=res[:, bass.ds(g * GB + b, 1), :].rearrange("p b d -> p (b d)"),
                                           op0=ALU.mult, op1=ALU.add).then_inc(s["r_grp_ready"], 1)

            def own_of(g):
                return own_last if last(g) else own_c

            def largest_1(g):
                own_of(g).group(0 if last(g) else g)
                dve.wait_ge(s["e_ready"], g + 2)
                own_of(g).step(v.tensor_reduce(amax[:, 0, :], e_all[:, bass.ds(g * GB, GB), :], AX.X, ALU.max,
                                               apply_absolute_value=True))

            def mean_squares(g, k):
                dve.wait_ge(s[f"ssq{k + 1}"], (g + 1) * GB)
                v.tensor_scalar(ms[:, k, :], ssq[:, k, :], 1.0 / (DM, F)[k], EPS, ALU.mult, ALU.add)\
                    .then_inc(s[f"ms{k + 1}"], 1)

            def mean_squares_half(g, half):
                dve.wait_ge(s["ssq2"], g * GB + 2 * half + 2)
                at = slice(2 * half, 2 * half + 2)
                v.tensor_scalar(ms[:, 1, at], ssq[:, 1, at], 1.0 / F, EPS, ALU.mult, ALU.add).then_inc(s["ms2"], 1)

            def scales(g, k, half=None):
                at = slice(0, GB) if half is None else slice(2 * half, 2 * half + 2)
                if k == 1:
                    dve.wait_ge(s["y_out_ready"], g + 1)
                dve.wait_ge(s[f"rr{k + 1}"], g + 1 + (half or 0))
                own_of(g).wait()
                link = own_of(g).link
                link(v.tensor_tensor(cl[:, k, at], amax[:, k, at], rr[:, k, at], ALU.mult))
                link(v.tensor_scalar(cl[:, k, at], cl[:, k, at], 1e-5, None, ALU.max))
                own_of(g).step(v.tensor_scalar(qk[:, k, at], cl[:, k, at], 1.0 / 127.0, wmean[:, k:k + 1], ALU.mult, ALU.mult))
                link(v.reciprocal(inv[:, k, at], cl[:, k, at]))
                link(v.scalar_tensor_tensor(out=qm[:, k, at], in0=inv[:, k, at], scalar=127.0, in1=rr[:, k, at],
                                            op0=ALU.mult, op1=ALU.mult))

            def round_1(g):
                for b in range(GB):
                    own_of(g).step(v.tensor_scalar(q1_f[:, b * DM:(b + 1) * DM],
                                                   e_all[:, bass.ds(g * GB + b, 1), :].rearrange("p b d -> p (b d)"),
                                                   qm[:, 0, b:b + 1], MAGIC, ALU.mult, ALU.add))
                own_of(g).wait()
                v.tensor_scalar(q1[:, :], q1_f[:, :], MAGIC, None, ALU.subtract).then_inc(s["q1_ready"], 1)

            def scale_h(g, b):
                dve.wait_ge(s["h_psum"], g * GB + b + 1)
                v.scalar_tensor_tensor(out=h_pre[:, b, :], in0=ffn_bank(g, b)[:, :], scalar=qk[:, 0, b:b + 1],
                                       in1=b1_sb[:, :], op0=ALU.mult, op1=ALU.add).then_inc(s["h_pre_ready"], 1)

            def largest_2(g, b):
                dve.wait_ge(s["h_act_ready"], g * GB + b + 1)
                own_of(g).step(v.tensor_reduce(amax[:, 1, b:b + 1], h_act[:, b, :], AX.X, ALU.max,
                                               apply_absolute_value=True))

            def round_2(g, first=0, end=GB):
                for b in range(first, end):
                    rounded = own_of(g).step(v.tensor_scalar(q2_f[:, b, :], h_act[:, b, :], qm[:, 1, b:b + 1], MAGIC,
                                                             ALU.mult, ALU.add))
                    if b > first:
                        own_of(g).wait(rounded - 1)
                        v.tensor_scalar(q2[:, b - 1, :], q2_f[:, b - 1, :], MAGIC, None, ALU.subtract)\
                            .then_inc(s["q2_ready"], 1)
                own_of(g).wait()
                v.tensor_scalar(q2[:, end - 1, :], q2_f[:, end - 1, :], MAGIC, None, ALU.subtract)\
                    .then_inc(s["q2_ready"], 1)

            def round_2_first(g, batches):
                for b in batches:
                    v.tensor_scalar(q2_f[:, b, :], h_act[:, b, :], qm[:, 1, b:b + 1], MAGIC, ALU.mult, ALU.add)\
                        .then_inc(s["q2_f_ready"], 1)

            def output(g):
                dve.wait_ge(s["o_psum"], g + 1)
                dve.wait_ge(s["out_sent"], g * 16 + 16)
                dve.wait_ge(s["res_b2_ready"], g + 2)
                for b in range(GB):
                    ins = v.scalar_tensor_tensor(out=y_out[:, b, :], in0=bank[7][:, b * DM:(b + 1) * DM],
                                                 scalar=qk[:, 1, b:b + 1],
                                                 in1=res[:, bass.ds(g * GB + b, 1), :].rearrange("p b d -> p (b d)"),
                                                 op0=ALU.mult, op1=ALU.add)
                ins.then_inc(s["y_out_ready"], 1)

            def vector_turn(i, ssm=True, ffn=True):
                if ffn:
                    own_c.resume(i - 1)
                if ssm:
                    x_times_dt(i)
                    for b in range(2):
                        scan(i, b)
                        mix(i, b)
                if ffn:
                    scales(i - 1, 0)
                    round_1(i - 1)
                if ssm:
                    for b in range(2, GB):
                        scan(i, b)
                        mix(i, b)
                if ffn:
                    scale_h(i - 1, 0)
                    scale_h(i - 1, 1)
                if ssm:
                    gate_y(i)
                if ffn:
                    scale_h(i - 1, 2)
                    scale_h(i - 1, 3)
                    for b in range(GB):
                        largest_2(i - 1, b)
                if ssm:
                    mean_square(i)
                if ffn:
                    mean_squares(i - 1, 1)
                if ssm:
                    add_residual(i)
                if ffn:
                    scales(i - 1, 1)
                    round_2(i - 1)
                if ssm:
                    largest_1(i)
                    mean_squares(i, 0)
                if ffn:
                    output(i - 1)

            vector_turn(0, ffn=False)
            with dve.Fori(1, NG - 1) as i:
                vector_turn(i)
            f, m = NG - 2, NG - 1
            own_c.resume(f)
            x_times_dt(m)
            for b in range(GB):
                scan(m, b)
                mix(m, b)
            scales(f, 0)
            round_1(f)
            gate_y(m)
            scale_h(f, 0)
            scale_h(f, 1)
            scale_h(f, 2)
            mean_square(m)
            scale_h(f, 3)
            largest_2(f, 0)
            add_residual(m)
            for b in range(1, GB):
                largest_2(f, b)
            mean_squares(f, 1)
            scales(f, 1)
            largest_1(m)
            mean_squares(m, 0)
            round_2(f, 0, 2)
            scales(m, 0)
            round_1(m)
            round_2(f, 2, GB)
            for b in range(GB):
                scale_h(m, b)
            largest_2(m, 0)
            largest_2(m, 1)
            mean_squares_half(m, 0)
            output(f)
            scales(m, 1, 0)
            mean_squares_half(m, 1)
            round_2_first(m, range(2))
            largest_2(m, 2)
            largest_2(m, 3)
            scales(m, 1, 1)
            round_2_first(m, range(2, GB))
            output(m)

        @block.tensor
        def _(pe):
            mm, tr = pe.matmul, pe.transpose

            pe.wait_ge(s["ident_ready"], 1)
            for g in range(NG):
                pe.wait_ge(x_in[g], 16)
                for b in range(GB):
                    ins = tr(bank[X_BANK[g]][:, b * L:(b + 1) * L], x_tok[:, g * GB + b, :], ident[:, :])
                ins.then_inc(s["x_T_psum"], 1)
            pe.wait_ge(s["rows_in"], 16 * ROWS)
            tr(bank[6][:, 0:C_END], rows[:, :], ident[0:C_END, 0:C_END]).then_inc(s["cols_psum"], 1)
            pe.wait_ge(s["cols_ready"], 1)
            pe.wait_ge(s["x_lo_ready"], 1)
            pe.wait_ge(s["proj_in"], 16)
            mm(bank[7][:, 0:B], proj_sb[:, :], col(C_COND, B), start=True, stop=True).then_inc(s["u_psum"], 1)
            pe.wait_ge(s["silu_ready"], 1)
            pe.wait_ge(s["gate_in"], 64)
            mm(bank[6][0:B, 64:64 + 2 * E], cond_silu[:, :], time_w_sb[:, :], start=True, stop=True)
            pe.wait_ge(s["agg_ready"], 1)
            for j in range(3):
                ins = mm(bank[6][0:B, 96:96 + E], agg[:, j, :], gate_w_sb[:, j, :], start=(j == 0), stop=(j == 2))
            ins.then_inc(s["gate_psum"], 1)

            def three(dst, w_hi, w_lo, m_hi, m_lo):
                mm(dst, w_hi, m_hi, start=True, stop=False)
                mm(dst, w_hi, m_lo, start=False, stop=False)
                return mm(dst, w_lo, m_hi, start=False, stop=True)

            def shared_up(g, c, first=False):
                if c == 3:
                    pe.wait_ge(s["gelu_s_done"], g * HC + 1)
                elif not first:
                    pe.wait_ge(s["pre_done"], g * U - 2 + c)
                w = slice(E * H + c * P, E * H + (c + 1) * P)
                at = bass.ds(g * GT, GT)
                three(bank[c % 3][:, :], up_hi[:, w], up_lo[:, w], x_hi[:, at], x_lo[:, at])\
                    .then_inc(s["up_s_done"], 1)

            def shared_down(g):
                pe.wait_ge(s["y_s_copied"], g + 1)
                pe.wait_ge(s["gelu_s_done"], (g + 1) * HC)
                pe.wait_ge(s["w_mask_T_ready"], g + 1)
                for b in range(GB):
                    dst = bank[3][:, b * DM:(b + 1) * DM]
                    mm(dst, w_mask_T[:, b, :], b2_rows[:, :], start=True, stop=False)
                    for c in range(HC):
                        ins = mm(dst, hid_s[:, c, b * L:(b + 1) * L], down[:, E * H + c * DM:E * H + (c + 1) * DM],
                                 start=False, stop=(c == HC - 1))
                ins.then_inc(s["down_s_done"], 1)

            def slot_up(g, u, e_at):
                if u < 3:
                    pe.wait_ge(s["gelu_s_done"], g * HC + u + 2)
                else:
                    pe.wait_ge(s["pre_done"], g * U + u - 2)
                at = bass.ds(g * GT + u // K * L, L)
                for c in range(HC):
                    w = bass.ds(e_at + c * P, P)
                    ins = three(bank[(u + 1) % 3][:, c * L:(c + 1) * L], up_hi[:, w], up_lo[:, w],
                                x_hi[:, at], x_lo[:, at])
                ins.then_inc(s["up_done"], 1)

            def slot_down(g, u, e_at):
                if u < K:
                    pe.wait_ge(s["y_added"], (g + 1) * GB)
                pe.wait_ge(s["gelu_done"], 2 + g * U + u + 1)
                b, k = divmod(u, K)
                for c in range(HC):
                    ins = mm(bank[4 + k][:, b * DM:(b + 1) * DM], hid[:, u % 4, c * L:(c + 1) * L],
                             down[:, bass.ds(e_at + c * DM, DM)], start=(c == 0), stop=(c == HC - 1))
                ins.then_inc(s["down_done"], 1)

            def transpose_c(g):
                pe.wait_ge(s["y_added"], (g + 2) * GB)
                pe.wait_ge(s["c_lo_ready"], g + 1)
                for b in range(GB):
                    ins = tr(bank[6][:, b * L:(b + 1) * L], c_grp[:, b, :], ident[:, :])
                ins.then_inc(s["c_T_psum"], 1)

            def slot_experts(first, n):
                _, values = nc.values_load_multi_w_load_instructions(
                    offset[0:1, bass.ds(first, n)], engines=(mybir.EngineType.PE,), min_val=0, max_val=(E - 1) * H,
                    skip_runtime_bounds_check_because="the gate keeps the offsets within the weights")
                return values

            pe.wait_ge(s["up_lo_ready"], 1)
            for c in range(HC - 1):
                shared_up(0, c, True)
            pe.wait_ge(s["spread_ready"], 1)
            mm(bank[6][:, 0:B * (K * E + K)], ones[0:B, :], spread[:, :, :].rearrange("k b e -> k (b e)"),
               start=True, stop=True).then_inc(s["sent_psum"], 1)
            pe.wait_ge(s["u_ready"], 1)
            for k in range(K):
                tr(bank[7][0:E, k * B:(k + 1) * B], pick[:, k, :], ident[0:B, 0:B])
            tr(bank[7][0:E + 1, 64:64 + B], w_all[:, :], ident[0:B, 0:B])
            tr(bank[7][0:E + 1, 128:256], mask[:, :], ident[:, :]).then_inc(s["gate_T_psum"], 1)
            shared_up(0, HC - 1, True)
            pe.wait_ge(s["gate_T_ready"], 1)
            pe.wait_ge(s["bias_in"], 48)
            for c in range(HC):
                ins = mm(bank[6][:, c * K * B:(c + 1) * K * B], eb1_rows[:, c * P:(c + 1) * P],
                         pick_T[:, :, :].rearrange("e k b -> e (k b)"), start=True, stop=True)
            ins.then_inc(s["slot_bias_psum"], 1)
            pe.wait_ge(s["mix_in"], 16)
            mm(bank[7][0:B, 0:P], u_T[:, :], mix_sb[:, 0, :], start=True, stop=True).then_inc(s["uw_psum"], 1)

            pe.sem_inc(s["down_done"], 4)
            pe.wait_ge(s["sent_ready"], 1)
            pe.wait_ge(s["up_lo_ready"], E + 1)
            e_at = slot_experts(0, K)
            slot_up(0, 0, e_at[0])
            slot_up(0, 1, e_at[1])
            pe.wait_ge(s["in_in"], 16 * 7)
            pe.wait_ge(s["slot_bias_ready"], 1)
            pe.wait_ge(s["uw_ready"], 1)
            for j in range(JI):
                tr(bank[7][:, j * P:(j + 1) * P], in_nat[:, j, :], ident[:, :])
            tr(bank[7][:, DI:DI + NH], in_nat_dt[:, :], ident[0:NH, 0:NH]).then_inc(s["in_psum"], 1)
            for j in range(JI):
                ins = tr(bank[6][:, j * P:(j + 1) * P], out_nat[:, j * P:(j + 1) * P], ident[:, :])
            ins.then_inc(s["out_psum"], 1)
            pe.wait_ge(s["x_lo_ready"], NG)
            pe.wait_ge(s["down_s_in"], 16)
            shared_down(0)
            pe.wait_ge(s["in_ready"], 1)
            pe.wait_ge(s["abs_done"], 2)
            mm(bank[7][:, 0:2], ones[:, :], wsum[:, :], start=True, stop=True).then_inc(s["sum_psum"], 1)
            pe.wait_ge(s["downs_in"], 16)

            def transpose_tap(g):
                pe.wait_ge(s["in_tap_ready"], g + 1)
                pe.wait_ge(s["in_ready"], g + 1)
                for c in range(JC):
                    ins = tr(bank[7][:, c * P:(c + 1) * P], in_tap[:, c, :], ident[:, :])
                ins.then_inc(s["in_psum"], 1)

            def tensor_group(g, more):
                e_at = slot_experts(g * U, U)
                for u in range(2, U):
                    slot_up(g, u, e_at[u])
                    slot_down(g, u - 2, e_at[u - 2])
                if more:
                    shared_up(g + 1, 0)
                slot_down(g, U - 2, e_at[U - 2])
                if more:
                    shared_up(g + 1, 1)
                slot_down(g, U - 1, e_at[U - 1])
                if more:
                    shared_up(g + 1, 2)
                    shared_up(g + 1, 3)
                    e_next = slot_experts((g + 1) * U, K)
                    slot_up(g + 1, 0, e_next[0])
                    slot_up(g + 1, 1, e_next[1])
                transpose_tap(g)
                transpose_c(g)
                if more:
                    shared_down(g + 1)

            with pe.Fori(0, NG - 1) as g:
                tensor_group(g, True)
            tensor_group(NG - 1, False)

            pe.wait_ge(s["in_ready"], KW + 1)
            pe.wait_ge(s["c_lo_ready"], NG + 1)
            for b in range(B):
                at = slice(b * L, (b + 1) * L)
                w = slice(DI, DI + NH)
                ins = three(bank[7][:, b * NH:(b + 1) * NH], c_hi[:, at], c_lo[:, at], in_hi[:, w], in_lo[:, w])
            ins.then_inc(s["dt_psum"], 1)
            for k, (q, bk) in enumerate(((w1_q, 6), (w2_q, 5))):
                pe.wait_ge(s["w_q_ready"], k + 1)
                for c in range(FC):
                    src = q[:, c, :] if k == 0 else q[:, c * P:(c + 1) * P]
                    ins = tr(bank[bk][:, c * P // 2:(c + 1) * P // 2].bitcast(bf16), src, identb[:, :])
                ins.then_inc(s["w_qT_psum"], 1)

            def conv_proj(g, j):
                if j < 2:
                    pe.wait_ge(s["z_ready"], g * JI + j + 1)
                else:
                    pe.wait_ge(s["xbc_ready"], g * JC + j - 1)
                dst = bank[j % 2][:, :].rearrange("p (b t) -> p b t", t=L)
                hi = c_hi[:, bass.ds(g * GT, GT)].rearrange("p (b t) -> p b t", t=L)
                lo = c_lo[:, bass.ds(g * GT, GT)].rearrange("p (b t) -> p b t", t=L)
                for k in range(KW):
                    w0 = TAP0 + (KW - 1 - k) * CD + j * P
                    w = slice(w0, w0 + P)
                    to, of = slice(k, L), slice(0, L - k)
                    mm(dst[:, :, to], in_hi[:, w], hi[:, :, of], start=(k == 0), stop=False)
                    mm(dst[:, :, to], in_hi[:, w], lo[:, :, of], start=False, stop=False)
                    ins = mm(dst[:, :, to], in_lo[:, w], hi[:, :, of], start=False, stop=(k == KW - 1))
                ins.then_inc(s["xbc_psum"], 1)

            def z_proj(g, j):
                pe.wait_ge(s["xbc_ready"], g * JC + 2 + j + 1)
                w, at = slice(j * P, (j + 1) * P), bass.ds(g * GT, GT)
                three(bank[j][:, :], in_hi[:, w], in_lo[:, w], c_hi[:, at], c_lo[:, at]).then_inc(s["z_psum"], 1)

            def transpose_x(g):
                pe.wait_ge(s["xbc_ready"], g * JC + JI)
                pe.wait_ge(s["e_ready"], g + 1)
                for b in range(GB):
                    for j in range(JI):
                        ins = tr(bank[2 + b // 2][:, (b % 2 * JI + j) * P:(b % 2 * JI + j + 1) * P],
                                 xbc[:, j, b * L:(b + 1) * L], ident[:, :])
                    if b % 2:
                        ins.then_inc(s["xs_T_psum"], 1)

            def c_dot_b(g):
                pe.wait_ge(s["xbc_ready"], (g + 1) * JC)
                for b in range(GB):
                    ins = mm(bank[4][:, b * L:(b + 1) * L], xbc[:, JI, b * L:(b + 1) * L],
                             xbc[:, JI + 1, b * L:(b + 1) * L], start=True, stop=True)
                ins.then_inc(s["g_psum"], 1)

            def spread_decays(g, b):
                if b >= 2:
                    pe.wait_ge(s["scan_done"], g * GB + b - 1)
                for h in range(NH):
                    for k in range(3):
                        ins = mm(bank[5 + b % 2][:, h * L:(h + 1) * L],
                                 dA_parts[:, k, bass.ds((g * GB + b) * NH + h, 1)].broadcast_to([P, P]), identb[:, :],
                                 start=(k == 0), stop=(k == 2))
                ins.then_inc(s["bc_psum"], 1)

            def heads(g, b):
                pe.wait_ge(s["mix_ready"], g * GB + b + 1)
                pe.wait_ge(s["x_dt_ready"], g * 2 + 2)
                for h in range(NH):
                    lo = h % 2 * HD
                    ins = mm(bank[2 + h // 2][lo:lo + HD, b * L:(b + 1) * L], x_dt[:, b, h * HD:(h + 1) * HD],
                             mixer[:, b % 2, h * L:(h + 1) * L], start=True, stop=True)
                ins.then_inc(s["y_psum"], 1)

            def out_proj(g, batches):
                pe.wait_ge(s["y_g_ready"], (g + 2) * JI)
                for b in batches:
                    for j in range(JI):
                        ins = mm(bank[4][:, b * DM:(b + 1) * DM], y_g[:, j, b * L:(b + 1) * L], out_T[:, j, :],
                                 start=(j == 0), stop=(j == JI - 1))
                if GB - 1 in batches:
                    ins.then_inc(s["out_proj_psum"], 1)

            def sum_squares(g):
                pe.wait_ge(s["y_sq_ready"], (g + 1) * JI)
                for b in range(GB):
                    for j in range(JI):
                        ins = mm(bank[7][:, b:b + 1], y_sq[:, j, b * L:(b + 1) * L], ones[:, 0:1],
                                 start=(j == 0), stop=(j == JI - 1))
                ins.then_inc(s["ss_psum"], 1)

            def transpose_r(g):
                pe.wait_ge(s["r_grp_ready"], (g + 1) * GB)
                for b in range(GB):
                    ins = tr(bank[2][:, b * L:(b + 1) * L], r_grp[:, b, :], ident[:, :])
                ins.then_inc(s["rT_psum"], 1)

            def mix_condition(g):
                mm(bank[3][:, :], zeros[:, :], w1_qT[:, :], start=True, stop=False)
                for b in range(GB):
                    for k in range(3):
                        mm(bank[3][:, b * P:(b + 1) * P], identb[:, bass.ds(g * GB + b, 1)].broadcast_to([P, P]),
                           uw_parts[:, k, :], start=False, stop=False)

            def mix_product(g):
                pe.wait_ge(s["rT_ready"], g + 1)
                for b in range(GB):
                    ins = mm(bank[3][:, b * P:(b + 1) * P], r_T[:, b * L:(b + 1) * L], mix_sb[:, 1, :],
                             start=False, stop=(b == GB - 1))
                ins.then_inc(s["e_psum"], 1)

            def transpose_q1(g):
                pe.wait_ge(s["q1_ready"], g + 1)
                if not last(g):
                    pe.wait_ge(s["y_out_ready"], g + 1)
                for b in range(GB):
                    ins = tr(q1_bank(g)[:, b * L // 2:(b + 1) * L // 2].bitcast(bf16), q1[:, b * DM:(b + 1) * DM],
                             identb[:, :])
                ins.then_inc(s["q1T_psum"], 1)

            def ffn_up(g, b, scanned=False):
                pe.wait_ge(s["q1T_ready"], g + 1)
                if scanned:
                    pe.wait_ge(s["scan_done"], (g + 1) * GB + 3 + b)
                if b >= 2:
                    pe.wait_ge(s["h_pre_ready"], g * GB + b - 1)
                mm(ffn_bank(g, b)[:, :], q1_T[:, b * L:(b + 1) * L], w1_qT[:, :], start=True, stop=True)\
                    .then_inc(s["h_psum"], 1)

            def transpose_q2(g, b):
                pe.wait_ge(s["q2_ready"], g * GB + b + 1)
                if b >= 2:
                    pe.wait_ge(s["q2T_ready"], g * GB + b - 1)
                for c in range(FC):
                    ins = tr(ffn_bank(g, b)[:, c * L // 2:(c + 1) * L // 2].bitcast(bf16),
                             q2[:, b, c * P:(c + 1) * P], identb[:, :])
                ins.then_inc(s["q2T_psum"], 1)

            def ffn_down(g):
                if last(g):
                    pe.wait_ge(s["y_out_ready"], g + 1)
                for b in range(GB):
                    pe.wait_ge(s["q2T_ready"], g * GB + b + 1)
                    for c in range(FC):
                        ins = mm(bank[7][:, b * DM:(b + 1) * DM], q2_T[:, b, c * L:(c + 1) * L], w2_qT[:, c, :],
                                 start=(c == 0), stop=(c == FC - 1))
                ins.then_inc(s["o_psum"], 1)

            def tensor_turn(i, proj=True, ssm=True, ffn=True):
                if ssm:
                    transpose_x(i)
                    c_dot_b(i)
                    spread_decays(i, 0)
                    spread_decays(i, 1)
                if proj:
                    conv_proj(i + 1, 0)
                if ssm:
                    heads(i, 0)
                    spread_decays(i, 2)
                    heads(i, 1)
                    spread_decays(i, 3)
                if ffn:
                    transpose_q1(i - 1)
                if proj:
                    conv_proj(i + 1, 1)
                if ffn:
                    ffn_up(i - 1, 0, ssm)
                    ffn_up(i - 1, 1, ssm)
                if ssm:
                    heads(i, 2)
                    heads(i, 3)
                if proj:
                    conv_proj(i + 1, 2)
                if ffn:
                    ffn_up(i - 1, 2)
                    ffn_up(i - 1, 3)
                if ssm:
                    out_proj(i, range(2))
                    sum_squares(i)
                    out_proj(i, range(2, GB))
                    mix_condition(i)
                if proj:
                    conv_proj(i + 1, 3)
                    for j in range(JI):
                        z_proj(i + 1, j)
                if ssm:
                    transpose_r(i)
                if ffn:
                    transpose_q2(i - 1, 0)
                    transpose_q2(i - 1, 1)
                if ssm:
                    mix_product(i)
                if ffn:
                    transpose_q2(i - 1, 2)
                    transpose_q2(i - 1, 3)
                    ffn_down(i - 1)

            pe.sem_inc(s["xs_T_psum"], 2)
            pe.sem_inc(s["g_psum"], 1)
            tensor_turn(-1, ssm=False, ffn=False)
            pe.wait_ge(s["dA_ready"], 1)
            pe.wait_ge(s["w_qT_ready"], 2)
            tensor_turn(0, ffn=False)
            with pe.Fori(1, NG - 1) as i:
                tensor_turn(i)
            f, m = NG - 2, NG - 1
            transpose_x(m)
            c_dot_b(m)
            spread_decays(m, 0)
            spread_decays(m, 1)
            heads(m, 0)
            spread_decays(m, 2)
            heads(m, 1)
            spread_decays(m, 3)
            heads(m, 2)
            heads(m, 3)
            transpose_q1(f)
            ffn_up(f, 0, True)
            ffn_up(f, 1, True)
            out_proj(m, range(2))
            ffn_up(f, 2)
            sum_squares(m)
            ffn_up(f, 3)
            out_proj(m, range(2, GB))
            mix_condition(m)
            transpose_r(m)
            mix_product(m)
            transpose_q2(f, 0)
            transpose_q2(f, 1)
            transpose_q1(m)
            ffn_up(m, 0)
            ffn_up(m, 1)
            transpose_q2(f, 2)
            transpose_q2(f, 3)
            ffn_up(m, 2)
            ffn_up(m, 3)
            ffn_down(f)
            for b in range(GB):
                transpose_q2(m, b)
            ffn_down(m)

    return nc


_INS = ["x", "cond_1024", "L0_cond_gate_w", "L0_cond_gate_b", "L0_cond_time_w", "L0_cond_time_b", "L0_cond_ew1",
        "L0_cond_eb1", "L0_cond_ew2", "L0_cond_eb2", "L0_cond_sw1", "L0_cond_sb1", "L0_cond_sw2", "L0_cond_sb2",
        "L0_attn_in_proj_w", "L0_attn_conv_w", "L0_attn_conv_b", "L0_attn_dt_bias", "L0_attn_A_log", "L0_attn_D",
        "L0_attn_norm_w", "L0_attn_out_proj_w", "L0_cond2_weight_matrix", "L0_cond2_W_proj", "L0_cond2_b_proj",
        "L0_ffn_w1", "L0_ffn_b1", "L0_ffn_w2", "L0_ffn_b2"]


def kernel(**inputs):
    import numpy as _np
    import concourse.bacc as _bacc
    from concourse import mybir as _mybir
    from concourse.bass_utils import run_bass_kernel_spmd as _run

    nc = _bacc.Bacc("TRN2", target_bir_lowering=False, num_devices=1)
    arrays, args = {}, []
    for name in _INS:
        a = _np.ascontiguousarray(inputs[name])
        arrays[f"in_{name}"] = a
        args.append(nc.dram_tensor(f"in_{name}", a.shape, _mybir.dt.from_np(a.dtype), kind="ExternalInput").ap())
    args.append(nc.dram_tensor("out_dram", inputs["x"].shape, _mybir.dt.float32, kind="ExternalOutput").ap())
    build(nc, *args)
    r = _run(nc, [arrays], core_ids=[0])
    return r.results[0]["out_dram"]
```
